# Optimizing a Trainium2 kernel written in Bass

```python
import numpy as np
import jax
import jax.numpy as jnp

def _softmax(x, axis=-1):
    return jax.nn.softmax(x, axis=axis)

def _gelu(x):
    return jax.nn.gelu(x, approximate=True)

def _silu(x):
    return jax.nn.silu(x)

def _sigmoid(x):
    return jax.nn.sigmoid(x)

def _layernorm(x, axis=-1, eps=1e-05):
    m = jnp.mean(x, axis=axis, keepdims=True)
    v = jnp.var(x, axis=axis, keepdims=True)
    return (x - m) / jnp.sqrt(v + eps)

def _scatter_add(tgt, idx, src, axis=0):
    return tgt.at[idx].add(src)

def _segment_sum(src, seg, n):
    return jax.ops.segment_sum(src, seg, n)
kernel_name = 'mk_early_fusion_d1_tok_img1024_r4_a8685e'

def setup_inputs(seed: int=0):
    np.random.seed(seed)
    _w = jnp.asarray

    def _rec_inputs():
        import jax
        import jax.numpy as jnp
        _rk = jax.random.key(seed)
        x = -0.00150118 + 0.499729 * jax.random.normal(jax.random.fold_in(_rk, 1), (8, 256, 64, 2), jnp.float32)
        txt = 0.00326275 + 2.8086 * jax.random.normal(jax.random.fold_in(_rk, 2), (8, 512, 256), jnp.float32)
        return (x, txt)
    x, txt = _rec_inputs()

    def _L0_tok_setup():
        import jax, jax.numpy as jnp
        import numpy as np
        import math
        H = 256
        N = 64
        CH = 1
        SEQ_L = 256
        key = jax.random.key(seed)
        k1, k2, k3, k4 = jax.random.split(key, 4)
        log_dt = jax.random.uniform(k1, (H,), dtype=jnp.float32, minval=math.log(0.001), maxval=math.log(0.1))
        inv_A_real = jnp.log(0.5 * jnp.ones((H, N), jnp.float32)) + 0.1 * jax.random.normal(k2, (H, N), dtype=jnp.float32)
        A_imag = jnp.broadcast_to(math.pi * jnp.arange(N, dtype=jnp.float32), (H, N)).copy()
        B_ri = jax.random.normal(k3, (H, N, 2), dtype=jnp.float32) * 0.5
        C_ri = jax.random.normal(k4, (CH, H, N, 2), dtype=jnp.float32) * 0.5
        return {'log_dt': log_dt, 'inv_A_real': inv_A_real, 'A_imag': A_imag, 'B_ri': B_ri, 'C_ri': C_ri, 'L': SEQ_L}
    _L0_tok_all = _L0_tok_setup()
    _L0_tok_in = {k: v for k, v in _L0_tok_all.items() if k in ('log_dt', 'inv_A_real', 'A_imag', 'B_ri')}
    del _L0_tok_all

    def _L0_attn_setup():
        import jax, jax.numpy as jnp
        import numpy as np
        H, KV, DH = (16, 4, 64)

        def _rotate_half(t):
            t1, t2 = (t[..., :DH // 2], t[..., DH // 2:])
            return jnp.concatenate([-t2, t1], axis=-1)
        key = jax.random.key(seed)
        k1, k2, k3, k4, k5 = jax.random.split(key, 5)
        B, L, D = (1, 1024, 256)
        s = 0.02
        return {'x': jax.random.normal(k1, (B, L, D), dtype=jnp.float32), 'Wq': jax.random.normal(k2, (D, H * DH), dtype=jnp.float32) * s, 'Wk': jax.random.normal(k3, (D, KV * DH), dtype=jnp.float32) * s, 'Wv': jax.random.normal(k4, (D, KV * DH), dtype=jnp.float32) * s, 'Wo': jax.random.normal(k5, (H * DH, D), dtype=jnp.float32) * s}
    _L0_attn_all = _L0_attn_setup()
    _L0_attn_in = {k: v for k, v in _L0_attn_all.items() if k in ('Wq', 'Wk', 'Wv', 'Wo')}
    del _L0_attn_all

    def _L0_ffn_setup():
        import jax, jax.numpy as jnp
        import numpy as np
        HIDDEN = 256
        NUM_EXPERTS = 8
        TOP_K = 2
        B, S = (4, 256)
        key = jax.random.key(seed)
        ks = jax.random.split(key, 8)
        H, E = (HIDDEN, NUM_EXPERTS)
        sc = lambda fan_in: 1.0 / np.sqrt(fan_in)
        x = jax.random.normal(ks[0], (B, S, H), dtype=jnp.float32)
        Wr = jax.random.uniform(ks[1], (H, E), minval=-sc(H), maxval=sc(H), dtype=jnp.float32)
        br = jax.random.uniform(ks[2], (E,), minval=-sc(H), maxval=sc(H), dtype=jnp.float32)
        W1 = jax.random.uniform(ks[3], (E, H, 2 * H), minval=-sc(H), maxval=sc(H), dtype=jnp.float32)
        b1 = jax.random.uniform(ks[4], (E, 2 * H), minval=-sc(H), maxval=sc(H), dtype=jnp.float32)
        W2 = jax.random.uniform(ks[5], (E, 2 * H, H), minval=-sc(2 * H), maxval=sc(2 * H), dtype=jnp.float32)
        b2 = jax.random.uniform(ks[6], (E, H), minval=-sc(2 * H), maxval=sc(2 * H), dtype=jnp.float32)
        return {'x': x, 'Wr': Wr, 'br': br, 'W1': W1, 'b1': b1, 'W2': W2, 'b2': b2}
    _L0_ffn_all = _L0_ffn_setup()
    _L0_ffn_in = {k: v for k, v in _L0_ffn_all.items() if k in ('Wr', 'br', 'W1', 'b1', 'W2', 'b2')}
    del _L0_ffn_all
    return {'x': x, 'txt': txt, 'L0_tok_log_dt': _L0_tok_in['log_dt'], 'L0_tok_inv_A_real': _L0_tok_in['inv_A_real'], 'L0_tok_A_imag': _L0_tok_in['A_imag'], 'L0_tok_B_ri': _L0_tok_in['B_ri'], 'L0_attn_Wq': _L0_attn_in['Wq'], 'L0_attn_Wk': _L0_attn_in['Wk'], 'L0_attn_Wv': _L0_attn_in['Wv'], 'L0_attn_Wo': _L0_attn_in['Wo'], 'L0_ffn_Wr': _L0_ffn_in['Wr'], 'L0_ffn_br': _L0_ffn_in['br'], 'L0_ffn_W1': _L0_ffn_in['W1'], 'L0_ffn_b1': _L0_ffn_in['b1'], 'L0_ffn_W2': _L0_ffn_in['W2'], 'L0_ffn_b2': _L0_ffn_in['b2']}

def reference(x, txt, L0_tok_log_dt, L0_tok_inv_A_real, L0_tok_A_imag, L0_tok_B_ri, L0_attn_Wq, L0_attn_Wk, L0_attn_Wv, L0_attn_Wo, L0_ffn_Wr, L0_ffn_br, L0_ffn_W1, L0_ffn_b1, L0_ffn_W2, L0_ffn_b2):
    import jax
    import jax.numpy as jnp

    def _L0_tok_ref(log_dt, inv_A_real, A_imag, B_ri, C_ri, L):
        import jax, jax.numpy as jnp
        import numpy as np
        import math
        H = 256
        N = 64
        CH = 1
        SEQ_L = 256
        dt = jnp.exp(log_dt)
        A = -jnp.exp(inv_A_real) + 1j * A_imag
        B = B_ri[..., 0] + 1j * B_ri[..., 1]
        C = C_ri[..., 0] + 1j * C_ri[..., 1]
        dtA = A * dt[:, None]
        dA = (1.0 + dtA / 2) / (1.0 - dtA / 2)
        C_term = C * B[None]
        log_dA = jnp.log(dA)
        V = jnp.exp(log_dA[:, :, None] * jnp.arange(L))
        K = 2.0 * jnp.einsum('chn,hnl->chl', C_term, V).real
        return K.astype(jnp.float32)

    def _L0_attn_ref(x, Wq, Wk, Wv, Wo):
        import jax, jax.numpy as jnp
        import numpy as np
        H, KV, DH = (16, 4, 64)

        def _rotate_half(t):
            t1, t2 = (t[..., :DH // 2], t[..., DH // 2:])
            return jnp.concatenate([-t2, t1], axis=-1)
        B, L, D = x.shape
        G = H // KV
        q = (x @ Wq).reshape(B, L, H, DH)
        k = (x @ Wk).reshape(B, L, KV, DH)
        v = (x @ Wv).reshape(B, L, KV, DH)
        inv_freq = 1.0 / 10000.0 ** (jnp.arange(0, DH, 2, dtype=jnp.float32) / DH)
        t = jnp.arange(L, dtype=jnp.float32)
        freqs = t[:, None] * inv_freq[None, :]
        emb = jnp.concatenate([freqs, freqs], axis=-1)[None, :, None, :]
        cos, sin = (jnp.cos(emb), jnp.sin(emb))
        q = q * cos + _rotate_half(q) * sin
        k = k * cos + _rotate_half(k) * sin
        qg = q.reshape(B, L, KV, G, DH)
        scale = DH ** (-0.5)
        attn = jnp.einsum('bqkgd,bskd->bkgqs', qg, k) * scale
        attn = jax.nn.softmax(attn, axis=-1)
        out = jnp.einsum('bkgqs,bskd->bqkgd', attn, v).reshape(B, L, H * DH)
        return out @ Wo

    def _L0_ffn_ref(x, Wr, br, W1, b1, W2, b2):
        import jax, jax.numpy as jnp
        import numpy as np
        HIDDEN = 256
        NUM_EXPERTS = 8
        TOP_K = 2
        B, S = (4, 256)
        B_, S_, H = x.shape
        xf = x.reshape(-1, H)
        logits = xf @ Wr + br
        topk_w, topk_idx = jax.lax.top_k(logits, TOP_K)
        topk_w = jax.nn.softmax(topk_w, axis=-1)
        gate = jnp.sum(jax.nn.one_hot(topk_idx, NUM_EXPERTS, dtype=xf.dtype) * topk_w[..., None], axis=1)
        h = jax.nn.relu(jnp.einsum('th,ehf->etf', xf, W1) + b1[:, None, :])
        y = jnp.einsum('etf,efh->eth', h, W2) + b2[:, None, :]
        out = jnp.einsum('te,eth->th', gate, y)
        return out.reshape(B_, S_, H)
    h = _L0_tok_ref(L0_tok_log_dt, L0_tok_inv_A_real, L0_tok_A_imag, L0_tok_B_ri, x, 256)
    h = jnp.concatenate([h, txt], axis=1)
    h = h + _L0_attn_ref(_layernorm(h, axis=-1), L0_attn_Wq, L0_attn_Wk, L0_attn_Wv, L0_attn_Wo)
    h = h + _L0_ffn_ref(_layernorm(h, axis=-1), L0_ffn_Wr, L0_ffn_br, L0_ffn_W1, L0_ffn_b1, L0_ffn_W2, L0_ffn_b2)
    return h

_drawn_inputs = setup_inputs


def setup_inputs(seed=0):
    import zlib

    import numpy as np

    out = dict(_drawn_inputs(seed))
    spreads = {}
    factors = {'L0_tok_inv_A_real': 2.679,
     'L0_attn_Wq': 8.0,
     'L0_attn_Wk': 8.0,
     'L0_attn_Wv': 8.0,
     'L0_attn_Wo': 8.0,
     'L0_ffn_br': 27.488,
     'L0_ffn_b1': 58.103,
     'L0_ffn_b2': 30.701,
     'L0_ffn_Wr': 2.799,
     'L0_ffn_W1': 3.988,
     'L0_ffn_W2': 3.003}
    for name, (base, spread) in spreads.items():
        noise = np.random.default_rng([zlib.crc32(name.encode()), seed]).standard_normal(out[name].shape)
        drawn = base * np.exp(spread * noise) if base else spread * noise
        out[name] = jnp.asarray(drawn.astype(out[name].dtype))
    for name, factor in factors.items():
        out[name] = (out[name] * factor).astype(out[name].dtype)
    return out
```

```python
import math
from contextlib import ExitStack

import numpy as np

import concourse.bass as bass
from concourse import mybir

P = 128
NB, SEQ, D = 8, 768, 256
IMG, TXT = 256, 512
NS = 64
HEADS, KV, DH = 16, 4, 64
GH = HEADS // KV
TT = SEQ // P
IT = IMG // P
KC = D // P
TOK = NB * SEQ
NE, FF, TOPK = 8, 512, 2
FC = FF // P
EPS = 1e-5
NIT = NB * KV
QKV = GH * DH + 2 * DH
QK = GH * DH + DH
STRIDE = TOK + P
SLOTS = NE * STRIDE
NT = TOK * TOPK // P + NE

F32 = mybir.dt.float32
F32R = mybir.dt.float32r
I32 = mybir.dt.int32
U32 = mybir.dt.uint32
ALU = mybir.AluOpType
ACT = mybir.ActivationFunctionType
AX = mybir.AxisListType


def hold(eng, sem, value):
    eng.wait_ge(sem, value)
    eng.nop(nofuse=True)


class Tally:

    def __init__(self, eng, sem, base=0):
        self.eng, self.sem, self.base, self.n = eng, sem, base, 0

    def mark(self, ins):
        self.n += 1
        ins.then_inc(self.sem, 1)
        return self.n

    def link(self, ins):
        self.eng.wait_ge(self.sem, self.base + self.mark(ins))


def vandermonde(nc, sem, io, ident, img_d):
    AN, BN = 4, 64
    GM = NB * AN
    HH = IMG // P
    SL = 16
    LOG2E, MAGIC = 1.4426950408889634, 12582912.0
    LN2HI, LN2LO = 0.693359375, -2.12194440e-4
    with ExitStack() as ctx:
        def sb(name, shape, dt=F32):
            return ctx.enter_context(nc.sbuf_tensor(name, shape, dt))

        logdt, dt = sb("logdt", [P, HH]), sb("dt", [P, HH])
        inva, aim = sb("inva", [P, HH, NS]), sb("aim", [P, HH, NS])
        bri = sb("bri", [P, HH, NS, 2])
        cnat = sb("cnat", [P, NB, HH, NS, 2])
        ex = [sb(f"ex{n}", [P, HH]) for n in range(6)]
        exi = sb("exi", [P, HH], I32)
        nat = [sb(f"nat{n}", [P, HH * NS]) for n in range(8)]
        zre, zim = sb("zre", [P, P]), sb("zim", [P, P])
        b2 = sb("b2", [P, HH, NS, 2])
        wre, wim = sb("wre", [P, BN + 1, P]), sb("wim", [P, BN + 1, P])
        ct = sb("ct", [P, NB, 2, P])
        b2t = sb("b2t", [P, 2, P])
        bare, baim = sb("bare", [P, AN, P]), sb("baim", [P, AN, P])
        ure, uim = sb("ure", [P, AN, P]), sb("uim", [P, AN, P])
        gre, gim = sb("gre", [P, NB, AN, P]), sb("gim", [P, NB, AN, P])
        tm = [sb(f"tm{n}", [P, SL, P]) for n in range(4)]
        kt = sb("kt", [P, HH * 32, BN])
        ps = ctx.enter_context(nc.psum_tensor("ps_v", [P, 8, 512], F32))

        loaded_a, loaded_c = sem("v_loaded_a"), sem("v_loaded_c")
        exp_done, dve = sem("v_exp_done"), sem("v_dve")
        nat_ready, tr_z, tr_c = sem("v_nat_ready"), sem("v_tr_z"), sem("v_tr_c")
        ct_ready, g_ready, bank_full, bank_out = sem("v_ct_ready"), sem("v_g_ready"), sem("v_bank_full"), sem("v_bank_out")
        stored = sem("v_stored")
        id_ready = sem("v_id_ready")

        with nc.Block() as block:
            @block.sync
            def _(sp):
                sp.dma_start(logdt[:], io["log_dt"].rearrange("(a p) -> p a", p=P), allow_slow_non_contiguous=True).then_inc(loaded_a, 16)
                sp.dma_start(inva[:], io["inv_A_real"].rearrange("(a p) n -> p a n", p=P)).then_inc(loaded_a, 16)
                sp.dma_start(aim[:], io["A_imag"].rearrange("(a p) n -> p a n", p=P)).then_inc(loaded_a, 16)
                sp.dma_start(bri[:], io["B_ri"].rearrange("(a p) n r -> p a n r", p=P)).then_inc(loaded_a, 16)
                for c in range(NB):
                    sp.dma_start(cnat[:, c], io["x"][c].rearrange("(a p) n r -> p a n r", p=P)).then_inc(loaded_c, 16)
                out = img_d.rearrange("c (q j) (a b) -> j c a q b", j=4, a=AN)
                for hh in range(HH):
                    sp.wait_ge(bank_out, 4 * (hh + 1))
                    for j in range(4):
                        for c in range(NB):
                            sp.dma_start(out[j, c][:, hh * 32:hh * 32 + 32, :],
                                         kt[32 * j + AN * c:32 * j + AN * (c + 1), hh * 32:hh * 32 + 32, :]).then_inc(stored, 16)
                sp.wait_ge(stored, 16 * HH * 4 * NB)

            @block.gpsimd
            def _(pool):
                pool.memset(ident[:], 0.0).then_inc(id_ready, 1)
                pool.wait_ge(id_ready, 1)
                pool.affine_select(out=ident[:], in_=ident[:], compare_op=ALU.not_equal, fill=1.0, base=0,
                                   pattern=[[-1, P]], channel_multiplier=1).then_inc(id_ready, 1)

            @block.scalar
            def _(act):
                act.wait_ge(loaded_a, 64)
                act.activation(nat[0][:], inva[:].rearrange("p a n -> p (a n)"), ACT.Exp).then_inc(exp_done, 1)
                for q in range(4):
                    act.wait_ge(tr_c, q + 1)
                    act.activation(ct[:].rearrange("p c r h -> p (c r h)")[:, 512 * q:512 * q + 512], ps[:, 1 + q], ACT.Copy).then_inc(ct_ready, 1)
                for q in range(8):
                    act.wait_ge(bank_full, q + 1)
                    act.activation(kt[:, 8 * q:8 * q + 8, :], ps[:, q].rearrange("p (q b) -> p q b", b=BN), ACT.Copy).then_inc(bank_out, 1)

            @block.tensor
            def _(pe):
                pe.wait_ge(id_ready, 2)
                pe.wait_ge(loaded_c, 16 * NB)
                for q in range(4):
                    for k in range(4):
                        c, r = (4 * q + k) // 2, k % 2
                        last = pe.transpose(ps[:, 1 + q, P * k:P * k + P], cnat[:, c].rearrange("p a n r -> p (a n) r")[:, :, r], ident[:])
                    last.then_inc(tr_c, 1)
                pe.wait_ge(nat_ready, 1)
                b2v = b2[:].rearrange("p a n r -> p (a n) r")
                for k, src in enumerate((zre[:], zim[:], b2v[:, :, 0], b2v[:, :, 1])):
                    last = pe.transpose(ps[:, 0, P * k:P * k + P], src, ident[:])
                last.then_inc(tr_z, 1)
                pe.wait_ge(g_ready, NB)
                for q in range(8):
                    if q in (1, 2, 3, 4):
                        pe.wait_ge(ct_ready, q)
                    lo = NS * (q // 4)
                    for k in range(8):
                        for j in range(4):
                            h = 4 * (8 * (q % 4) + k) + j
                            for n, (g, w) in enumerate(((gre, wre), (gim, wim))):
                                last = pe.matmul(ps[GM * j:GM * j + GM, q, BN * k:BN * k + BN],
                                                 g[:].rearrange("p c a h -> p (c a) h")[lo:lo + NS, :, h],
                                                 w[lo:lo + NS, 0:BN, h], start=(n == 0), stop=(n == 1))
                    last.then_inc(bank_full, 1)

            @block.vector
            def _(v):
                t = Tally(v, dve)
                link, mark = t.link, t.mark
                v.wait_ge(loaded_a, 64)
                x, tk, kf, r, p, s = (e[:] for e in ex)
                link(v.tensor_scalar(x, logdt[:], 88.0, -87.0, ALU.min, ALU.max))
                link(v.tensor_scalar(tk, x, LOG2E, MAGIC, ALU.mult, ALU.add))
                link(v.tensor_scalar(kf, tk, MAGIC, None, ALU.subtract))
                link(v.scalar_tensor_tensor(out=r, in0=kf, scalar=-LN2HI, in1=x, op0=ALU.mult, op1=ALU.add))
                link(v.scalar_tensor_tensor(out=s, in0=kf, scalar=-LN2LO, in1=r, op0=ALU.mult, op1=ALU.add))
                link(v.tensor_scalar(p, s, 1 / math.factorial(7), None, ALU.mult))
                for n in range(6, 0, -1):
                    link(v.scalar_tensor_tensor(out=p, in0=p, scalar=1 / math.factorial(n), in1=s, op0=ALU.add, op1=ALU.mult))
                link(v.tensor_scalar(exi[:], kf, 127.0, None, ALU.add))
                link(v.tensor_scalar(exi[:], exi[:], 23, None, ALU.logical_shift_left))
                link(v.scalar_tensor_tensor(out=dt[:], in0=p, scalar=1.0, in1=exi[:].bitcast(F32), op0=ALU.add, op1=ALU.mult))
                e, a, w, d1, w2, num, rden, a2 = (n_[:] for n_ in nat)
                v.wait_ge(exp_done, 1)
                for hh in range(HH):
                    cols = slice(hh * NS, hh * NS + NS)
                    v.tensor_scalar(a[:, cols], e[:, cols], dt[:, hh:hh + 1], -0.5, ALU.mult, ALU.mult)
                    link(v.tensor_scalar(w[:, cols], aim[:, hh, :], dt[:, hh:hh + 1], 0.5, ALU.mult, ALU.mult))
                link(v.tensor_scalar(d1, a, -1.0, 1.0, ALU.mult, ALU.add))
                link(v.tensor_tensor(d1, d1, d1, ALU.mult))
                link(v.tensor_tensor(w2, w, w, ALU.mult))
                link(v.tensor_tensor(d1, d1, w2, ALU.add))
                link(v.reciprocal(rden, d1))
                link(v.tensor_tensor(a2, a, a, ALU.mult))
                link(v.tensor_tensor(a2, a2, w2, ALU.add))
                link(v.tensor_scalar(num, a2, -1.0, 1.0, ALU.mult, ALU.add))
                mark(v.tensor_tensor(zre[:], num, rden, ALU.mult))
                mark(v.scalar_tensor_tensor(out=zim[:], in0=w, scalar=2.0, in1=rden, op0=ALU.mult, op1=ALU.mult))
                v.tensor_scalar(b2[:], bri[:], 2.0, None, ALU.mult).then_inc(nat_ready, 1)
                mark(v.memset(wre[:, 0, :], 1.0))
                mark(v.memset(wim[:, 0, :], 0.0))
                mark(v.memset(ure[:, 0, :], 1.0))
                mark(v.memset(uim[:, 0, :], 0.0))
                v.wait_ge(tr_z, 1)
                mark(v.tensor_copy(wre[:, 1, :], ps[:, 0, 0:P]))
                mark(v.tensor_copy(wim[:, 1, :], ps[:, 0, P:2 * P]))
                link(v.tensor_copy(b2t[:], ps[:, 0, 2 * P:4 * P].rearrange("p (r h) -> p r h", r=2)))

                def cmul(ore, oim, ar, ai, br, bi):
                    n = ore.shape[1]
                    t1, t2, t3, t4 = (tm[k][:, 0:n] for k in range(4))
                    mark(v.tensor_tensor(t1, ar, br, ALU.mult))
                    mark(v.tensor_tensor(t2, ai, bi, ALU.mult))
                    mark(v.tensor_tensor(t3, ar, bi, ALU.mult))
                    link(v.tensor_tensor(t4, ai, br, ALU.mult))
                    mark(v.tensor_tensor(ore, t1, t2, ALU.subtract))
                    link(v.tensor_tensor(oim, t3, t4, ALU.add))

                def over(ap, n):
                    return ap.unsqueeze(1).to_broadcast([P, n, P])

                k = 1
                while k < BN:
                    for j in range(0, k, SL):
                        n = min(SL, k - j)
                        cmul(wre[:, k + 1 + j:k + 1 + j + n], wim[:, k + 1 + j:k + 1 + j + n],
                             wre[:, 1 + j:1 + j + n], wim[:, 1 + j:1 + j + n], over(wre[:, k], n), over(wim[:, k], n))
                    k *= 2
                mark(v.tensor_copy(ure[:, 1, :], wre[:, BN, :]))
                link(v.tensor_copy(uim[:, 1, :], wim[:, BN, :]))
                for j in range(2, AN):
                    cmul(ure[:, j:j + 1], uim[:, j:j + 1], ure[:, j - 1:j], uim[:, j - 1:j], ure[:, 1:2], uim[:, 1:2])
                cmul(bare[:], baim[:], ure[:], uim[:], over(b2t[:, 0], AN), over(b2t[:, 1], AN))
                v.wait_ge(ct_ready, 4)
                t1, t2, t3, t4 = (tm[k][:, 0:AN] for k in range(4))
                for c in range(NB):
                    cr, ci = over(ct[:, c, 0], AN), over(ct[:, c, 1], AN)
                    mark(v.tensor_tensor(t1, bare[:], cr, ALU.mult))
                    mark(v.tensor_tensor(t2, baim[:], ci, ALU.mult))
                    mark(v.tensor_tensor(t3, bare[:], ci, ALU.mult))
                    link(v.scalar_tensor_tensor(out=t4, in0=baim[:], scalar=-1.0, in1=cr, op0=ALU.mult, op1=ALU.mult))
                    mark(v.tensor_tensor(gre[:, c], t1, t2, ALU.subtract))
                    v.tensor_tensor(gim[:, c], t4, t3, ALU.subtract).then_inc(g_ready, 1)
                    v.wait_ge(g_ready, c + 1)


def norm_in(nc, sem, io, ident, img_d, xnT_d):
    with ExitStack() as ctx:
        def sb(name, shape, dt=F32):
            return ctx.enter_context(nc.sbuf_tensor(name, shape, dt))

        x = sb("n_x", [P, 2, TT, D])
        st = sb("n_st", [P, TT, 6])
        mv = sb("n_mv", [P, TT, 2])
        ve, sd, y, y2 = (sb(f"n_s{n}", [P, TT]) for n in range(4))
        rstd = sb("n_rstd", [P, TT])
        xn = sb("n_xn", [P, 2, TT, D])
        xt = sb("n_xt", [P, 2, KC, SEQ])
        ps = ctx.enter_context(nc.psum_tensor("ps_n", [P, 2, 3, 512], F32))
        x_in = [sem(f"n_x_in{q}") for q in range(2)]
        xn_free, ps_free = sem("n_xn_free"), sem("n_ps_free")
        dve, var_ready, sd_ready, xn_ready = sem("n_dve"), sem("n_var_ready"), sem("n_sd_ready"), sem("n_xn_ready")
        tr_done, xt_ready = sem("n_tr_done"), sem("n_xt_ready")
        stored = [sem(f"n_stored{q}") for q in range(2)]
        LINKS = 2 * TT + 5

        with nc.Block() as block:
            @block.sync
            def _(sp):
                def load(b, q):
                    sp.dma_start(x[:, q, 0:IT, :], img_d[b].rearrange("(t p) d -> p t d", p=P)).then_inc(x_in[q], 16)
                    sp.dma_start(x[:, q, IT:TT, :], io["txt"][b].rearrange("(t p) d -> p t d", p=P)).then_inc(x_in[q], 16)

                for q in range(2):
                    sp.nop().then_inc(stored[q], 16)
                    load(q, q)
                with sp.Fori(1, NB // 2) as k:
                    for q in range(2):
                        sp.wait_ge(xn_ready, k * 2 + q - 1)
                        load(k * 2 + q, q)

            @block.vector
            def _(v):
                with v.Fori(0, NB // 2) as k:
                    for q in range(2):
                        b = k * 2 + q
                        t = Tally(v, dve, b * LINKS)
                        link, mark = t.link, t.mark
                        hold(v, x_in[q], k * 32 + 32)
                        for i in range(TT):
                            mark(v.bn_stats(st[:, i, :], x[:, q, i, :]))
                        hold(v, dve, t.base + t.n)
                        for i in range(TT):
                            mark(v.bn_aggr(mv[:, i, :], st[:, i, :]))
                        v.wait_ge(dve, t.base + t.n)
                        v.tensor_scalar(ve[:], mv[:, :, 1], EPS, None, ALU.add).then_inc(var_ready, 1)
                        v.wait_ge(sd_ready, b + 1)
                        link(v.reciprocal(y[:], sd[:]))
                        link(v.tensor_tensor(y2[:], y[:], y[:], ALU.mult))
                        link(v.tensor_tensor(y2[:], y2[:], ve[:], ALU.mult))
                        link(v.tensor_scalar(y2[:], y2[:], -0.5, 1.5, ALU.mult, ALU.add))
                        link(v.tensor_tensor(rstd[:], y[:], y2[:], ALU.mult))
                        assert t.n == LINKS
                        v.wait_ge(xn_free, b + 1)
                        for i in range(TT):
                            last = v.tensor_scalar(xn[:, q, i, :], x[:, q, i, :], mv[:, i, 0:1], rstd[:, i:i + 1], ALU.subtract, ALU.mult)
                        last.then_inc(xn_ready, 1)

            @block.tensor
            def _(pe):
                pe.nop().then_inc(xn_free, 2)
                with pe.Fori(0, NB // 2) as k:
                    for q in range(2):
                        pe.wait_ge(xn_ready, k * 2 + q + 1)
                        pe.wait_ge(ps_free, k * 2 + q + 1)
                        for n in range(3):
                            for m in range(4):
                                c, i = (4 * n + m) // TT, (4 * n + m) % TT
                                last = pe.transpose(ps[:, q, n, P * m:P * m + P], xn[:, q, i, P * c:P * c + P], ident[:])
                            if n < 2:
                                last.then_inc(tr_done, 1)
                        last.then_inc(xn_free, 1)

            @block.scalar
            def _(act):
                act.nop().then_inc(ps_free, 2)
                with act.Fori(0, NB // 2) as k:
                    for q in range(2):
                        b = k * 2 + q
                        act.wait_ge(var_ready, b + 1)
                        act.activation(sd[:], ve[:], ACT.Sqrt).then_inc(sd_ready, 1)
                        act.wait_ge(stored[q], k * 16 + 16)
                        for n in range(3):
                            if n < 2:
                                act.wait_ge(tr_done, b * 2 + n + 1)
                            else:
                                act.wait_ge(xn_free, b + 3)
                            out = act.activation(xt[:, q].rearrange("p c s -> p (c s)")[:, 512 * n:512 * n + 512], ps[:, q, n], ACT.Copy)
                            if n < 2:
                                out.then_inc(xt_ready, 1)
                        out.then_inc(ps_free, 1)
                        act.wait_ge(ps_free, b + 3)
                        act.dma_start(xnT_d[b], xt[:, q]).then_inc(stored[q], 16)
                for q in range(2):
                    act.wait_ge(stored[q], 16 * (NB // 2) + 16)


def attention(nc, sem, io, ident, xnT_d, oT_d):
    LAG = 3
    STEPS = GH * TT
    HALF = SEQ // 2
    CT = HALF // P
    GRP = 2 * CT
    NG = STEPS // GRP
    RING = 4
    HL = 2 * DH
    PROJ_AT = [3 * t for t in range(TT)]
    TRQ_AT = [3 * t + 4 for t in range(TT)]
    TRK_AT = [3 * t + 5 for t in range(TT)]
    VCOPY_AT = 22
    LOADS = (1 + 3 * KC) * 16
    LINKS = 4 * TT
    with ExitStack() as ctx:
        def sb(name, shape, dt=F32):
            return ctx.enter_context(nc.sbuf_tensor(name, shape, dt))

        cos, sin = sb("a_cos", [P, TT, QK]), sb("a_sin", [P, TT, QK])
        xnT = sb("a_xnT", [P, KC, SEQ])
        wg = sb("a_wg", [P, KC, QKV])
        raw = sb("a_raw", [P, TT, QKV])
        m1, m2, rot = sb("a_m1", [P, QK]), sb("a_m2", [P, QK]), sb("a_rot", [P, QK])
        qs = sb("a_qs", [P, 2, (GH + 1) * HL + DH])
        qT = sb("a_qT", [P, 2, GH, SEQ], F32R)
        kT = sb("a_kT", [P, 2, 2, SEQ], F32R)
        val = sb("a_val", [P, 2, TT, DH])
        nmax, rsum, inv = sb("a_nmax", [P, RING]), sb("a_rsum", [P, RING]), sb("a_inv", [P, RING])
        prob = sb("a_prob", [P, RING, SEQ])
        probT = sb("a_probT", [P, 2, TT, 2, HALF])
        oT = sb("a_oT", [P, 2, HALF])
        S = ctx.enter_context(nc.psum_tensor("ps_s", [P, 2, 2, 512], F32))
        T = ctx.enter_context(nc.psum_tensor("ps_t", [P, 2, 512], F32))
        O = ctx.enter_context(nc.psum_tensor("ps_o", [P, 512], F32))
        X = ctx.enter_context(nc.psum_tensor("ps_x", [P, 512], F32))

        tables_in, xw_in = sem("a_tables_in"), sem("a_xw_in")
        proj_done, trq_done, trk_done = sem("a_proj_done"), sem("a_trq_done"), sem("a_trk_done")
        raw_ready, qs_ready, q_ready, k_ready, v_ready = (sem(f"a_{n}_ready") for n in ("raw", "qs", "q", "k", "v"))
        dve, hi_ready = sem("a_dve"), sem("a_hi_ready")
        scores_ready, max_ready, exp_ready, inv_ready, norm_ready = (sem(f"a_{n}_ready") for n in ("scores", "max", "exp", "inv", "norm"))
        t_done, probT_ready, pv_done, o_out = sem("a_t_done"), sem("a_probT_ready"), sem("a_pv_done"), sem("a_o_out")
        o_stored = [sem(f"a_o_stored{q}") for q in range(2)]

        def wait(eng, s, value):
            if not isinstance(value, int) or value > 0:
                eng.wait_ge(s, value)

        def loop(eng, iteration, drain):
            iteration(0, 0)
            with eng.Fori(0, (NIT - 2) // 2) as k:
                iteration(k * 2 + 1, 1)
                iteration(k * 2 + 2, 0)
            iteration(NIT - 1, 1)
            if drain:
                drain()

        def real(i, n):
            return n >= 0 or not (isinstance(i, int) and i == 0)

        last_it = lambda i: isinstance(i, int) and i == NIT - 1

        def where(s):
            s %= STEPS
            return (s // GRP) % 2, (s % GRP) // 2, s % 2, s // GRP // 2

        with nc.Block() as block:
            @block.sync
            def _(sp):
                sp.dma_start(cos[:], io["cos"]).then_inc(tables_in, 16)
                sp.dma_start(sin[:], io["sin"]).then_inc(tables_in, 16)

                def load(n, b, g):
                    wait(sp, proj_done, n * TT)
                    sp.dma_start(xnT[:], xnT_d[b]).then_inc(xw_in, 16)
                    for c in range(KC):
                        rows = slice(P * c, P * c + P)
                        sp.dma_start(wg[:, c, 0:GH * DH], io["Wq"][rows, GH * DH * g:GH * DH * (g + 1)]).then_inc(xw_in, 16)
                        sp.dma_start(wg[:, c, GH * DH:QK], io["Wk"][rows, DH * g:DH * (g + 1)]).then_inc(xw_in, 16)
                        sp.dma_start(wg[:, c, QK:QKV], io["Wv"][rows, DH * g:DH * (g + 1)]).then_inc(xw_in, 16)

                load(0, 0, 0)
                for g in range(1, KV):
                    load(g, 0, g)
                with sp.Fori(1, NB) as b:
                    for g in range(KV):
                        load(b * KV + g, b, g)

            @block.tensor
            def _(pe):
                def project(n, t):
                    if t == 0:
                        pe.wait_ge(xw_in, n * LOADS + LOADS)
                        wait(pe, k_ready, n * TT)
                    elif t == 1:
                        pe.wait_ge(raw_ready, n * TT + 1)
                    else:
                        pe.wait_ge(k_ready, n * TT + t - 1)
                    for c in range(KC):
                        last = pe.matmul(X[:, 0:QKV], xnT[:, c, P * t:P * t + P], wg[:, c, :], start=(c == 0), stop=(c == KC - 1))
                    last.then_inc(proj_done, 1)

                def turn_q(n, t):
                    pe.wait_ge(qs_ready, n * TT + t + 1)
                    if t < TT - 1:
                        pe.wait_ge(raw_ready, n * TT + t + 2)
                    else:
                        pe.wait_ge(k_ready, n * TT + t)
                    for h in range(GH):
                        last = pe.transpose(X[:, P * h:P * h + P], qs[:, t % 2, HL * h:HL * h + HL], ident[:])
                    last.then_inc(trq_done, 1)

                def turn_k(n, t):
                    pe.wait_ge(q_ready, n * TT + t + 1)
                    for h in range(2):
                        at = GH * HL + DH * h
                        last = pe.transpose(X[:, P * h:P * h + P], qs[:, t % 2, at:at + HL], ident[:])
                    last.then_inc(trk_done, 1)

                def scores(i, par, s):
                    hp, t, j, c = where(s)
                    if s == 0:
                        pe.wait_ge(k_ready, i * TT + TT)
                    wait(pe, exp_ready, i * STEPS + s - 1)
                    for r in range(2):
                        for w in range(2):
                            last = pe.matmul(S[:, s % 2, r, 0:HALF], qT[:, par, 2 * hp + j, HALF * c + P * t:HALF * c + P * t + P],
                                             kT[:, par, w, HALF * r:HALF * r + HALF], start=(w == 0), stop=(w == 1))
                    last.then_inc(scores_ready, 1)

                def turn_probs(i, s):
                    pe.wait_ge(norm_ready, i * STEPS + s + 1)
                    for half in range(2):
                        wait(pe, probT_ready, (i * STEPS + s) * 2 - 1 + half)
                        for n in range(CT):
                            kt = CT * half + n
                            last = pe.transpose(T[:, half, P * n:P * n + P], prob[:, s % RING, P * kt:P * kt + P], ident[:])
                        last.then_inc(t_done, 1)

                def values(i, par, g, kt):
                    if kt == 0:
                        pe.wait_ge(probT_ready, (i * NG + g) * 2 * GRP + 2 * GRP)
                        wait(pe, o_out, i * NG + g)
                    for j in range(2):
                        last = pe.matmul(O[DH * j:DH * j + DH, 0:HALF], val[:, (par + (g < 0)) % 2, kt, :], probT[:, g % 2, kt, j, :],
                                         start=(kt == 0), stop=(kt == TT - 1))
                    if kt == TT - 1:
                        last.then_inc(pv_done, 1)

                def back(i, par, s):
                    if real(i, s - LAG) and s - LAG < STEPS:
                        turn_probs(i, s - LAG)
                    g, kt = (s - LAG - GRP) // GRP, (s - LAG - GRP) % GRP
                    if real(i, g):
                        values(i, par, g, kt)

                def iteration(i, par):
                    for s in range(STEPS):
                        scores(i, par, s)
                        if not last_it(i):
                            if s in PROJ_AT:
                                project(i + 1, PROJ_AT.index(s))
                            if s in TRQ_AT:
                                turn_q(i + 1, TRQ_AT.index(s))
                            if s in TRK_AT:
                                turn_k(i + 1, TRK_AT.index(s))
                        back(i, par, s)

                def drain():
                    for s in range(STEPS, STEPS + LAG + GRP):
                        back(NIT - 1, 1, s)

                project(0, 0)
                for t in range(TT):
                    if t < TT - 1:
                        project(0, t + 1)
                    turn_q(0, t)
                    turn_k(0, t)
                loop(pe, iteration, drain)

            @block.scalar
            def _(act):
                def copy_raw(n, t):
                    act.wait_ge(proj_done, n * TT + t + 1)
                    if t == 0:
                        wait(act, v_ready, n)
                    act.activation(raw[:, t, :], X[:, 0:QKV], ACT.Copy).then_inc(raw_ready, 1)

                def exps(i, s):
                    act.wait_ge(max_ready, i * STEPS + s + 1)
                    wait(act, t_done, (i * STEPS + s - RING + 1) * 2)
                    act.activation(prob[:, s % RING, :].rearrange("p (r k) -> p r k", r=2), S[:, s % 2, :, 0:HALF], ACT.Exp,
                                   bias=nmax[:, s % RING:s % RING + 1], scale=1.0,
                                   accum_out=rsum[:, s % RING:s % RING + 1]).then_inc(exp_ready, 1)

                def copy_probT(i, s):
                    hp, t, j, c = where(s)
                    g = s // GRP
                    if s % GRP == 0:
                        wait(act, pv_done, i * NG + g - 1)
                    for half in range(2):
                        act.wait_ge(t_done, (i * STEPS + s) * 2 + half + 1)
                        act.activation(probT[:, g % 2, CT * half:CT * half + CT, j, P * t:P * t + P],
                                       T[:, half, 0:HALF].rearrange("p (k q) -> p k q", k=CT), ACT.Copy).then_inc(probT_ready, 1)

                def copy_o(i, g):
                    act.wait_ge(pv_done, i * NG + g + 1)
                    wait(act, o_stored[g % 2], (i * (NG // 2) + g // 2) * 16)
                    act.activation(oT[:, g % 2, :], O[:, 0:HALF], ACT.Copy).then_inc(o_out, 1)

                def store_o(i, g):
                    act.wait_ge(o_out, i * NG + g + 1)
                    it, gg = (i, g) if g >= 0 else (i - 1, g + NG)
                    act.dma_start(oT_d[it][:, gg % 2, HALF * (gg // 2):HALF * (gg // 2) + HALF], oT[:, g % 2, :]).then_inc(o_stored[g % 2], 16)

                def back(i, s):
                    g, k = (s - LAG - 2 * GRP) // GRP, (s - LAG - 2 * GRP) % GRP
                    if k == 0 and real(i, g):
                        copy_o(i, g)
                    n = s - LAG
                    if real(i, n) and n < STEPS:
                        copy_probT(i, n)
                    if k == 1 and real(i, g):
                        store_o(i, g)

                def iteration(i, par):
                    for s in range(STEPS):
                        if real(i, s - 1):
                            exps(i, s - 1)
                        if not last_it(i) and s in PROJ_AT:
                            copy_raw(i + 1, PROJ_AT.index(s))
                        back(i, s)

                def drain():
                    exps(NIT - 1, STEPS - 1)
                    for s in range(STEPS, STEPS + LAG + GRP + 2):
                        back(NIT - 1, s)
                    for q in range(2):
                        act.wait_ge(o_stored[q], NIT * NG // 2 * 16)

                for t in range(TT):
                    copy_raw(0, t)
                loop(act, iteration, drain)

            @block.gpsimd
            def _(pool):
                with pool.Fori(0, NIT * STEPS // RING) as k:
                    for s in range(RING):
                        hold(pool, inv_ready, k * RING + s + 1)
                        pool.tensor_scalar(prob[:, s, :], prob[:, s, :], inv[:, s:s + 1], 1.0, ALU.mult, ALU.mult).then_inc(norm_ready, 1)

            @block.vector
            def _(v):
                def heads(ap):
                    return ap.rearrange("p (h d) -> p h d", d=DH)

                def rotate(n, t, part):
                    k = Tally(v, dve, n * LINKS + t * 4)
                    x, c, s = raw[:, t, 0:QK], cos[:, t, :], sin[:, t, :]
                    lo, hi = slice(0, DH // 2), slice(DH // 2, DH)
                    parts = qs[:, t % 2, 0:(GH + 1) * HL].rearrange("p (h r d) -> p h r d", r=2, d=DH)
                    if part == 0:
                        v.wait_ge(raw_ready, n * TT + t + 1)
                        k.mark(v.tensor_tensor(m1[:], x, c, ALU.mult))
                        k.mark(v.tensor_tensor(heads(m2[:])[:, :, lo], heads(x)[:, :, hi], heads(s)[:, :, lo], ALU.mult))
                        k.mark(v.tensor_tensor(heads(m2[:])[:, :, hi], heads(x)[:, :, lo], heads(s)[:, :, hi], ALU.mult))
                    elif part == 1:
                        v.wait_ge(dve, k.base + 3)
                        v.tensor_tensor(rot[:], m1[:], m2[:], ALU.add).then_inc(dve, 1)
                        v.wait_ge(dve, k.base + 4)
                        v.tensor_copy(parts[:, :, 0, :].bitcast(F32R), heads(rot[:])).then_inc(hi_ready, 1)
                    else:
                        v.wait_ge(hi_ready, n * TT + t + 1)
                        v.tensor_copy(qs[:, t % 2, (GH + 1) * HL:], parts[:, GH, 0, :])
                        v.tensor_tensor(parts[:, :, 1, :].bitcast(F32R), heads(rot[:]), parts[:, :, 0, :], ALU.subtract).then_inc(qs_ready, 1)

                def copy_q(n, par, t):
                    v.wait_ge(trq_done, n * TT + t + 1)
                    v.tensor_copy(qT[:, par, :, P * t:P * t + P], X[:].rearrange("p (h q) -> p h q", h=GH)).then_inc(q_ready, 1)

                def copy_k(n, par, t):
                    v.wait_ge(trk_done, n * TT + t + 1)
                    v.tensor_copy(kT[:, par, :, P * t:P * t + P], X[:, 0:2 * P].rearrange("p (h q) -> p h q", h=2)).then_inc(k_ready, 1)

                def copy_v(n, par):
                    wait(v, pv_done, (n - 1) * NG)
                    v.tensor_copy(val[:, par], raw[:, :, QK:QKV]).then_inc(v_ready, 1)

                def maxima(i, s):
                    v.wait_ge(scores_ready, i * STEPS + s + 1)
                    v.tensor_reduce(nmax[:, s % RING:s % RING + 1], S[:, s % 2, :, 0:HALF], AX.XY, ALU.max, negate=True).then_inc(max_ready, 1)

                def invert(i, s):
                    v.wait_ge(exp_ready, i * STEPS + s + 1)
                    v.reciprocal(inv[:, s % RING:s % RING + 1], rsum[:, s % RING:s % RING + 1]).then_inc(inv_ready, 1)

                def iteration(i, par):
                    for s in range(STEPS):
                        maxima(i, s)
                        if real(i, s - 1):
                            invert(i, s - 1)
                        if not last_it(i):
                            if s in TRK_AT:
                                copy_k(i + 1, 1 - par, TRK_AT.index(s))
                            if s in TRQ_AT:
                                copy_q(i + 1, 1 - par, TRQ_AT.index(s))
                            for part in range(3):
                                if s - 1 - part in PROJ_AT:
                                    rotate(i + 1, PROJ_AT.index(s - 1 - part), part)
                            if s == VCOPY_AT:
                                copy_v(i + 1, 1 - par)

                v.wait_ge(tables_in, 32)
                for t in range(TT):
                    for part in range(3):
                        rotate(0, t, part)
                    copy_q(0, 0, t)
                    copy_k(0, 0, t)
                copy_v(0, 0)
                loop(v, iteration, lambda: invert(NIT - 1, STEPS - 1))


def route(nc, sem, io, ident, img_d, oT_d, xs_d, h1, pos, gate, run, base):
    with ExitStack() as ctx:
        def sb(name, shape, dt=F32):
            return ctx.enter_context(nc.sbuf_tensor(name, shape, dt))

        wo = sb("r_wo", [P, KV * 2, D])
        wr, br = sb("r_wr", [P, KC, NE]), sb("r_br", [P, NE])
        below, ones = sb("r_below", [P, P]), sb("r_ones", [P, P])
        eight = sb("r_eight", [P, NE])
        oT = sb("r_oT", [P, 3, KV, 2, P])
        st, mv = sb("r_st", [P, TT, 6]), sb("r_mv", [P, TT, 2])
        ve, sd, y, y2, rstd = (sb(f"r_s{n}", [P, TT]) for n in range(5))
        xn = sb("r_xn", [P, 2, TT, D])
        xT = sb("r_xT", [P, KC, SEQ])
        lg, m8, i8 = sb("r_lg", [P, TT, NE]), sb("r_m8", [P, TT, 8]), sb("r_i8", [P, TT, 8], U32)
        top = sb("r_top", [P, TT, TOPK])
        hot = sb("r_hot", [P, TOPK, TT, NE])
        mask, off, slot = sb("r_mask", [P, TT, NE]), sb("r_off", [P, TT, NE]), sb("r_slot", [P, TT, NE])
        pick = sb("r_pick", [P, TOPK, TT, NE])
        posf = sb("r_posf", [P, TOPK, TT])
        idx = sb("r_idx", [P, 2, TOPK, TT], U32)
        gr = sb("r_gr", [P, TT])
        dl, ex, den = (sb(f"r_g{n}", [P, TT]) for n in range(3))
        A = ctx.enter_context(nc.psum_tensor("ps_ra", [P, 2, 512], F32))
        XT = ctx.enter_context(nc.psum_tensor("ps_rx", [P, 3, 512], F32))
        L = ctx.enter_context(nc.psum_tensor("ps_rl", [P, 512], F32))
        C = ctx.enter_context(nc.psum_tensor("ps_rc", [P, 2, TT, NE], F32))

        w_in, h_in, const = sem("r_w_in"), sem("r_h_in"), sem("r_const")
        oT_in = [sem(f"r_oT_in{q}") for q in range(3)]
        oT_free, h1_ready, var_ready, sd_ready, xn_ready = (sem(f"r_{n}") for n in ("oT_free", "h1_ready", "var_ready", "sd_ready", "xn_ready"))
        rstd_ready, run_ready, xn_free = sem("r_rstd_ready"), sem("r_run_ready"), sem("r_xn_free")
        tr_done, xT_ready, lg_done = sem("r_tr_done"), sem("r_xT_ready"), sem("r_lg_done")
        mask_ready, count_done, gap_ready, ex_ready, idx_ready = (sem(f"r_{n}") for n in ("mask_ready", "count_done", "gap_ready", "ex_ready", "idx_ready"))
        norm_dve, pick_dve, place_dve = sem("r_norm_dve"), sem("r_pick_dve"), sem("r_place_dve")
        scattered = [sem(f"r_scattered{q}") for q in range(2)]
        NORM, PICK, PLACE = 2 * TT + 4, 2 * TT + 4, TT + 8

        def loop(iteration, drain, eng):
            iteration(0, 0)
            with eng.Fori(0, (NB - 2) // 2) as k:
                iteration(k * 2 + 1, 1)
                iteration(k * 2 + 2, 0)
            iteration(NB - 1, 1)
            drain()

        first = lambda b: isinstance(b, int) and b == 0


        with nc.Block() as block:
            @block.sync
            def _(sp):
                sp.dma_start(wo[:], io["Wo"].rearrange("(k p) n -> p k n", p=P)).then_inc(w_in, 16)
                sp.dma_start(wr[:], io["Wr"].rearrange("(k p) n -> p k n", p=P)).then_inc(w_in, 16)
                sp.dma_start(br[:], io["br"].unsqueeze(0).to_broadcast([P, NE])).then_inc(w_in, 16)
                with sp.Fori(0, NB) as b:
                    sp.dma_start(h1[:, b, 0:IT, :], img_d[b].rearrange("(t p) d -> p t d", p=P)).then_inc(h_in, 16)
                    sp.dma_start(h1[:, b, IT:TT, :], io["txt"][b].rearrange("(t p) d -> p t d", p=P)).then_inc(h_in, 16)
                oT_b = oT_d.rearrange("(b g) p h s -> b p g h s", g=KV)
                sp.nop().then_inc(oT_free, 3)
                with sp.Fori(0, NB) as b:
                    for t in range(TT):
                        sp.wait_ge(oT_free, b * TT + t + 1)
                        for g in range(KV):
                            sp.dma_start(oT[:, t % 3, g], oT_b[b][:, g, :, P * t:P * t + P]).then_inc(oT_in[t % 3], 16)

            @block.gpsimd
            def _(pool):
                pool.memset(ones[:], 1.0).then_inc(const, 1)
                pool.wait_ge(const, 1)
                pool.affine_select(out=below[:], in_=ones[:], compare_op=ALU.is_gt, fill=0.0, base=0,
                                   pattern=[[1, P]], channel_multiplier=-1).then_inc(const, 1)
                pool.iota(eight[:], [[1, NE]], base=0, channel_multiplier=0, allow_small_or_imprecise_dtypes=True).then_inc(const, 1)
                pool.iota(base[:], [[STRIDE, NE]], base=0, channel_multiplier=0, allow_small_or_imprecise_dtypes=True).then_inc(const, 1)
                pool.nop().then_inc(xn_free, 2)
                with pool.Fori(0, NB // 2) as k:
                    for q in range(2):
                        hold(pool, idx_ready, k * 2 + q + 2)
                        for t in range(TT):
                            for e in range(TOPK):
                                pool.indirect_dma_start(out=xs_d, out_offset=bass.IndirectOffsetOnAxis(ap=idx[:, q, e, t:t + 1], axis=0),
                                                        in_=xn[:, q, t, :], in_offset=None).then_inc(scattered[q], 16)
                        pool.wait_ge(scattered[q], k * (TT * TOPK * 16) + TT * TOPK * 16)
                        pool.nop().then_inc(xn_free, 1)

            @block.tensor
            def _(pe):
                def project(b):
                    for t in range(TT):
                        pe.wait_ge(oT_in[t % 3], b * (TT // 3 * KV * 16) + (t // 3 + 1) * KV * 16)
                        pe.wait_ge(h1_ready, b * TT + t + 1)
                        for c in range(KV * 2):
                            last = pe.matmul(A[:, t % 2, 0:D], oT[:, t % 3, c // 2, c % 2, :], wo[:, c, :], start=(c == 0), stop=(c == KV * 2 - 1))
                        last.then_inc(oT_free, 1)

                def logits(b, q):
                    pe.wait_ge(xn_ready, b + 1)
                    for n in range(3):
                        for m in range(4):
                            c, t = (4 * n + m) // TT, (4 * n + m) % TT
                            last = pe.transpose(XT[:, n, P * m:P * m + P], xn[:, q, t, P * c:P * c + P], ident[:])
                        last.then_inc(tr_done, 1)
                    pe.wait_ge(xT_ready, b * 3 + 3)
                    pe.wait_ge(mask_ready, b + 1)
                    for t in range(TT):
                        for c in range(KC):
                            last = pe.matmul(L[:, NE * t:NE * t + NE], xT[:, c, P * t:P * t + P], wr[:, c, :], start=(c == 0), stop=(c == KC - 1))
                    last.then_inc(lg_done, 1)

                def counts(b):
                    pe.wait_ge(mask_ready, b + 2)
                    pe.wait_ge(idx_ready, b + 1)
                    m = mask[:].rearrange("p t e -> p (t e)")
                    pe.matmul(C[:, 0].rearrange("p t e -> p (t e)"), below[:], m, start=True, stop=True)
                    pe.matmul(C[:, 1].rearrange("p t e -> p (t e)"), ones[:], m, start=True, stop=True).then_inc(count_done, 1)

                def iteration(b, q):
                    if not first(b):
                        logits(b - 1, 1 - q)
                    project(b)
                    if not first(b):
                        counts(b - 1)

                def drain():
                    logits(NB - 1, 1)
                    counts(NB - 1)

                pe.wait_ge(w_in, 48)
                pe.wait_ge(const, 4)
                loop(iteration, drain, pe)

            @block.scalar
            def _(act):
                def root(b):
                    act.wait_ge(var_ready, b + 1)
                    act.activation(sd[:], ve[:], ACT.Sqrt).then_inc(sd_ready, 1)

                def turned(b):
                    for n in range(3):
                        act.wait_ge(tr_done, b * 3 + n + 1)
                        act.activation(xT[:].rearrange("p c s -> p (c s)")[:, 512 * n:512 * n + 512], XT[:, n], ACT.Copy).then_inc(xT_ready, 1)

                def exp_gap(b):
                    act.wait_ge(gap_ready, b + 1)
                    act.activation(ex[:], dl[:], ACT.Exp).then_inc(ex_ready, 1)

                def iteration(b, q):
                    if not first(b):
                        turned(b - 1)
                        exp_gap(b - 1)
                    root(b)

                def drain():
                    turned(NB - 1)
                    exp_gap(NB - 1)

                loop(iteration, drain, act)

            @block.vector
            def _(v):
                def norm(b, q):
                    k = Tally(v, norm_dve, b * NORM)
                    if first(b):
                        v.wait_ge(h_in, 16 * 2 * NB)
                    for t in range(TT):
                        v.wait_ge(oT_free, b * TT + t + 4)
                        v.tensor_tensor(h1[:, b, t, :], A[:, t % 2, 0:D], h1[:, b, t, :], ALU.add).then_inc(h1_ready, 1)
                    for t in range(TT):
                        hold(v, h1_ready, b * TT + t + 3)
                        k.mark(v.bn_stats(st[:, t, :], h1[:, b, t, :]))
                    hold(v, norm_dve, k.base + k.n)
                    for t in range(TT):
                        k.mark(v.bn_aggr(mv[:, t, :], st[:, t, :]))
                    v.wait_ge(norm_dve, k.base + k.n)
                    v.tensor_scalar(ve[:], mv[:, :, 1], EPS, None, ALU.add).then_inc(var_ready, 1)
                    v.wait_ge(sd_ready, b + 1)
                    k.link(v.reciprocal(y[:], sd[:]))
                    k.link(v.tensor_tensor(y2[:], y[:], y[:], ALU.mult))
                    k.link(v.tensor_tensor(y2[:], y2[:], ve[:], ALU.mult))
                    k.link(v.tensor_scalar(y2[:], y2[:], -0.5, 1.5, ALU.mult, ALU.add))
                    assert k.n == NORM
                    v.tensor_tensor(rstd[:], y[:], y2[:], ALU.mult).then_inc(rstd_ready, 1)
                    v.wait_ge(rstd_ready, b + 1)
                    v.wait_ge(xn_free, b + 1)
                    for t in range(TT):
                        last = v.tensor_scalar(xn[:, q, t, :], h1[:, b, t, :], mv[:, t, 0:1], rstd[:, t:t + 1], ALU.subtract, ALU.mult)
                    last.then_inc(xn_ready, 1)

                def choose(b):
                    k = Tally(v, pick_dve, b * PICK)
                    v.wait_ge(lg_done, b + 1)
                    k.mark(v.tensor_tensor(lg[:], L[:, 0:TT * NE].rearrange("p (t e) -> p t e", e=NE), br[:].unsqueeze(1).to_broadcast([P, TT, NE]), ALU.add))
                    hold(v, pick_dve, k.base + k.n)
                    for t in range(TT):
                        k.mark(v.max(m8[:, t, :], lg[:, t, :]))
                    hold(v, pick_dve, k.base + k.n)
                    for t in range(TT):
                        k.mark(v.max_index(i8[:, t, :], m8[:, t, :], lg[:, t, :]))
                    v.wait_ge(pick_dve, k.base + k.n)
                    k.link(v.tensor_copy(top[:], i8[:, :, 0:TOPK]))
                    for e in range(TOPK):
                        k.mark(v.tensor_tensor(hot[:, e], eight[:].unsqueeze(1).to_broadcast([P, TT, NE]),
                                               top[:, :, e:e + 1].to_broadcast([P, TT, NE]), ALU.is_equal))
                    v.wait_ge(pick_dve, k.base + k.n)
                    assert k.n == PICK
                    v.tensor_tensor(mask[:], hot[:, 0], hot[:, 1], ALU.add).then_inc(mask_ready, 1)
                    v.tensor_tensor(dl[:], m8[:, :, 1], m8[:, :, 0], ALU.subtract).then_inc(gap_ready, 1)

                def place(b, q):
                    k = Tally(v, place_dve, b * PLACE)
                    v.wait_ge(ex_ready, b + 1)
                    k.link(v.tensor_scalar(den[:], ex[:], 1.0, None, ALU.add))
                    k.link(v.reciprocal(gr[:], den[:]))
                    v.tensor_copy(gate[:, b, 0, :], gr[:])
                    v.tensor_tensor(gate[:, b, 1, :], ex[:], gr[:], ALU.mult)
                    v.wait_ge(count_done, b + 1)
                    k.link(v.tensor_copy(off[:, 0, :], run[:]))
                    for t in range(TT):
                        out = off[:, t + 1, :] if t < TT - 1 else run[:]
                        k.link(v.tensor_tensor(out, off[:, t, :], C[:, 1, t, :], ALU.add))
                    k.link(v.tensor_tensor(slot[:], off[:], C[:, 0], ALU.add))
                    for e in range(TOPK):
                        k.mark(v.tensor_tensor(pick[:, e], hot[:, e], slot[:], ALU.mult))
                    v.wait_ge(place_dve, k.base + k.n)
                    k.mark(v.tensor_reduce(posf[:], pick[:], AX.X, ALU.add))
                    v.wait_ge(place_dve, k.base + k.n)
                    k.mark(v.tensor_copy(pos[:, b, :, :], posf[:]))
                    assert k.n == PLACE, k.n
                    v.tensor_copy(idx[:, q], posf[:]).then_inc(idx_ready, 1)

                def iteration(b, q):
                    if not first(b):
                        choose(b - 1)
                    norm(b, q)
                    if not first(b):
                        place(b - 1, 1 - q)

                def drain():
                    choose(NB - 1)
                    place(NB - 1, 1)

                v.nop().then_inc(h1_ready, 2)
                v.nop().then_inc(mask_ready, 1)
                v.nop().then_inc(idx_ready, 1)
                v.wait_ge(w_in, 48)
                v.wait_ge(const, 4)
                v.tensor_copy(run[:], base[:]).then_inc(run_ready, 1)
                v.wait_ge(run_ready, 1)
                loop(iteration, drain, v)


def tiles(nc, sem, xs_d, run, base, pos, exp_i, src_i, tail_i):
    with ExitStack() as ctx:
        def sb(name, shape, dt=F32):
            return ctx.enter_context(nc.sbuf_tensor(name, shape, dt))

        n, cnt, end = sb("t_n", [P, NE]), sb("t_cnt", [P, NE]), sb("t_end", [P, NE])
        ni = sb("t_ni", [P, NE], I32)
        last = sb("t_last", [P, 1])
        j, jr, e, start, ind = (sb(f"t_{x}", [P, NT]) for x in ("j", "jr", "e", "start", "ind"))
        src, move = sb("t_src", [P, NT]), sb("t_move", [P, NE])
        where, moved, past = (sb(f"t_{x}", [P, NB * TOPK * TT]) for x in ("where", "moved", "past"))
        zeros = sb("t_zeros", [P, D])
        dve, tab_ready, j_ready, zeroed = sem("t_dve"), sem("t_tab_ready"), sem("t_j_ready"), sem("t_zeroed")

        with nc.Block() as block:
            @block.gpsimd
            def _(pool):
                pool.iota(j[:], [[1, NT]], base=0, channel_multiplier=0, allow_small_or_imprecise_dtypes=True).then_inc(j_ready, 1)
                pool.memset(zeros[:], 0.0).then_inc(j_ready, 1)

            @block.vector
            def _(v):
                k = Tally(v, dve)
                link = k.link
                link(v.tensor_copy(tail_i[:], run[:]))
                link(v.tensor_tensor(n[:], run[:], base[:], ALU.subtract))
                link(v.tensor_scalar(ni[:], n[:], float(P - 1), None, ALU.add))
                link(v.tensor_scalar(ni[:], ni[:], 7, None, ALU.arith_shift_right))
                link(v.tensor_copy(cnt[:], ni[:]))
                link(v.tensor_copy(end[:, 0:1], cnt[:, 0:1]))
                for x in range(1, NE):
                    link(v.tensor_tensor(end[:, x:x + 1], end[:, x - 1:x], cnt[:, x:x + 1], ALU.add))
                link(v.tensor_scalar(last[:], end[:, NE - 1:NE], -1.0, None, ALU.add))
                v.wait_ge(j_ready, 1)
                link(v.tensor_scalar(jr[:], j[:], last[:], None, ALU.min))
                link(v.memset(e[:], 0.0))
                link(v.memset(start[:], 0.0))
                for x in range(NE - 1):
                    link(v.tensor_scalar(ind[:], jr[:], end[:, x:x + 1], None, ALU.is_ge))
                    link(v.tensor_tensor(e[:], e[:], ind[:], ALU.add))
                    link(v.scalar_tensor_tensor(out=start[:], in0=ind[:], scalar=cnt[:, x:x + 1], in1=start[:], op0=ALU.mult, op1=ALU.add))
                link(v.tensor_tensor(start[:], jr[:], start[:], ALU.subtract))
                link(v.tensor_scalar(start[:], start[:], float(P), None, ALU.mult))
                link(v.scalar_tensor_tensor(out=src[:], in0=e[:], scalar=float(STRIDE), in1=start[:], op0=ALU.mult, op1=ALU.add))
                link(v.tensor_copy(exp_i[:], e[:]))
                link(v.tensor_copy(src_i[:], src[:]))
                link(v.tensor_scalar(move[:], cnt[:], float(P), -float(STRIDE), ALU.mult, ALU.add))
                link(v.tensor_copy(where[:], pos[:].rearrange("p b k t -> p (b k t)")))
                link(v.tensor_copy(moved[:], where[:]))
                for x in range(NE - 1):
                    link(v.tensor_scalar(past[:], where[:], float((x + 1) * STRIDE), None, ALU.is_ge))
                    link(v.scalar_tensor_tensor(out=moved[:], in0=past[:], scalar=move[:, x:x + 1], in1=moved[:], op0=ALU.mult, op1=ALU.add))
                v.tensor_copy(pos[:].rearrange("p b k t -> p (b k t)"), moved[:]).then_inc(tab_ready, 1)

            @block.sync
            def _(sp):
                sp.wait_ge(tab_ready, 1)
                sp.wait_ge(j_ready, 2)
                for x in range(NE):
                    r = sp.value_load(tail_i[0:1, x:x + 1], min_val=x * STRIDE, max_val=x * STRIDE + TOK)
                    sp.dma_start(xs_d[bass.ds(r, P), :], zeros[:]).then_inc(zeroed, 16)
                sp.wait_ge(zeroed, 16 * NE)


def experts(nc, sem, io, ident, xs_d, ys_d, exp_i, src_i):
    RING = 4
    with ExitStack() as ctx:
        def sb(name, shape, dt=F32):
            return ctx.enter_context(nc.sbuf_tensor(name, shape, dt))

        w1, w2 = sb("e_w1", [P, NE, KC, FF]), sb("e_w2", [P, NE, FC, D])
        b1, b2 = sb("e_b1", [P, NE, FF]), sb("e_b2", [P, NE, D])
        x, xT = sb("e_x", [P, RING, D]), sb("e_xT", [P, 2, D])
        h, hT, y = sb("e_h", [P, 2, FF]), sb("e_hT", [P, 2, FF]), sb("e_y", [P, RING, D])
        X = ctx.enter_context(nc.psum_tensor("ps_ex", [P, 2, 512], F32))
        H = ctx.enter_context(nc.psum_tensor("ps_eh", [P, 2, 512], F32))
        HT = ctx.enter_context(nc.psum_tensor("ps_et", [P, 2, 512], F32))
        Y = ctx.enter_context(nc.psum_tensor("ps_ey", [P, 2, 512], F32))
        w_in = sem("e_w_in")
        x_in = [sem(f"e_x_in{q}") for q in range(RING)]
        xt_done, xT_ready, h_done, h_ready, ht_done, hT_ready, y_done, y_ready = (
            sem(f"e_{n}") for n in ("xt_done", "xT_ready", "h_done", "h_ready", "ht_done", "hT_ready", "y_done", "y_ready"))
        stored = [sem(f"e_stored{q}") for q in range(RING)]

        def wait(eng, s, value):
            if not isinstance(value, int) or value > 0:
                eng.wait_ge(s, value)

        def loop(eng, tile):
            for n in range(RING):
                tile(n, n)
            with eng.Fori(1, NT // RING - 1) as k:
                for n in range(RING):
                    tile(k * RING + n, n)
            for n in range(RING):
                tile(NT - RING + n, n)

        def more(j, ahead):
            return not (isinstance(j, int) and j + ahead >= NT)

        def at(table, j):
            return table[0:1, bass.ds(j, 1)]

        with nc.Block() as block:
            @block.sync
            def _(sp):
                def load(j, n):
                    row = sp.value_load(at(src_i, j), min_val=0, max_val=SLOTS - P)
                    sp.dma_start(x[:, n, :], xs_d[bass.ds(row, P), :]).then_inc(x_in[n], 16)
                for n in range(RING):
                    load(n, n)
                sp.dma_start(w1[:], io["W1"].rearrange("e (c p) f -> p e c f", p=P)).then_inc(w_in, 16)
                sp.dma_start(b1[:], io["b1"].unsqueeze(0).to_broadcast([P, NE, FF])).then_inc(w_in, 16)
                sp.dma_start(w2[:], io["W2"].rearrange("e (c p) f -> p e c f", p=P)).then_inc(w_in, 16)
                sp.dma_start(b2[:], io["b2"].unsqueeze(0).to_broadcast([P, NE, D])).then_inc(w_in, 16)

                def tile(j, n):
                    if more(j, RING):
                        sp.wait_ge(xt_done, j + 1)
                        load(j + RING, n)

                loop(sp, tile)

            @block.tensor
            def _(pe):
                def turn_x(j, n):
                    q = n % 2
                    pe.wait_ge(x_in[n], (j >> 2) * 16 + 16)
                    wait(pe, xT_ready, j - 1)
                    for c in range(KC):
                        last = pe.transpose(X[:, q, P * c:P * c + P], x[:, n, P * c:P * c + P], ident[:])
                    last.then_inc(xt_done, 1)

                def up(j, q, ex):
                    pe.wait_ge(xT_ready, j + 1)
                    wait(pe, h_ready, j - 1)
                    for c in range(KC):
                        last = pe.matmul(H[:, q, :], xT[:, q, P * c:P * c + P], w1[:, bass.ds(ex, 1), c, :], start=(c == 0), stop=(c == KC - 1))
                    last.then_inc(h_done, 1)

                def turn_h(j, q):
                    pe.wait_ge(h_ready, j + 1)
                    wait(pe, hT_ready, j - 1)
                    for c in range(FC):
                        last = pe.transpose(HT[:, q, P * c:P * c + P], h[:, q, P * c:P * c + P], ident[:])
                    last.then_inc(ht_done, 1)

                def down(j, q, ex):
                    pe.wait_ge(hT_ready, j + 1)
                    wait(pe, y_ready, j - 1)
                    for c in range(FC):
                        last = pe.matmul(Y[:, q, 0:D], hT[:, q, P * c:P * c + P], w2[:, bass.ds(ex, 1), c, :], start=(c == 0), stop=(c == FC - 1))
                    last.then_inc(y_done, 1)

                def expert(j):
                    return pe.value_load(at(exp_i, j), min_val=0, max_val=NE - 1)

                def tile(j, n):
                    q = n % 2
                    if more(j, 1):
                        turn_x(j + 1, (n + 1) % RING)
                    up(j, q, expert(j))
                    if not (isinstance(j, int) and j == 0):
                        down(j - 1, 1 - q, expert(j - 1))
                    turn_h(j, q)

                turn_x(0, 0)
                pe.wait_ge(w_in, 64)
                loop(pe, tile)
                down(NT - 1, 1, expert(NT - 1))

            @block.scalar
            def _(act):
                def copy_x(j, q):
                    act.wait_ge(xt_done, j + 1)
                    wait(act, h_done, j - 1)
                    act.activation(xT[:, q, :], X[:, q, 0:D], ACT.Copy).then_inc(xT_ready, 1)

                def relu_h(j, q):
                    act.wait_ge(ht_done, j + 1)
                    wait(act, y_done, j - 1)
                    act.activation(hT[:, q, :], HT[:, q, :], ACT.Relu).then_inc(hT_ready, 1)

                def store(j, n):
                    act.wait_ge(y_ready, j + 1)
                    act.dma_start(ys_d[j], y[:, n, :]).then_inc(stored[n], 16)

                def tile(j, n):
                    q = n % 2
                    if more(j, 1):
                        copy_x(j + 1, 1 - q)
                    relu_h(j, q)
                    if not (isinstance(j, int) and j < 2):
                        store(j - 2, (n - 2) % RING)

                copy_x(0, 0)
                loop(act, tile)
                for n in (2, 3):
                    store(NT - RING + n, n)
                for n in range(RING):
                    act.wait_ge(stored[n], NT // RING * 16)

            @block.vector
            def _(v):
                def bias_h(j, q):
                    ex = v.value_load(at(exp_i, j), min_val=0, max_val=NE - 1)
                    v.wait_ge(h_done, j + 1)
                    wait(v, ht_done, j - 1)
                    v.tensor_tensor(h[:, q, :], H[:, q, :], b1[:, bass.ds(ex, 1), :].rearrange("p o f -> p (o f)"), ALU.add).then_inc(h_ready, 1)

                def bias_y(j, n):
                    q = n % 2
                    ex = v.value_load(at(exp_i, j), min_val=0, max_val=NE - 1)
                    v.wait_ge(y_done, j + 1)
                    wait(v, stored[n], (j >> 2) * 16)
                    v.tensor_tensor(y[:, n, :], Y[:, q, 0:D], b2[:, bass.ds(ex, 1), :].rearrange("p o f -> p (o f)"), ALU.add).then_inc(y_ready, 1)

                def tile(j, n):
                    bias_h(j, n % 2)
                    if not (isinstance(j, int) and j == 0):
                        bias_y(j - 1, (n - 1) % RING)

                v.wait_ge(w_in, 64)
                loop(v, tile)
                bias_y(NT - 1, RING - 1)


def combine(nc, sem, ys_d, h1, pos, gate, out):
    with ExitStack() as ctx:
        def sb(name, shape, dt=F32):
            return ctx.enter_context(nc.sbuf_tensor(name, shape, dt))

        idx = sb("c_idx", [P, 2, TOPK, TT], U32)
        gt = sb("c_gt", [P, 2, TOPK, TT])
        yg = sb("c_yg", [P, 2, TOPK, TT, D])
        part, res = sb("c_part", [P, TT, D]), sb("c_res", [P, 2, TT, D])
        idx_ready, gt_ready, part_ready, res_ready = (sem(f"c_{n}") for n in ("idx_ready", "gt_ready", "part_ready", "res_ready"))
        gathered = [sem(f"c_gathered{q}") for q in range(2)]
        stored = [sem(f"c_stored{q}") for q in range(2)]

        with nc.Block() as block:
            @block.vector
            def _(v):
                def indices(b, q):
                    v.tensor_copy(gt[:, q], gate[:, b, :, :]).then_inc(gt_ready, 1)
                    v.tensor_copy(idx[:, q], pos[:, b, :, :]).then_inc(idx_ready, 1)

                def total(b, k, q):
                    v.wait_ge(gathered[q], k * (TT * TOPK * 16) + TT * TOPK * 16)
                    v.wait_ge(gt_ready, b + 1)
                    for t in range(TT):
                        last = v.scalar_tensor_tensor(out=part[:, t, :], in0=yg[:, q, 0, t, :], scalar=gt[:, q, 0, t:t + 1], in1=h1[:, b, t, :],
                                                      op0=ALU.mult, op1=ALU.add)
                    last.then_inc(part_ready, 1)
                    v.wait_ge(part_ready, b + 1)
                    v.wait_ge(stored[q], k * 16 + 16)
                    for t in range(TT):
                        last = v.scalar_tensor_tensor(out=res[:, q, t, :], in0=yg[:, q, 1, t, :], scalar=gt[:, q, 1, t:t + 1], in1=part[:, t, :],
                                                      op0=ALU.mult, op1=ALU.add)
                    last.then_inc(res_ready, 1)
                    v.wait_ge(res_ready, b + 1)

                indices(0, 0)
                indices(1, 1)
                with v.Fori(0, NB // 2 - 1) as k:
                    for q in range(2):
                        total(k * 2 + q, k, q)
                        indices(k * 2 + q + 2, q)
                for q in range(2):
                    total(NB - 2 + q, NB // 2 - 1, q)

            @block.gpsimd
            def _(pool):
                with pool.Fori(0, NB // 2) as k:
                    for q in range(2):
                        hold(pool, idx_ready, k * 2 + q + 1)
                        for t in range(TT):
                            for e in range(TOPK):
                                pool.indirect_dma_start(out=yg[:, q, e, t, :], out_offset=None, in_=ys_d.rearrange("t p d -> (t p) d"),
                                                        in_offset=bass.IndirectOffsetOnAxis(ap=idx[:, q, e, t:t + 1], axis=0)).then_inc(gathered[q], 16)

            @block.sync
            def _(sp):
                for q in range(2):
                    sp.nop().then_inc(stored[q], 16)
                with sp.Fori(0, NB // 2) as k:
                    for q in range(2):
                        sp.wait_ge(res_ready, k * 2 + q + 1)
                        sp.dma_start(out[k * 2 + q].rearrange("(t p) d -> p t d", p=P), res[:, q]).then_inc(stored[q], 16)
                for q in range(2):
                    sp.wait_ge(stored[q], NB // 2 * 16 + 16)


def program(nc, x, txt, log_dt, inv_A_real, A_imag, B_ri, Wq, Wk, Wv, Wo, Wr, br, W1, b1, W2, b2, cos, sin, out):
    io = dict(x=x, txt=txt, log_dt=log_dt, inv_A_real=inv_A_real, A_imag=A_imag, B_ri=B_ri, Wo=Wo, Wr=Wr, br=br,
              W1=W1, b1=b1, W2=W2, b2=b2, cos=cos, sin=sin, Wq=Wq, Wk=Wk, Wv=Wv)
    img_d = nc.dram_tensor("img_d", (NB, IMG, D), F32, kind="Internal").ap()
    xnT_d = nc.dram_tensor("xnT_d", (NB, P, KC, SEQ), F32, kind="Internal").ap()
    oT_d = nc.dram_tensor("oT_d", (NIT, P, 2, SEQ), F32, kind="Internal").ap()
    xs_d = nc.dram_tensor("xs_d", (SLOTS, D), F32, kind="Internal").ap()
    ys_d = nc.dram_tensor("ys_d", (NT, P, D), F32, kind="Internal").ap()
    with ExitStack() as ctx:
        def sb(name, shape, dt=F32):
            return ctx.enter_context(nc.sbuf_tensor(name, shape, dt))

        def sem(name):
            return ctx.enter_context(nc.semaphore(name))

        ident = sb("ident", [P, P])
        vandermonde(nc, sem, io, ident, img_d)
        norm_in(nc, sem, io, ident, img_d, xnT_d)
        attention(nc, sem, io, ident, xnT_d, oT_d)
        h1 = sb("h1", [P, NB, TT, D])
        pos = sb("pos", [P, NB, TOPK, TT], U32)
        gate = sb("gate", [P, NB, TOPK, TT])
        run, base = sb("run", [P, NE]), sb("base", [P, NE])
        route(nc, sem, io, ident, img_d, oT_d, xs_d, h1, pos, gate, run, base)
        exp_i, src_i = sb("exp_i", [P, NT], I32), sb("src_i", [P, NT], I32)
        tail_i = sb("tail_i", [P, NE], I32)
        tiles(nc, sem, xs_d, run, base, pos, exp_i, src_i, tail_i)
        experts(nc, sem, io, ident, xs_d, ys_d, exp_i, src_i)
        combine(nc, sem, ys_d, h1, pos, gate, out)


def rotary_tables():
    f = np.float32
    inv_freq = (f(1.0) / f(10000.0) ** (np.arange(0, DH, 2, dtype=f) / f(DH))).astype(f)
    angle = np.arange(SEQ, dtype=f)[:, None] * inv_freq[None, :]
    scale = np.array([DH ** -0.5] * GH + [1.0], f)

    def table(half_a, half_b):
        t = scale[None, :, None] * np.concatenate([half_a, half_b], 1)[:, None, :]
        return np.ascontiguousarray(t.reshape(TT, P, QK).transpose(1, 0, 2).astype(f))

    return table(np.cos(angle), np.cos(angle)), table(-np.sin(angle), np.sin(angle))


_INS = ["x", "txt", "L0_tok_log_dt", "L0_tok_inv_A_real", "L0_tok_A_imag", "L0_tok_B_ri",
        "L0_attn_Wq", "L0_attn_Wk", "L0_attn_Wv", "L0_attn_Wo",
        "L0_ffn_Wr", "L0_ffn_br", "L0_ffn_W1", "L0_ffn_b1", "L0_ffn_W2", "L0_ffn_b2"]


def kernel(**inputs):
    import numpy as _np
    import concourse.bacc as _bacc
    from concourse import mybir as _mybir
    from concourse.bass_utils import run_bass_kernel_spmd as _run

    nc = _bacc.Bacc("TRN2", target_bir_lowering=False, num_devices=1)
    cos, sin = rotary_tables()
    arrays, args = {}, []
    for name, a in [(n, inputs[n]) for n in _INS] + [("cos", cos), ("sin", sin)]:
        a = _np.ascontiguousarray(a)
        arrays[f"in_{name}_dram"] = a
        args.append(nc.dram_tensor(f"in_{name}_dram", a.shape, _mybir.dt.from_np(a.dtype), kind="ExternalInput").ap())
    args.append(nc.dram_tensor("out_0_dram", (NB, SEQ, D), F32, kind="ExternalOutput").ap())
    program(nc, *args)
    r = _run(nc, [arrays], core_ids=[0])
    return r.results[0]["out_0_dram"]
```

```python
import math
from contextlib import ExitStack

import numpy as np

import concourse.bass as bass
from concourse import mybir

P = 128
NB, SEQ, D = 8, 768, 256
IMG, TXT = 256, 512
NS = 64
HEADS, KV, DH = 16, 4, 64
GH = HEADS // KV
TT = SEQ // P
IT = IMG // P
KC = D // P
TOK = NB * SEQ
NE, FF, TOPK = 8, 512, 2
FC = FF // P
EPS = 1e-5
NIT = NB * KV
STRIDE = TOK + P
SLOTS = NE * STRIDE
NT = TOK * TOPK // P + NE

F32 = mybir.dt.float32
F32R = mybir.dt.float32r
I32 = mybir.dt.int32
U32 = mybir.dt.uint32
ALU = mybir.AluOpType
ACT = mybir.ActivationFunctionType
AX = mybir.AxisListType


def hold(eng, sem, value):
    eng.wait_ge(sem, value)
    eng.nop(nofuse=True)


class Tally:

    def __init__(self, eng, sem, base=0):
        self.eng, self.sem, self.base, self.n = eng, sem, base, 0

    def mark(self, ins):
        self.n += 1
        ins.then_inc(self.sem, 1)
        return self.n

    def link(self, ins):
        self.eng.wait_ge(self.sem, self.base + self.mark(ins))


def vandermonde(nc, sem, io, ident, img_d):
    AN, BN = 4, 64
    GM = NB * AN
    HH = IMG // P
    SL = 16
    LOG2E, MAGIC = 1.4426950408889634, 12582912.0
    LN2HI, LN2LO = 0.693359375, -2.12194440e-4
    with ExitStack() as ctx:
        def sb(name, shape, dt=F32):
            return ctx.enter_context(nc.sbuf_tensor(name, shape, dt))

        logdt, dt = sb("logdt", [P, HH]), sb("dt", [P, HH])
        inva, aim = sb("inva", [P, HH, NS]), sb("aim", [P, HH, NS])
        bri = sb("bri", [P, HH, NS, 2])
        cnat = sb("cnat", [P, NB, HH, NS, 2])
        ex = [sb(f"ex{n}", [P, HH]) for n in range(6)]
        exi = sb("exi", [P, HH], I32)
        nat = [sb(f"nat{n}", [P, HH * NS]) for n in range(8)]
        zre, zim = sb("zre", [P, P]), sb("zim", [P, P])
        b2 = sb("b2", [P, HH, NS, 2])
        wre, wim = sb("wre", [P, BN + 1, P]), sb("wim", [P, BN + 1, P])
        ct = sb("ct", [P, NB, 2, P])
        b2t = sb("b2t", [P, 2, P])
        bare, baim = sb("bare", [P, AN, P]), sb("baim", [P, AN, P])
        ure, uim = sb("ure", [P, AN, P]), sb("uim", [P, AN, P])
        gre, gim = sb("gre", [P, NB, AN, P]), sb("gim", [P, NB, AN, P])
        tm = [sb(f"tm{n}", [P, SL, P]) for n in range(4)]
        kt = sb("kt", [P, HH * 32, BN])
        ps = ctx.enter_context(nc.psum_tensor("ps_v", [P, 8, 512], F32))

        loaded_a, loaded_c = sem("v_loaded_a"), sem("v_loaded_c")
        exp_done, dve = sem("v_exp_done"), sem("v_dve")
        nat_ready, tr_z, tr_c = sem("v_nat_ready"), sem("v_tr_z"), sem("v_tr_c")
        ct_ready, g_ready, bank_full, bank_out = sem("v_ct_ready"), sem("v_g_ready"), sem("v_bank_full"), sem("v_bank_out")
        stored = sem("v_stored")
        id_ready = sem("v_id_ready")

        with nc.Block() as block:
            @block.sync
            def _(sp):
                sp.dma_start(logdt[:], io["log_dt"].rearrange("(a p) -> p a", p=P), allow_slow_non_contiguous=True).then_inc(loaded_a, 16)
                sp.dma_start(inva[:], io["inv_A_real"].rearrange("(a p) n -> p a n", p=P)).then_inc(loaded_a, 16)
                sp.dma_start(aim[:], io["A_imag"].rearrange("(a p) n -> p a n", p=P)).then_inc(loaded_a, 16)
                sp.dma_start(bri[:], io["B_ri"].rearrange("(a p) n r -> p a n r", p=P)).then_inc(loaded_a, 16)
                for c in range(NB):
                    sp.dma_start(cnat[:, c], io["x"][c].rearrange("(a p) n r -> p a n r", p=P)).then_inc(loaded_c, 16)
                out = img_d.rearrange("c (q j) (a b) -> j c a q b", j=4, a=AN)
                for hh in range(HH):
                    sp.wait_ge(bank_out, 4 * (hh + 1))
                    for j in range(4):
                        for c in range(NB):
                            sp.dma_start(out[j, c][:, hh * 32:hh * 32 + 32, :],
                                         kt[32 * j + AN * c:32 * j + AN * (c + 1), hh * 32:hh * 32 + 32, :]).then_inc(stored, 16)
                sp.wait_ge(stored, 16 * HH * 4 * NB)

            @block.gpsimd
            def _(pool):
                pool.memset(ident[:], 0.0).then_inc(id_ready, 1)
                pool.wait_ge(id_ready, 1)
                pool.affine_select(out=ident[:], in_=ident[:], compare_op=ALU.not_equal, fill=1.0, base=0,
                                   pattern=[[-1, P]], channel_multiplier=1).then_inc(id_ready, 1)

            @block.scalar
            def _(act):
                act.wait_ge(loaded_a, 64)
                act.activation(nat[0][:], inva[:].rearrange("p a n -> p (a n)"), ACT.Exp).then_inc(exp_done, 1)
                for q in range(4):
                    act.wait_ge(tr_c, q + 1)
                    act.activation(ct[:].rearrange("p c r h -> p (c r h)")[:, 512 * q:512 * q + 512], ps[:, 1 + q], ACT.Copy).then_inc(ct_ready, 1)
                for q in range(8):
                    act.wait_ge(bank_full, q + 1)
                    act.activation(kt[:, 8 * q:8 * q + 8, :], ps[:, q].rearrange("p (q b) -> p q b", b=BN), ACT.Copy).then_inc(bank_out, 1)

            @block.tensor
            def _(pe):
                pe.wait_ge(id_ready, 2)
                pe.wait_ge(loaded_c, 16 * NB)
                for q in range(4):
                    for k in range(4):
                        c, r = (4 * q + k) // 2, k % 2
                        last = pe.transpose(ps[:, 1 + q, P * k:P * k + P], cnat[:, c].rearrange("p a n r -> p (a n) r")[:, :, r], ident[:])
                    last.then_inc(tr_c, 1)
                pe.wait_ge(nat_ready, 1)
                b2v = b2[:].rearrange("p a n r -> p (a n) r")
                for k, src in enumerate((zre[:], zim[:], b2v[:, :, 0], b2v[:, :, 1])):
                    last = pe.transpose(ps[:, 0, P * k:P * k + P], src, ident[:])
                last.then_inc(tr_z, 1)
                pe.wait_ge(g_ready, NB)
                for q in range(8):
                    if q in (1, 2, 3, 4):
                        pe.wait_ge(ct_ready, q)
                    lo = NS * (q // 4)
                    for k in range(8):
                        for j in range(4):
                            h = 4 * (8 * (q % 4) + k) + j
                            for n, (g, w) in enumerate(((gre, wre), (gim, wim))):
                                last = pe.matmul(ps[GM * j:GM * j + GM, q, BN * k:BN * k + BN],
                                                 g[:].rearrange("p c a h -> p (c a) h")[lo:lo + NS, :, h],
                                                 w[lo:lo + NS, 0:BN, h], start=(n == 0), stop=(n == 1))
                    last.then_inc(bank_full, 1)

            @block.vector
            def _(v):
                t = Tally(v, dve)
                link, mark = t.link, t.mark
                v.wait_ge(loaded_a, 64)
                x, tk, kf, r, p, s = (e[:] for e in ex)
                link(v.tensor_scalar(x, logdt[:], 88.0, -87.0, ALU.min, ALU.max))
                link(v.tensor_scalar(tk, x, LOG2E, MAGIC, ALU.mult, ALU.add))
                link(v.tensor_scalar(kf, tk, MAGIC, None, ALU.subtract))
                link(v.scalar_tensor_tensor(out=r, in0=kf, scalar=-LN2HI, in1=x, op0=ALU.mult, op1=ALU.add))
                link(v.scalar_tensor_tensor(out=s, in0=kf, scalar=-LN2LO, in1=r, op0=ALU.mult, op1=ALU.add))
                link(v.tensor_scalar(p, s, 1 / math.factorial(7), None, ALU.mult))
                for n in range(6, 0, -1):
                    link(v.scalar_tensor_tensor(out=p, in0=p, scalar=1 / math.factorial(n), in1=s, op0=ALU.add, op1=ALU.mult))
                link(v.tensor_scalar(exi[:], kf, 127.0, None, ALU.add))
                link(v.tensor_scalar(exi[:], exi[:], 23, None, ALU.logical_shift_left))
                link(v.scalar_tensor_tensor(out=dt[:], in0=p, scalar=1.0, in1=exi[:].bitcast(F32), op0=ALU.add, op1=ALU.mult))
                e, a, w, d1, w2, num, rden, a2 = (n_[:] for n_ in nat)
                v.wait_ge(exp_done, 1)
                for hh in range(HH):
                    cols = slice(hh * NS, hh * NS + NS)
                    v.tensor_scalar(a[:, cols], e[:, cols], dt[:, hh:hh + 1], -0.5, ALU.mult, ALU.mult)
                    link(v.tensor_scalar(w[:, cols], aim[:, hh, :], dt[:, hh:hh + 1], 0.5, ALU.mult, ALU.mult))
                link(v.tensor_scalar(d1, a, -1.0, 1.0, ALU.mult, ALU.add))
                link(v.tensor_tensor(d1, d1, d1, ALU.mult))
                link(v.tensor_tensor(w2, w, w, ALU.mult))
                link(v.tensor_tensor(d1, d1, w2, ALU.add))
                link(v.reciprocal(rden, d1))
                link(v.tensor_tensor(a2, a, a, ALU.mult))
                link(v.tensor_tensor(a2, a2, w2, ALU.add))
                link(v.tensor_scalar(num, a2, -1.0, 1.0, ALU.mult, ALU.add))
                mark(v.tensor_tensor(zre[:], num, rden, ALU.mult))
                mark(v.scalar_tensor_tensor(out=zim[:], in0=w, scalar=2.0, in1=rden, op0=ALU.mult, op1=ALU.mult))
                v.tensor_scalar(b2[:], bri[:], 2.0, None, ALU.mult).then_inc(nat_ready, 1)
                mark(v.memset(wre[:, 0, :], 1.0))
                mark(v.memset(wim[:, 0, :], 0.0))
                mark(v.memset(ure[:, 0, :], 1.0))
                mark(v.memset(uim[:, 0, :], 0.0))
                v.wait_ge(tr_z, 1)
                mark(v.tensor_copy(wre[:, 1, :], ps[:, 0, 0:P]))
                mark(v.tensor_copy(wim[:, 1, :], ps[:, 0, P:2 * P]))
                link(v.tensor_copy(b2t[:], ps[:, 0, 2 * P:4 * P].rearrange("p (r h) -> p r h", r=2)))

                def cmul(ore, oim, ar, ai, br, bi):
                    n = ore.shape[1]
                    t1, t2, t3, t4 = (tm[k][:, 0:n] for k in range(4))
                    mark(v.tensor_tensor(t1, ar, br, ALU.mult))
                    mark(v.tensor_tensor(t2, ai, bi, ALU.mult))
                    mark(v.tensor_tensor(t3, ar, bi, ALU.mult))
                    link(v.tensor_tensor(t4, ai, br, ALU.mult))
                    mark(v.tensor_tensor(ore, t1, t2, ALU.subtract))
                    link(v.tensor_tensor(oim, t3, t4, ALU.add))

                def over(ap, n):
                    return ap.unsqueeze(1).to_broadcast([P, n, P])

                k = 1
                while k < BN:
                    for j in range(0, k, SL):
                        n = min(SL, k - j)
                        cmul(wre[:, k + 1 + j:k + 1 + j + n], wim[:, k + 1 + j:k + 1 + j + n],
                             wre[:, 1 + j:1 + j + n], wim[:, 1 + j:1 + j + n], over(wre[:, k], n), over(wim[:, k], n))
                    k *= 2
                mark(v.tensor_copy(ure[:, 1, :], wre[:, BN, :]))
                link(v.tensor_copy(uim[:, 1, :], wim[:, BN, :]))
                for j in range(2, AN):
                    cmul(ure[:, j:j + 1], uim[:, j:j + 1], ure[:, j - 1:j], uim[:, j - 1:j], ure[:, 1:2], uim[:, 1:2])
                cmul(bare[:], baim[:], ure[:], uim[:], over(b2t[:, 0], AN), over(b2t[:, 1], AN))
                v.wait_ge(ct_ready, 4)
                t1, t2, t3, t4 = (tm[k][:, 0:AN] for k in range(4))
                for c in range(NB):
                    cr, ci = over(ct[:, c, 0], AN), over(ct[:, c, 1], AN)
                    mark(v.tensor_tensor(t1, bare[:], cr, ALU.mult))
                    mark(v.tensor_tensor(t2, baim[:], ci, ALU.mult))
                    mark(v.tensor_tensor(t3, bare[:], ci, ALU.mult))
                    link(v.scalar_tensor_tensor(out=t4, in0=baim[:], scalar=-1.0, in1=cr, op0=ALU.mult, op1=ALU.mult))
                    mark(v.tensor_tensor(gre[:, c], t1, t2, ALU.subtract))
                    v.tensor_tensor(gim[:, c], t4, t3, ALU.subtract).then_inc(g_ready, 1)
                    v.wait_ge(g_ready, c + 1)


def norm_in(nc, sem, io, ident, img_d, xnT_d):
    with ExitStack() as ctx:
        def sb(name, shape, dt=F32):
            return ctx.enter_context(nc.sbuf_tensor(name, shape, dt))

        x = sb("n_x", [P, 2, TT, D])
        st = sb("n_st", [P, TT, 6])
        mv = sb("n_mv", [P, TT, 2])
        ve, sd, y, y2 = (sb(f"n_s{n}", [P, TT]) for n in range(4))
        rstd = sb("n_rstd", [P, TT])
        xn = sb("n_xn", [P, 2, TT, D])
        xt = sb("n_xt", [P, 2, KC, SEQ])
        ps = ctx.enter_context(nc.psum_tensor("ps_n", [P, 2, 3, 512], F32))
        x_in = [sem(f"n_x_in{q}") for q in range(2)]
        xn_free, ps_free = sem("n_xn_free"), sem("n_ps_free")
        dve, var_ready, sd_ready, xn_ready = sem("n_dve"), sem("n_var_ready"), sem("n_sd_ready"), sem("n_xn_ready")
        tr_done, xt_ready = sem("n_tr_done"), sem("n_xt_ready")
        stored = [sem(f"n_stored{q}") for q in range(2)]
        LINKS = 2 * TT + 5

        with nc.Block() as block:
            @block.sync
            def _(sp):
                def load(b, q):
                    sp.dma_start(x[:, q, 0:IT, :], img_d[b].rearrange("(t p) d -> p t d", p=P)).then_inc(x_in[q], 16)
                    sp.dma_start(x[:, q, IT:TT, :], io["txt"][b].rearrange("(t p) d -> p t d", p=P)).then_inc(x_in[q], 16)

                for q in range(2):
                    sp.nop().then_inc(stored[q], 16)
                    load(q, q)
                with sp.Fori(1, NB // 2) as k:
                    for q in range(2):
                        sp.wait_ge(xn_ready, k * 2 + q - 1)
                        load(k * 2 + q, q)

            @block.vector
            def _(v):
                with v.Fori(0, NB // 2) as k:
                    for q in range(2):
                        b = k * 2 + q
                        t = Tally(v, dve, b * LINKS)
                        link, mark = t.link, t.mark
                        hold(v, x_in[q], k * 32 + 32)
                        for i in range(TT):
                            mark(v.bn_stats(st[:, i, :], x[:, q, i, :]))
                        hold(v, dve, t.base + t.n)
                        for i in range(TT):
                            mark(v.bn_aggr(mv[:, i, :], st[:, i, :]))
                        v.wait_ge(dve, t.base + t.n)
                        v.tensor_scalar(ve[:], mv[:, :, 1], EPS, None, ALU.add).then_inc(var_ready, 1)
                        v.wait_ge(sd_ready, b + 1)
                        link(v.reciprocal(y[:], sd[:]))
                        link(v.tensor_tensor(y2[:], y[:], y[:], ALU.mult))
                        link(v.tensor_tensor(y2[:], y2[:], ve[:], ALU.mult))
                        link(v.tensor_scalar(y2[:], y2[:], -0.5, 1.5, ALU.mult, ALU.add))
                        link(v.tensor_tensor(rstd[:], y[:], y2[:], ALU.mult))
                        assert t.n == LINKS
                        v.wait_ge(xn_free, b + 1)
                        for i in range(TT):
                            last = v.tensor_scalar(xn[:, q, i, :], x[:, q, i, :], mv[:, i, 0:1], rstd[:, i:i + 1], ALU.subtract, ALU.mult)
                        last.then_inc(xn_ready, 1)

            @block.tensor
            def _(pe):
                pe.nop().then_inc(xn_free, 2)
                with pe.Fori(0, NB // 2) as k:
                    for q in range(2):
                        pe.wait_ge(xn_ready, k * 2 + q + 1)
                        pe.wait_ge(ps_free, k * 2 + q + 1)
                        for n in range(3):
                            for m in range(4):
                                c, i = (4 * n + m) // TT, (4 * n + m) % TT
                                last = pe.transpose(ps[:, q, n, P * m:P * m + P], xn[:, q, i, P * c:P * c + P], ident[:])
                            if n < 2:
                                last.then_inc(tr_done, 1)
                        last.then_inc(xn_free, 1)

            @block.scalar
            def _(act):
                act.nop().then_inc(ps_free, 2)
                with act.Fori(0, NB // 2) as k:
                    for q in range(2):
                        b = k * 2 + q
                        act.wait_ge(var_ready, b + 1)
                        act.activation(sd[:], ve[:], ACT.Sqrt).then_inc(sd_ready, 1)
                        act.wait_ge(stored[q], k * 16 + 16)
                        for n in range(3):
                            if n < 2:
                                act.wait_ge(tr_done, b * 2 + n + 1)
                            else:
                                act.wait_ge(xn_free, b + 3)
                            out = act.activation(xt[:, q].rearrange("p c s -> p (c s)")[:, 512 * n:512 * n + 512], ps[:, q, n], ACT.Copy)
                            if n < 2:
                                out.then_inc(xt_ready, 1)
                        out.then_inc(ps_free, 1)
                        act.wait_ge(ps_free, b + 3)
                        act.dma_start(xnT_d[b], xt[:, q]).then_inc(stored[q], 16)
                for q in range(2):
                    act.wait_ge(stored[q], 16 * (NB // 2) + 16)


def attention(nc, sem, io, ident, xnT_d, oT_d):
    LAG = 3
    STEPS = GH * TT
    HALF = SEQ // 2
    CT = HALF // P
    GRP = 2 * CT
    NG = STEPS // GRP
    RING = 4
    HL = 2 * DH
    HH = DH // 2
    TURN = [(0, 0), (0, 1), (1, 0), (1, 1)]
    Q_USES = [(1 + 2 * n, "q", c, h) for n, (c, h) in enumerate(TURN)]
    K_USES = [(9 + 2 * n, "k", c, h) for n, (c, h) in enumerate(TURN)]
    V_USES = [(9 + 2 * n, "v", n, 0) for n in range(TT // 2)]
    USES = [Q_USES, Q_USES, Q_USES + K_USES, Q_USES + V_USES]
    FIRST = V_USES + K_USES + Q_USES
    PER_BATCH = sum(len(u) for u in USES)
    ROT_AT = {("q", 0): 4, ("q", 1): 9, ("k", 0): 14, ("k", 1): 19}
    PAIRS = [("q", 0), ("q", 1)]
    ROTS = [PAIRS, PAIRS, PAIRS + [("k", 0), ("k", 1)], PAIRS]
    FIRST_ROTS = [("k", 0), ("k", 1)] + PAIRS
    ROTS_BATCH = sum(len(u) for u in ROTS)
    LINKS = 10
    VCOPY_AT = 22
    Q_MOVES, K_MOVES = 4 * GH, 8
    with ExitStack() as ctx:
        def sb(name, shape, dt=F32):
            return ctx.enter_context(nc.sbuf_tensor(name, shape, dt))

        table = sb("a_table", [P, 2, 2, SEQ])
        wq, wk, wv = sb("a_wq", [P, KC, 2, HEADS * HH]), sb("a_wk", [P, KC, 2, KV * HH]), sb("a_wv", [P, KC, KV * DH])
        xnow, xnext = sb("a_xnow", [P, KC, SEQ]), sb("a_xnext", [P, KC, SEQ])
        raw = sb("a_raw", [P, 2, 2, HALF])
        prod = sb("a_prod", [P, 4, HALF])
        qp, kp = sb("a_qp", [P, 2, 2, SEQ], F32R), sb("a_kp", [P, 2, 2, SEQ], F32R)
        qT = sb("a_qT", [P, 2, GH, SEQ], F32R)
        kT = sb("a_kT", [P, 2, 2, SEQ], F32R)
        vraw, val = sb("a_vraw", [P, TT, KV * DH]), sb("a_val", [P, 2, TT, DH])
        nmax, rsum, inv = sb("a_nmax", [P, RING]), sb("a_rsum", [P, RING]), sb("a_inv", [P, RING])
        prob = sb("a_prob", [P, RING, SEQ])
        probT = sb("a_probT", [P, 2, TT, 2, HALF])
        oT = sb("a_oT", [P, 2, HALF])
        S = ctx.enter_context(nc.psum_tensor("ps_s", [P, 2, 2, 512], F32))
        T = ctx.enter_context(nc.psum_tensor("ps_t", [P, 2, 512], F32))
        O = ctx.enter_context(nc.psum_tensor("ps_o", [P, 512], F32))
        X = ctx.enter_context(nc.psum_tensor("ps_x", [P, 512], F32))

        tables_in, w_in, xnow_in, xnext_in = (sem(f"a_{n}_in") for n in ("tables", "w", "xnow", "xnext"))
        x_done, x_out, dve, v_ready = (sem(f"a_{n}") for n in ("x_done", "x_out", "dve", "v_ready"))
        q_in, k_in = ([sem(f"a_{n}_in{q}") for q in range(2)] for n in "qk")
        scores_ready, max_ready, exp_ready, inv_ready, norm_ready = (sem(f"a_{n}_ready") for n in ("scores", "max", "exp", "inv", "norm"))
        t_done, probT_ready, pv_done, o_out = sem("a_t_done"), sem("a_probT_ready"), sem("a_pv_done"), sem("a_o_out")
        o_stored = [sem(f"a_o_stored{q}") for q in range(2)]

        def wait(eng, s, value):
            if not isinstance(value, int) or value > 0:
                eng.wait_ge(s, value)

        def loop(eng, iteration, drain):
            for g in range(KV):
                iteration(0, g)
            with eng.Fori(1, NB - 1) as b:
                for g in range(KV):
                    iteration(b, g)
            for g in range(KV):
                iteration(NB - 1, g)
            if drain:
                drain()

        def use_no(b, g, n):
            return b * PER_BATCH + (len(FIRST) + sum(len(u) for u in USES[:g]) + n)

        def rot_no(b, g, n):
            return b * ROTS_BATCH + (len(FIRST_ROTS) + sum(len(u) for u in ROTS[:g]) + n)

        def uses(b, g):
            if last_batch(b) and g == KV - 1:
                return []
            rows = USES[g][:len(Q_USES)] if last_batch(b) else USES[g]
            return [(use_no(b, g, n), s, job, c, h, rot_no(b, g, n // 2), n // 2 + sum(len(u) for u in ROTS[:g])) for n, (s, job, c, h) in enumerate(rows)]

        def rots(b, g):
            if last_batch(b) and g == KV - 1:
                return []
            rows = PAIRS if last_batch(b) else ROTS[g]
            return [(rot_no(b, g, n), n + sum(len(u) for u in ROTS[:g]), ROT_AT[job, c], job, c, use_no(b, g, 2 * n + 2)) for n, (job, c) in enumerate(rows)]

        def real(i, n):
            return n >= 0 or not (isinstance(i, int) and i == 0)

        last_batch = lambda b: isinstance(b, int) and b == NB - 1
        last_it = lambda i: isinstance(i, int) and i == NIT - 1

        def where(s):
            s %= STEPS
            return (s // GRP) % 2, (s % GRP) // 2, s % 2, s // GRP // 2

        with nc.Block() as block:
            @block.sync
            def _(sp):
                sp.dma_start(xnext[:], xnT_d[0]).then_inc(xnext_in, 16)
                for c in range(KC):
                    rows = slice(P * c, P * c + P)
                    sp.dma_start(wv[:, c], io["Wv"][rows]).then_inc(w_in, 16)
                    for h in range(2):
                        half = slice(HH * h, HH * h + HH)
                        sp.dma_start(wk[:, c, h].rearrange("p (x d) -> p x d", d=HH), io["Wk"][rows].rearrange("p (x d) -> p x d", d=DH)[:, :, half]).then_inc(w_in, 16)
                        sp.dma_start(wq[:, c, h].rearrange("p (x d) -> p x d", d=HH), io["Wq"][rows].rearrange("p (x d) -> p x d", d=DH)[:, :, half]).then_inc(w_in, 16)
                sp.dma_start(table[:], io["rotary"]).then_inc(tables_in, 16)
                sp.dma_start(xnow[:], xnT_d[0]).then_inc(xnow_in, 16)

                def move_k(par, g):
                    for w in range(2):
                        for x in range(2):
                            for h in range(2):
                                at = DH * (x ^ w) + HH * h
                                sp.dma_start(kT[at:at + HH, par, w, :].bitcast(F32), kp[HH * g:HH * g + HH, x, h, :].bitcast(F32)).then_inc(k_in[par], 16)

                def move_q(par, rot):
                    sp.wait_ge(dve, rot * LINKS + LINKS)
                    for x in range(2):
                        for h in range(2):
                            at = DH * x + HH * h
                            for j in range(GH):
                                sp.dma_start(qT[at:at + HH, par, j, :].bitcast(F32), qp[HH * j:HH * j + HH, x, h, :].bitcast(F32)).then_inc(q_in[par], 16)

                def iteration(b, g):
                    i, par = b * KV + g, g % 2
                    if last_batch(b) and g == KV - 1:
                        return
                    if g == 0 and not last_batch(b):
                        sp.wait_ge(x_done, use_no(b, 0, 0))
                        sp.dma_start(xnext[:], xnT_d[b + 1]).then_inc(xnext_in, 16)
                    wait(sp, scores_ready, i * STEPS)
                    if g == KV - 1:
                        sp.wait_ge(dve, rot_no(b, g, 0) * LINKS)
                    move_k(1 - par, (g + 1) % KV)
                    if g == KV - 1:
                        sp.wait_ge(x_done, use_no(b, KV - 2, len(Q_USES)))
                        sp.dma_start(xnow[:], xnT_d[b + 1]).then_inc(xnow_in, 16)
                    move_q(1 - par, rot_no(b, g, 1))

                sp.wait_ge(dve, 2 * LINKS)
                move_k(0, 0)
                move_q(0, len(FIRST_ROTS) - 1)
                loop(sp, iteration, None)

            @block.tensor
            def _(pe):
                def project(n, job, c, h, xn, g):
                    wait(pe, x_out, n)
                    if job == "v":
                        for t in range(2):
                            tok = slice(P * (2 * c + t), P * (2 * c + t) + P)
                            for k in range(KC):
                                last = pe.matmul(X[:, KV * DH * t:KV * DH * (t + 1)], xn[:, k, tok], wv[:, k, :], start=(k == 0), stop=(k == KC - 1))
                    else:
                        for k in range(KC):
                            w = wq[:, k, h, P * g:P * g + P] if job == "q" else wk[:, k, h, :]
                            last = pe.matmul(X[:, 0:HALF], w, xn[:, k, HALF * c:HALF * c + HALF], start=(k == 0), stop=(k == KC - 1))
                    last.then_inc(x_done, 1)

                def scores(b, g, s):
                    i, par = b * KV + g, g % 2
                    hp, t, j, c = where(s)
                    if s == 0:
                        pe.wait_ge(k_in[par], (b * 2 + (g // 2 + 1)) * (K_MOVES * 16))
                        pe.wait_ge(q_in[par], (b * 2 + (g // 2 + 1)) * (Q_MOVES * 16))
                    wait(pe, exp_ready, i * STEPS + s - 1)
                    for r in range(2):
                        for w in range(2):
                            last = pe.matmul(S[:, s % 2, r, 0:HALF], qT[:, par, 2 * hp + j, HALF * c + P * t:HALF * c + P * t + P],
                                             kT[:, par, w, HALF * r:HALF * r + HALF], start=(w == 0), stop=(w == 1))
                    last.then_inc(scores_ready, 1)

                def turn_probs(i, s):
                    pe.wait_ge(norm_ready, i * STEPS + s + 1)
                    for half in range(2):
                        wait(pe, probT_ready, (i * STEPS + s) * 2 - 1 + half)
                        for n in range(CT):
                            kt = CT * half + n
                            last = pe.transpose(T[:, half, P * n:P * n + P], prob[:, s % RING, P * kt:P * kt + P], ident[:])
                        last.then_inc(t_done, 1)

                def values(i, par, g, kt):
                    if g == 0 and kt == 0:
                        pe.wait_ge(v_ready, i + 1)
                    if kt == 0:
                        pe.wait_ge(probT_ready, (i * NG + g) * 2 * GRP + 2 * GRP)
                        wait(pe, o_out, i * NG + g)
                    for j in range(2):
                        last = pe.matmul(O[DH * j:DH * j + DH, 0:HALF], val[:, (par + (g < 0)) % 2, kt, :], probT[:, g % 2, kt, j, :],
                                         start=(kt == 0), stop=(kt == TT - 1))
                    if kt == TT - 1:
                        last.then_inc(pv_done, 1)

                def back(i, par, s):
                    if real(i, s - LAG) and s - LAG < STEPS:
                        turn_probs(i, s - LAG)
                    g, kt = (s - LAG - GRP) // GRP, (s - LAG - GRP) % GRP
                    if real(i, g):
                        values(i, par, g, kt)

                def iteration(b, g):
                    i, par = b * KV + g, g % 2
                    now = {s: rest for rest in uses(b, g) for s in (rest[1],)}
                    for s in range(STEPS):
                        scores(b, g, s)
                        if s in now:
                            n, _, job, c, h, _, _ = now[s]
                            if (g, s) == (0, Q_USES[0][0]):
                                pe.wait_ge(xnow_in, b * 16 + 16)
                            if (g, s) == (KV - 2, K_USES[0][0]):
                                pe.wait_ge(xnext_in, b * 16 + 32)
                            project(n, job, c, h, xnow if job == "q" and g < KV - 1 else xnext, (g + 1) % KV)
                        back(i, par, s)

                def drain():
                    for s in range(STEPS, STEPS + LAG + GRP):
                        back(NIT - 1, 1, s)

                pe.wait_ge(xnext_in, 16)
                pe.wait_ge(w_in, 16 * 5 * KC)
                for n, (_, job, c, h) in enumerate(FIRST):
                    project(n, job, c, h, xnext, 0)
                loop(pe, iteration, drain)

            @block.scalar
            def _(act):
                def evacuate(n, job, c, h, rot, at, b):
                    act.wait_ge(x_done, n + 1)
                    if job == "v":
                        if c == 0:
                            wait(act, v_ready, b * KV)
                        out = act.activation(vraw[:, 2 * c:2 * c + 2, :], X[:].rearrange("p (t d) -> p t d", t=2), ACT.Copy)
                    else:
                        if h == 0 and not (isinstance(rot, int) and rot < 2):
                            act.wait_ge(dve, (rot - 2) * LINKS + 4)
                        out = act.activation(raw[:, at % 2, h, :], X[:, 0:HALF], ACT.Copy)
                    out.then_inc(x_out, 1)

                def exps(i, s):
                    act.wait_ge(max_ready, i * STEPS + s + 1)
                    wait(act, t_done, (i * STEPS + s - RING + 1) * 2)
                    act.activation(prob[:, s % RING, :].rearrange("p (r k) -> p r k", r=2), S[:, s % 2, :, 0:HALF], ACT.Exp,
                                   bias=nmax[:, s % RING:s % RING + 1], scale=1.0,
                                   accum_out=rsum[:, s % RING:s % RING + 1]).then_inc(exp_ready, 1)

                def copy_probT(i, s):
                    hp, t, j, c = where(s)
                    g = s // GRP
                    if s % GRP == 0:
                        wait(act, pv_done, i * NG + g - 1)
                    for half in range(2):
                        act.wait_ge(t_done, (i * STEPS + s) * 2 + half + 1)
                        act.activation(probT[:, g % 2, CT * half:CT * half + CT, j, P * t:P * t + P],
                                       T[:, half, 0:HALF].rearrange("p (k q) -> p k q", k=CT), ACT.Copy).then_inc(probT_ready, 1)

                def copy_o(i, g):
                    act.wait_ge(pv_done, i * NG + g + 1)
                    wait(act, o_stored[g % 2], (i * (NG // 2) + g // 2) * 16)
                    act.activation(oT[:, g % 2, :], O[:, 0:HALF], ACT.Copy).then_inc(o_out, 1)

                def store_o(i, g):
                    act.wait_ge(o_out, i * NG + g + 1)
                    it, gg = (i, g) if g >= 0 else (i - 1, g + NG)
                    act.dma_start(oT_d[it][:, gg % 2, HALF * (gg // 2):HALF * (gg // 2) + HALF], oT[:, g % 2, :]).then_inc(o_stored[g % 2], 16)

                def back(i, s):
                    g, k = (s - LAG - 2 * GRP) // GRP, (s - LAG - 2 * GRP) % GRP
                    if k == 0 and real(i, g):
                        copy_o(i, g)
                    n = s - LAG
                    if real(i, n) and n < STEPS:
                        copy_probT(i, n)
                    if k == 1 and real(i, g):
                        store_o(i, g)

                def iteration(b, g):
                    i = b * KV + g
                    now = {s: rest for rest in uses(b, g) for s in (rest[1],)}
                    for s in range(STEPS):
                        if real(i, s - 1):
                            exps(i, s - 1)
                        if s in now:
                            n, _, job, c, h, rot, at = now[s]
                            evacuate(n, job, c, h, rot, at, b + 1)
                        back(i, s)

                def drain():
                    exps(NIT - 1, STEPS - 1)
                    for s in range(STEPS, STEPS + LAG + GRP + 2):
                        back(NIT - 1, s)
                    for q in range(2):
                        act.wait_ge(o_stored[q], NIT * NG // 2 * 16)

                for n, (_, job, c, h) in enumerate(FIRST):
                    rot = (n - len(V_USES)) // 2
                    evacuate(n, job, c, h, rot, rot, 0)
                loop(act, iteration, drain)

            @block.gpsimd
            def _(pool):
                with pool.Fori(0, NIT * STEPS // RING) as k:
                    for s in range(RING):
                        hold(pool, inv_ready, k * RING + s + 1)
                        pool.tensor_scalar(prob[:, s, :], prob[:, s, :], inv[:, s:s + 1], 1.0, ALU.mult, ALU.mult).then_inc(norm_ready, 1)

            @block.vector
            def _(v):
                def rotate(rot, at, job, c, part, made, free):
                    k = Tally(v, dve, rot * LINKS)
                    k.n = 2 * part
                    tok = slice(HALF * c, HALF * c + HALF)
                    lower, upper = raw[:, at % 2, 0, :], raw[:, at % 2, 1, :]
                    cos, sin = table[:, "qk".index(job), 0, tok], table[:, "qk".index(job), 1, tok]
                    parts = qp if job == "q" else kp
                    out = [prod[:, 0, :], prod[:, 2, :]]
                    if part == 0:
                        wait(v, dve, k.base)
                        v.wait_ge(x_out, made)
                        k.mark(v.tensor_tensor(prod[:, 0, :], lower, cos, ALU.mult))
                        k.mark(v.tensor_tensor(prod[:, 1, :], upper, sin, ALU.mult))
                        return
                    if part == 1:
                        k.mark(v.tensor_tensor(prod[:, 2, :], upper, cos, ALU.mult))
                        k.mark(v.tensor_tensor(prod[:, 3, :], lower, sin, ALU.mult))
                        return
                    v.wait_ge(dve, k.base + k.n)
                    if part == 2:
                        k.mark(v.tensor_tensor(out[0], prod[:, 0, :], prod[:, 1, :], ALU.subtract))
                        k.mark(v.tensor_tensor(out[1], prod[:, 2, :], prod[:, 3, :], ALU.add))
                    if part == 3:
                        if free:
                            v.wait_ge(*free)
                        for h in range(2):
                            k.mark(v.tensor_copy(parts[:, 0, h, tok], out[h]))
                    if part == 4:
                        for h in range(2):
                            k.mark(v.tensor_tensor(parts[:, 1, h, tok], out[h], parts[:, 0, h, tok].bitcast(F32), ALU.subtract))

                def copy_v(n, par, g):
                    wait(v, pv_done, (n - 1) * NG)
                    v.tensor_copy(val[:, par], vraw[:, :, DH * g:DH * g + DH]).then_inc(v_ready, 1)

                def maxima(i, s):
                    v.wait_ge(scores_ready, i * STEPS + s + 1)
                    v.tensor_reduce(nmax[:, s % RING:s % RING + 1], S[:, s % 2, :, 0:HALF], AX.XY, ALU.max, negate=True).then_inc(max_ready, 1)

                def invert(i, s):
                    v.wait_ge(exp_ready, i * STEPS + s + 1)
                    v.reciprocal(inv[:, s % RING:s % RING + 1], rsum[:, s % RING:s % RING + 1]).then_inc(inv_ready, 1)

                def iteration(b, g):
                    i, par = b * KV + g, g % 2
                    moved = {"q": (q_in[par], (b * 2 + (g // 2 + 1)) * (Q_MOVES * 16)), "k": (k_in[1], (b * 2 + 2) * (K_MOVES * 16))}
                    for s in range(STEPS):
                        maxima(i, s)
                        if real(i, s - 1):
                            invert(i, s - 1)
                        for rot, at, first, job, c, made in rots(b, g):
                            if first <= s < first + 5:
                                rotate(rot, at, job, c, s - first, made, moved[job] if c == 0 else None)
                        if s == VCOPY_AT and not last_it(i):
                            if g == KV - 1:
                                v.wait_ge(x_out, use_no(b + 1, 0, 0))
                            copy_v(i + 1, 1 - par, (g + 1) % KV)

                v.wait_ge(tables_in, 16)
                for rot, (job, c) in enumerate(FIRST_ROTS):
                    for part in range(5):
                        rotate(rot, rot, job, c, part, len(V_USES) + 2 * rot + 2, None)
                copy_v(0, 0, 0)
                loop(v, iteration, lambda: invert(NIT - 1, STEPS - 1))


def route(nc, sem, io, ident, img_d, oT_d, xs_d, h1, pos, gate, run, base, exp_i, src_i, tail_i, move, weights, weights_in):
    w1, w2, b1, b2 = weights
    with ExitStack() as ctx:
        def sb(name, shape, dt=F32):
            return ctx.enter_context(nc.sbuf_tensor(name, shape, dt))

        wo = sb("r_wo", [P, KV * 2, D])
        wr, br = sb("r_wr", [P, KC, NE]), sb("r_br", [P, NE])
        below, ones = sb("r_below", [P, P]), sb("r_ones", [P, P])
        eight = sb("r_eight", [P, NE])
        oT = sb("r_oT", [P, 3, KV, 2, P])
        st, mv = sb("r_st", [P, TT, 6]), sb("r_mv", [P, TT, 2])
        ve, sd, y, y2, rstd = (sb(f"r_s{n}", [P, TT]) for n in range(5))
        xn = sb("r_xn", [P, 2, TT, D])
        xT = sb("r_xT", [P, KC, SEQ])
        lg, m8, i8 = sb("r_lg", [P, TT, NE]), sb("r_m8", [P, TT, 8]), sb("r_i8", [P, TT, 8], U32)
        top = sb("r_top", [P, TT, TOPK])
        hot = sb("r_hot", [P, TOPK, TT, NE])
        mask, off, slot = sb("r_mask", [P, TT, NE]), sb("r_off", [P, TT, NE]), sb("r_slot", [P, TT, NE])
        pick = sb("r_pick", [P, TOPK, TT, NE])
        posf = sb("r_posf", [P, TOPK, TT])
        idx = sb("r_idx", [P, 2, TOPK, TT], U32)
        gr = sb("r_gr", [P, TT])
        tile_no, zeros = sb("r_tile_no", [P, NT]), sb("r_zeros", [P, D])
        dl, ex, den = (sb(f"r_g{n}", [P, TT]) for n in range(3))
        A = ctx.enter_context(nc.psum_tensor("ps_ra", [P, 3, 512], F32))
        XT = ctx.enter_context(nc.psum_tensor("ps_rx", [P, 3, 512], F32))
        L = ctx.enter_context(nc.psum_tensor("ps_rl", [P, 512], F32))
        C = ctx.enter_context(nc.psum_tensor("ps_rc", [P, 2, TT, NE], F32))

        w_in, const = sem("r_w_in"), sem("r_const")
        h_in = [sem(f"r_h_in{q}") for q in range(2)]
        oT_in = [sem(f"r_oT_in{q}") for q in range(3)]
        oT_free, h1_ready, var_ready, sd_ready, xn_ready = (sem(f"r_{n}") for n in ("oT_free", "h1_ready", "var_ready", "sd_ready", "xn_ready"))
        rstd_ready, run_ready, xn_free = sem("r_rstd_ready"), sem("r_run_ready"), sem("r_xn_free")
        tr_done, xT_ready, lg_done = sem("r_tr_done"), sem("r_xT_ready"), sem("r_lg_done")
        mask_ready, count_done, gap_ready, ex_ready, idx_ready = (sem(f"r_{n}") for n in ("mask_ready", "count_done", "gap_ready", "ex_ready", "idx_ready"))
        table_dve, table_ready, zeroed = (sem(f"r_{n}") for n in ("table_dve", "table_ready", "zeroed"))
        norm_dve, pick_dve, place_dve = sem("r_norm_dve"), sem("r_pick_dve"), sem("r_place_dve")
        scattered = [sem(f"r_scattered{q}") for q in range(2)]
        TURN_AT, LOGITS_AT = 2, 3
        NORM, PICK, PLACE = 2 * TT + 4, 2 * TT + 4, TT + 8

        def loop(iteration, drain, eng):
            iteration(0, 0)
            with eng.Fori(0, (NB - 2) // 2) as k:
                iteration(k * 2 + 1, 1)
                iteration(k * 2 + 2, 0)
            iteration(NB - 1, 1)
            drain()

        first = lambda b: isinstance(b, int) and b == 0


        with nc.Block() as block:
            @block.sync
            def _(sp):
                sp.dma_start(wo[:], io["Wo"].rearrange("(k p) n -> p k n", p=P)).then_inc(w_in, 16)
                sp.dma_start(wr[:], io["Wr"].rearrange("(k p) n -> p k n", p=P)).then_inc(w_in, 16)
                sp.dma_start(br[:], io["br"].unsqueeze(0).to_broadcast([P, NE])).then_inc(w_in, 16)
                oT_b = oT_d.rearrange("(b g) p h s -> b p g h s", g=KV)
                sp.nop().then_inc(oT_free, 3)

                def load(b):
                    for t in range(TT):
                        sp.wait_ge(oT_free, b * TT + t + 1)
                        for g in range(KV):
                            sp.dma_start(oT[:, t % 3, g], oT_b[b][:, g, :, P * t:P * t + P]).then_inc(oT_in[t % 3], 16)

                load(0)
                sp.dma_start(w1[:], io["W1"].rearrange("e (c p) f -> p e c f", p=P)).then_inc(weights_in, 16)
                load(1)
                sp.dma_start(b1[:], io["b1"].unsqueeze(0).to_broadcast([P, NE, FF])).then_inc(weights_in, 16)
                load(2)
                sp.dma_start(w2[:], io["W2"].rearrange("e (c p) f -> p e c f", p=P)).then_inc(weights_in, 16)
                load(3)
                sp.dma_start(b2[:], io["b2"].unsqueeze(0).to_broadcast([P, NE, D])).then_inc(weights_in, 16)
                with sp.Fori(4, NB) as b:
                    load(b)
                sp.wait_ge(weights_in, 64)
                sp.wait_ge(table_ready, 1)
                for q in range(2):
                    sp.wait_ge(scattered[q], NB // 2 * TT * TOPK * 16)
                for x in range(NE):
                    row = sp.value_load(tail_i[0:1, x:x + 1], min_val=x * STRIDE, max_val=x * STRIDE + TOK)
                    sp.dma_start(xs_d[bass.ds(row, P), :], zeros[:]).then_inc(zeroed, 16)
                sp.wait_ge(zeroed, 16 * NE)

            @block.gpsimd
            def _(pool):
                pool.memset(ones[:], 1.0).then_inc(const, 1)
                pool.wait_ge(const, 1)
                pool.affine_select(out=below[:], in_=ones[:], compare_op=ALU.is_gt, fill=0.0, base=0,
                                   pattern=[[1, P]], channel_multiplier=-1).then_inc(const, 1)
                pool.iota(eight[:], [[1, NE]], base=0, channel_multiplier=0, allow_small_or_imprecise_dtypes=True).then_inc(const, 1)
                pool.iota(base[:], [[STRIDE, NE]], base=0, channel_multiplier=0, allow_small_or_imprecise_dtypes=True).then_inc(const, 1)
                pool.iota(tile_no[:], [[1, NT]], base=0, channel_multiplier=0, allow_small_or_imprecise_dtypes=True).then_inc(const, 1)
                pool.memset(zeros[:], 0.0).then_inc(const, 1)
                pool.nop().then_inc(xn_free, 2)
                with pool.Fori(0, NB // 2) as k:
                    for q in range(2):
                        hold(pool, idx_ready, k * 2 + q + 2)
                        for t in range(TT):
                            for e in range(TOPK):
                                pool.indirect_dma_start(out=xs_d, out_offset=bass.IndirectOffsetOnAxis(ap=idx[:, q, e, t:t + 1], axis=0),
                                                        in_=xn[:, q, t, :], in_offset=None).then_inc(scattered[q], 16)
                        pool.wait_ge(scattered[q], k * (TT * TOPK * 16) + TT * TOPK * 16)
                        pool.nop().then_inc(xn_free, 1)

            @block.tensor
            def _(pe):
                def project(b, t):
                    pe.wait_ge(oT_in[t % 3], b * (TT // 3 * KV * 16) + (t // 3 + 1) * KV * 16)
                    pe.wait_ge(h1_ready, b * TT + t + 1)
                    for c in range(KV * 2):
                        last = pe.matmul(A[:, t % 3, 0:D], oT[:, t % 3, c // 2, c % 2, :], wo[:, c, :], start=(c == 0), stop=(c == KV * 2 - 1))
                    last.then_inc(oT_free, 1)

                def turn(b, q):
                    pe.wait_ge(xn_ready, b + 1)
                    for n in range(3):
                        for m in range(4):
                            c, t = (4 * n + m) // TT, (4 * n + m) % TT
                            last = pe.transpose(XT[:, n, P * m:P * m + P], xn[:, q, t, P * c:P * c + P], ident[:])
                        last.then_inc(tr_done, 1)

                def logits(b):
                    pe.wait_ge(xT_ready, b * 3 + 3)
                    pe.wait_ge(mask_ready, b + 1)
                    for t in range(TT):
                        for c in range(KC):
                            last = pe.matmul(L[:, NE * t:NE * t + NE], xT[:, c, P * t:P * t + P], wr[:, c, :], start=(c == 0), stop=(c == KC - 1))
                    last.then_inc(lg_done, 1)

                def counts(b):
                    pe.wait_ge(mask_ready, b + 2)
                    pe.wait_ge(idx_ready, b + 1)
                    m = mask[:].rearrange("p t e -> p (t e)")
                    pe.matmul(C[:, 0].rearrange("p t e -> p (t e)"), below[:], m, start=True, stop=True)
                    pe.matmul(C[:, 1].rearrange("p t e -> p (t e)"), ones[:], m, start=True, stop=True).then_inc(count_done, 1)

                def iteration(b, q):
                    for t in range(TT):
                        project(b, t)
                        if not first(b) and t == TURN_AT:
                            turn(b - 1, 1 - q)
                        if not first(b) and t == LOGITS_AT:
                            logits(b - 1)
                    if not first(b):
                        counts(b - 1)

                def drain():
                    turn(NB - 1, 1)
                    logits(NB - 1)
                    counts(NB - 1)

                pe.wait_ge(w_in, 48)
                pe.wait_ge(const, 4)
                loop(iteration, drain, pe)

            @block.scalar
            def _(act):
                def root(b):
                    act.wait_ge(var_ready, b + 1)
                    act.activation(sd[:], ve[:], ACT.Sqrt).then_inc(sd_ready, 1)

                def turned(b):
                    for n in range(3):
                        act.wait_ge(tr_done, b * 3 + n + 1)
                        act.activation(xT[:].rearrange("p c s -> p (c s)")[:, 512 * n:512 * n + 512], XT[:, n], ACT.Copy).then_inc(xT_ready, 1)

                def exp_gap(b):
                    act.wait_ge(gap_ready, b + 1)
                    act.activation(ex[:], dl[:], ACT.Exp).then_inc(ex_ready, 1)

                def load(b, q):
                    act.dma_start(h1[:, b, 0:IT, :], img_d[b].rearrange("(t p) d -> p t d", p=P)).then_inc(h_in[q], 16)
                    act.dma_start(h1[:, b, IT:TT, :], io["txt"][b].rearrange("(t p) d -> p t d", p=P)).then_inc(h_in[q], 16)

                def iteration(b, q):
                    if not first(b):
                        turned(b - 1)
                        if not isinstance(b, int):
                            load(b + 1, 1 - q)
                        exp_gap(b - 1)
                    root(b)

                load(0, 0)
                load(1, 1)

                def drain():
                    turned(NB - 1)
                    exp_gap(NB - 1)

                loop(iteration, drain, act)

            @block.vector
            def _(v):
                def add(b, q, t):
                    if t == 0:
                        v.wait_ge(h_in[q], (b >> 1) * 32 + 32)
                    if t < TT:
                        v.wait_ge(oT_free, b * TT + t + 4)
                        v.tensor_tensor(h1[:, b, t, :], A[:, t % 3, 0:D], h1[:, b, t, :], ALU.add).then_inc(h1_ready, 1)
                    if t > 0:
                        hold(v, h1_ready, b * TT + t + 3)
                        v.bn_stats(st[:, t - 1, :], h1[:, b, t - 1, :]).then_inc(norm_dve, 1)

                def norm(b, q):
                    k = Tally(v, norm_dve, b * NORM)
                    k.n = TT
                    hold(v, norm_dve, k.base + k.n)
                    for t in range(TT):
                        k.mark(v.bn_aggr(mv[:, t, :], st[:, t, :]))
                    v.wait_ge(norm_dve, k.base + k.n)
                    v.tensor_scalar(ve[:], mv[:, :, 1], EPS, None, ALU.add).then_inc(var_ready, 1)
                    v.wait_ge(sd_ready, b + 1)
                    k.link(v.reciprocal(y[:], sd[:]))
                    k.link(v.tensor_tensor(y2[:], y[:], y[:], ALU.mult))
                    k.link(v.tensor_tensor(y2[:], y2[:], ve[:], ALU.mult))
                    k.link(v.tensor_scalar(y2[:], y2[:], -0.5, 1.5, ALU.mult, ALU.add))
                    assert k.n == NORM
                    v.tensor_tensor(rstd[:], y[:], y2[:], ALU.mult).then_inc(rstd_ready, 1)
                    v.wait_ge(rstd_ready, b + 1)
                    v.wait_ge(xn_free, b + 1)
                    for t in range(TT):
                        last = v.tensor_scalar(xn[:, q, t, :], h1[:, b, t, :], mv[:, t, 0:1], rstd[:, t:t + 1], ALU.subtract, ALU.mult)
                    last.then_inc(xn_ready, 1)

                def choose(b):
                    k = Tally(v, pick_dve, b * PICK)
                    v.wait_ge(lg_done, b + 1)
                    k.mark(v.tensor_tensor(lg[:], L[:, 0:TT * NE].rearrange("p (t e) -> p t e", e=NE), br[:].unsqueeze(1).to_broadcast([P, TT, NE]), ALU.add))
                    hold(v, pick_dve, k.base + k.n)
                    for t in range(TT):
                        k.mark(v.max(m8[:, t, :], lg[:, t, :]))
                    hold(v, pick_dve, k.base + k.n)
                    for t in range(TT):
                        k.mark(v.max_index(i8[:, t, :], m8[:, t, :], lg[:, t, :]))
                    v.wait_ge(pick_dve, k.base + k.n)
                    k.link(v.tensor_copy(top[:], i8[:, :, 0:TOPK]))
                    for e in range(TOPK):
                        k.mark(v.tensor_tensor(hot[:, e], eight[:].unsqueeze(1).to_broadcast([P, TT, NE]),
                                               top[:, :, e:e + 1].to_broadcast([P, TT, NE]), ALU.is_equal))
                    v.wait_ge(pick_dve, k.base + k.n)
                    assert k.n == PICK
                    v.tensor_tensor(mask[:], hot[:, 0], hot[:, 1], ALU.add).then_inc(mask_ready, 1)
                    v.tensor_tensor(dl[:], m8[:, :, 1], m8[:, :, 0], ALU.subtract).then_inc(gap_ready, 1)

                def place(b, q):
                    k = Tally(v, place_dve, b * PLACE)
                    v.wait_ge(ex_ready, b + 1)
                    k.link(v.tensor_scalar(den[:], ex[:], 1.0, None, ALU.add))
                    k.link(v.reciprocal(gr[:], den[:]))
                    v.tensor_copy(gate[:, b, 0, :], gr[:])
                    v.tensor_tensor(gate[:, b, 1, :], ex[:], gr[:], ALU.mult)
                    v.wait_ge(count_done, b + 1)
                    k.link(v.tensor_copy(off[:, 0, :], run[:]))
                    for t in range(TT):
                        out = off[:, t + 1, :] if t < TT - 1 else run[:]
                        k.link(v.tensor_tensor(out, off[:, t, :], C[:, 1, t, :], ALU.add))
                    k.link(v.tensor_tensor(slot[:], off[:], C[:, 0], ALU.add))
                    for e in range(TOPK):
                        k.mark(v.tensor_tensor(pick[:, e], hot[:, e], slot[:], ALU.mult))
                    v.wait_ge(place_dve, k.base + k.n)
                    k.mark(v.tensor_reduce(posf[:], pick[:], AX.X, ALU.add))
                    v.wait_ge(place_dve, k.base + k.n)
                    k.mark(v.tensor_copy(pos[:, b, :, :], posf[:]))
                    assert k.n == PLACE, k.n
                    v.tensor_copy(idx[:, q], posf[:]).then_inc(idx_ready, 1)

                def iteration(b, q):
                    for t in range(TT + 1):
                        add(b, q, t)
                        if not first(b) and t == LOGITS_AT:
                            choose(b - 1)
                    norm(b, q)
                    if not first(b):
                        place(b - 1, 1 - q)

                def drain():
                    choose(NB - 1)
                    place(NB - 1, 1)
                    tile_table(v, sb, table_dve, run, base, tile_no, exp_i, src_i, tail_i, move).then_inc(table_ready, 1)

                v.nop().then_inc(h1_ready, 3)
                v.nop().then_inc(mask_ready, 1)
                v.nop().then_inc(idx_ready, 1)
                v.wait_ge(w_in, 48)
                v.wait_ge(const, 6)
                v.tensor_copy(run[:], base[:]).then_inc(run_ready, 1)
                v.wait_ge(run_ready, 1)
                loop(iteration, drain, v)


def tile_table(v, sb, dve, run, base, j, exp_i, src_i, tail_i, move):
    n, cnt, end = sb("t_n", [P, NE]), sb("t_cnt", [P, NE]), sb("t_end", [P, NE])
    ni = sb("t_ni", [P, NE], I32)
    last = sb("t_last", [P, 1])
    jr, e, start, ind = (sb(f"t_{x}", [P, NT]) for x in ("jr", "e", "start", "ind"))
    k = Tally(v, dve)
    link, mark = k.link, k.mark
    mark(v.tensor_copy(tail_i[:], run[:]))
    mark(v.memset(e[:], 0.0))
    mark(v.memset(start[:], 0.0))
    link(v.tensor_tensor(n[:], run[:], base[:], ALU.subtract))
    link(v.tensor_scalar(ni[:], n[:], float(P - 1), None, ALU.add))
    link(v.tensor_scalar(ni[:], ni[:], 7, None, ALU.arith_shift_right))
    link(v.tensor_copy(cnt[:], ni[:]))
    mark(v.tensor_scalar(move[:], cnt[:], float(P), -float(STRIDE), ALU.mult, ALU.add))
    link(v.tensor_copy(end[:, 0:1], cnt[:, 0:1]))
    for x in range(1, NE):
        link(v.tensor_tensor(end[:, x:x + 1], end[:, x - 1:x], cnt[:, x:x + 1], ALU.add))
    link(v.tensor_scalar(last[:], end[:, NE - 1:NE], -1.0, None, ALU.add))
    link(v.tensor_scalar(jr[:], j[:], last[:], None, ALU.min))
    for x in range(NE - 1):
        link(v.tensor_scalar(ind[:], jr[:], end[:, x:x + 1], None, ALU.is_ge))
        mark(v.tensor_tensor(e[:], e[:], ind[:], ALU.add))
        link(v.scalar_tensor_tensor(out=start[:], in0=ind[:], scalar=cnt[:, x:x + 1], in1=start[:], op0=ALU.mult, op1=ALU.add))
    link(v.tensor_tensor(start[:], jr[:], start[:], ALU.subtract))
    link(v.tensor_scalar(start[:], start[:], float(P), None, ALU.mult))
    mark(v.tensor_copy(exp_i[:], e[:]))
    return v.scalar_tensor_tensor(out=src_i[:], in0=e[:], scalar=float(STRIDE), in1=start[:], op0=ALU.mult, op1=ALU.add)


def experts(nc, sem, ident, xs_d, ys_d, exp_i, src_i, pos, move, weights):
    RING = 4
    w1, w2, b1, b2 = weights
    with ExitStack() as ctx:
        def sb(name, shape, dt=F32):
            return ctx.enter_context(nc.sbuf_tensor(name, shape, dt))

        x, xT = sb("e_x", [P, RING, D]), sb("e_xT", [P, 2, D])
        h, hT, y = sb("e_h", [P, 2, FF]), sb("e_hT", [P, 2, FF]), sb("e_y", [P, RING, D])
        X = ctx.enter_context(nc.psum_tensor("ps_ex", [P, 2, 512], F32))
        H = ctx.enter_context(nc.psum_tensor("ps_eh", [P, 2, 512], F32))
        HT = ctx.enter_context(nc.psum_tensor("ps_et", [P, 2, 512], F32))
        Y = ctx.enter_context(nc.psum_tensor("ps_ey", [P, 2, 512], F32))
        x_in = [sem(f"e_x_in{q}") for q in range(RING)]
        xt_done, xT_ready, h_done, h_ready, ht_done, hT_ready, y_done, y_ready = (
            sem(f"e_{n}") for n in ("xt_done", "xT_ready", "h_done", "h_ready", "ht_done", "hT_ready", "y_done", "y_ready"))
        stored = [sem(f"e_stored{q}") for q in range(RING)]

        def wait(eng, s, value):
            if not isinstance(value, int) or value > 0:
                eng.wait_ge(s, value)

        where, moved, past = (sb(f"e_{x}", [P, NB * TOPK * TT]) for x in ("where", "moved", "past"))
        pos_dve = sem("e_pos_dve")

        def loop(eng, tile, between=None):
            for n in range(RING):
                tile(n, n)
            if between:
                between()
            with eng.Fori(1, NT // RING - 1) as k:
                for n in range(RING):
                    tile(k * RING + n, n)
            for n in range(RING):
                tile(NT - RING + n, n)

        def more(j, ahead):
            return not (isinstance(j, int) and j + ahead >= NT)

        def at(table, j):
            return table[0:1, bass.ds(j, 1)]

        with nc.Block() as block:
            @block.sync
            def _(sp):
                def load(j, n):
                    row = sp.value_load(at(src_i, j), min_val=0, max_val=SLOTS - P)
                    sp.dma_start(x[:, n, :], xs_d[bass.ds(row, P), :]).then_inc(x_in[n], 16)
                for n in range(RING):
                    load(n, n)

                def tile(j, n):
                    if more(j, RING):
                        sp.wait_ge(xt_done, j + 1)
                        load(j + RING, n)

                loop(sp, tile)

            @block.tensor
            def _(pe):
                def turn_x(j, n):
                    q = n % 2
                    pe.wait_ge(x_in[n], (j >> 2) * 16 + 16)
                    wait(pe, xT_ready, j - 1)
                    for c in range(KC):
                        last = pe.transpose(X[:, q, P * c:P * c + P], x[:, n, P * c:P * c + P], ident[:])
                    last.then_inc(xt_done, 1)

                def up(j, q, ex):
                    pe.wait_ge(xT_ready, j + 1)
                    wait(pe, h_ready, j - 1)
                    for c in range(KC):
                        last = pe.matmul(H[:, q, :], xT[:, q, P * c:P * c + P], w1[:, bass.ds(ex, 1), c, :], start=(c == 0), stop=(c == KC - 1))
                    last.then_inc(h_done, 1)

                def turn_h(j, q):
                    pe.wait_ge(h_ready, j + 1)
                    wait(pe, hT_ready, j - 1)
                    for c in range(FC):
                        last = pe.transpose(HT[:, q, P * c:P * c + P], h[:, q, P * c:P * c + P], ident[:])
                    last.then_inc(ht_done, 1)

                def down(j, q, ex):
                    pe.wait_ge(hT_ready, j + 1)
                    wait(pe, y_ready, j - 1)
                    for c in range(FC):
                        last = pe.matmul(Y[:, q, 0:D], hT[:, q, P * c:P * c + P], w2[:, bass.ds(ex, 1), c, :], start=(c == 0), stop=(c == FC - 1))
                    last.then_inc(y_done, 1)

                def expert(j):
                    return pe.value_load(at(exp_i, j), min_val=0, max_val=NE - 1)

                def tile(j, n):
                    q = n % 2
                    if more(j, 1):
                        turn_x(j + 1, (n + 1) % RING)
                    up(j, q, expert(j))
                    if not (isinstance(j, int) and j == 0):
                        down(j - 1, 1 - q, expert(j - 1))
                    turn_h(j, q)

                turn_x(0, 0)
                loop(pe, tile)
                down(NT - 1, 1, expert(NT - 1))

            @block.scalar
            def _(act):
                def copy_x(j, q):
                    act.wait_ge(xt_done, j + 1)
                    wait(act, h_done, j - 1)
                    act.activation(xT[:, q, :], X[:, q, 0:D], ACT.Copy).then_inc(xT_ready, 1)

                def relu_h(j, q):
                    act.wait_ge(ht_done, j + 1)
                    wait(act, y_done, j - 1)
                    act.activation(hT[:, q, :], HT[:, q, :], ACT.Relu).then_inc(hT_ready, 1)

                def store(j, n):
                    act.wait_ge(y_ready, j + 1)
                    act.dma_start(ys_d[j], y[:, n, :]).then_inc(stored[n], 16)

                def tile(j, n):
                    q = n % 2
                    if more(j, 1):
                        copy_x(j + 1, 1 - q)
                    relu_h(j, q)
                    if not (isinstance(j, int) and j < 2):
                        store(j - 2, (n - 2) % RING)

                copy_x(0, 0)
                loop(act, tile)
                for n in (2, 3):
                    store(NT - RING + n, n)
                for n in range(RING):
                    act.wait_ge(stored[n], NT // RING * 16)

            @block.vector
            def _(v):
                def bias_h(j, q):
                    ex = v.value_load(at(exp_i, j), min_val=0, max_val=NE - 1)
                    v.wait_ge(h_done, j + 1)
                    wait(v, ht_done, j - 1)
                    v.tensor_tensor(h[:, q, :], H[:, q, :], b1[:, bass.ds(ex, 1), :].rearrange("p o f -> p (o f)"), ALU.add).then_inc(h_ready, 1)

                def bias_y(j, n):
                    q = n % 2
                    ex = v.value_load(at(exp_i, j), min_val=0, max_val=NE - 1)
                    v.wait_ge(y_done, j + 1)
                    wait(v, stored[n], (j >> 2) * 16)
                    v.tensor_tensor(y[:, n, :], Y[:, q, 0:D], b2[:, bass.ds(ex, 1), :].rearrange("p o f -> p (o f)"), ALU.add).then_inc(y_ready, 1)

                def tile(j, n):
                    bias_h(j, n % 2)
                    if not (isinstance(j, int) and j == 0):
                        bias_y(j - 1, (n - 1) % RING)

                def renumber():
                    k = Tally(v, pos_dve)
                    k.link(v.tensor_copy(where[:], pos[:].rearrange("p b k t -> p (b k t)")))
                    k.link(v.tensor_copy(moved[:], where[:]))
                    for x in range(NE - 1):
                        k.link(v.tensor_scalar(past[:], where[:], float((x + 1) * STRIDE), None, ALU.is_ge))
                        k.link(v.scalar_tensor_tensor(out=moved[:], in0=past[:], scalar=move[:, x:x + 1], in1=moved[:], op0=ALU.mult, op1=ALU.add))
                    k.link(v.tensor_copy(pos[:].rearrange("p b k t -> p (b k t)"), moved[:]))

                loop(v, tile, renumber)
                bias_y(NT - 1, RING - 1)


def combine(nc, sem, ys_d, h1, pos, gate, out):
    with ExitStack() as ctx:
        def sb(name, shape, dt=F32):
            return ctx.enter_context(nc.sbuf_tensor(name, shape, dt))

        idx = sb("c_idx", [P, 2, TOPK, TT], U32)
        gt = sb("c_gt", [P, 2, TOPK, TT])
        yg = sb("c_yg", [P, 2, TOPK, TT, D])
        part, res = sb("c_part", [P, TT, D]), sb("c_res", [P, 2, TT, D])
        idx_ready, gt_ready, part_ready, res_ready = (sem(f"c_{n}") for n in ("idx_ready", "gt_ready", "part_ready", "res_ready"))
        gathered = [sem(f"c_gathered{q}") for q in range(2)]
        stored = [sem(f"c_stored{q}") for q in range(2)]

        with nc.Block() as block:
            @block.vector
            def _(v):
                def indices(b, q):
                    v.tensor_copy(gt[:, q], gate[:, b, :, :]).then_inc(gt_ready, 1)
                    v.tensor_copy(idx[:, q], pos[:, b, :, :]).then_inc(idx_ready, 1)

                def total(b, k, q):
                    v.wait_ge(gathered[q], k * (TT * TOPK * 16) + TT * TOPK * 16)
                    v.wait_ge(gt_ready, b + 1)
                    for t in range(TT):
                        last = v.scalar_tensor_tensor(out=part[:, t, :], in0=yg[:, q, 0, t, :], scalar=gt[:, q, 0, t:t + 1], in1=h1[:, b, t, :],
                                                      op0=ALU.mult, op1=ALU.add)
                    last.then_inc(part_ready, 1)
                    v.wait_ge(part_ready, b + 1)
                    v.wait_ge(stored[q], k * 16 + 16)
                    for t in range(TT):
                        last = v.scalar_tensor_tensor(out=res[:, q, t, :], in0=yg[:, q, 1, t, :], scalar=gt[:, q, 1, t:t + 1], in1=part[:, t, :],
                                                      op0=ALU.mult, op1=ALU.add)
                    last.then_inc(res_ready, 1)
                    v.wait_ge(res_ready, b + 1)

                indices(0, 0)
                indices(1, 1)
                with v.Fori(0, NB // 2 - 1) as k:
                    for q in range(2):
                        total(k * 2 + q, k, q)
                        indices(k * 2 + q + 2, q)
                for q in range(2):
                    total(NB - 2 + q, NB // 2 - 1, q)

            @block.gpsimd
            def _(pool):
                with pool.Fori(0, NB // 2) as k:
                    for q in range(2):
                        hold(pool, idx_ready, k * 2 + q + 1)
                        for t in range(TT):
                            for e in range(TOPK):
                                pool.indirect_dma_start(out=yg[:, q, e, t, :], out_offset=None, in_=ys_d.rearrange("t p d -> (t p) d"),
                                                        in_offset=bass.IndirectOffsetOnAxis(ap=idx[:, q, e, t:t + 1], axis=0)).then_inc(gathered[q], 16)

            @block.sync
            def _(sp):
                for q in range(2):
                    sp.nop().then_inc(stored[q], 16)
                with sp.Fori(0, NB // 2) as k:
                    for q in range(2):
                        sp.wait_ge(res_ready, k * 2 + q + 1)
                        sp.dma_start(out[k * 2 + q].rearrange("(t p) d -> p t d", p=P), res[:, q]).then_inc(stored[q], 16)
                for q in range(2):
                    sp.wait_ge(stored[q], NB // 2 * 16 + 16)


def program(nc, x, txt, log_dt, inv_A_real, A_imag, B_ri, Wq, Wk, Wv, Wo, Wr, br, W1, b1, W2, b2, rotary, out):
    io = dict(x=x, txt=txt, log_dt=log_dt, inv_A_real=inv_A_real, A_imag=A_imag, B_ri=B_ri, Wo=Wo, Wr=Wr, br=br,
              W1=W1, b1=b1, W2=W2, b2=b2, rotary=rotary, Wq=Wq, Wk=Wk, Wv=Wv)
    img_d = nc.dram_tensor("img_d", (NB, IMG, D), F32, kind="Internal").ap()
    xnT_d = nc.dram_tensor("xnT_d", (NB, P, KC, SEQ), F32, kind="Internal").ap()
    oT_d = nc.dram_tensor("oT_d", (NIT, P, 2, SEQ), F32, kind="Internal").ap()
    xs_d = nc.dram_tensor("xs_d", (SLOTS, D), F32, kind="Internal").ap()
    ys_d = nc.dram_tensor("ys_d", (NT, P, D), F32, kind="Internal").ap()
    with ExitStack() as ctx:
        def sb(name, shape, dt=F32):
            return ctx.enter_context(nc.sbuf_tensor(name, shape, dt))

        def sem(name):
            return ctx.enter_context(nc.semaphore(name))

        ident = sb("ident", [P, P])
        vandermonde(nc, sem, io, ident, img_d)
        norm_in(nc, sem, io, ident, img_d, xnT_d)
        attention(nc, sem, io, ident, xnT_d, oT_d)
        h1 = sb("h1", [P, NB, TT, D])
        pos = sb("pos", [P, NB, TOPK, TT], U32)
        gate = sb("gate", [P, NB, TOPK, TT])
        run, base = sb("run", [P, NE]), sb("base", [P, NE])
        exp_i, src_i = sb("exp_i", [P, NT], I32), sb("src_i", [P, NT], I32)
        tail_i, move = sb("tail_i", [P, NE], I32), sb("move", [P, NE])
        with ExitStack() as held:
            def weight(name, shape):
                return held.enter_context(nc.sbuf_tensor(name, shape, F32))

            weights = (weight("ew1", [P, NE, KC, FF]), weight("ew2", [P, NE, FC, D]), weight("eb1", [P, NE, FF]), weight("eb2", [P, NE, D]))
            route(nc, sem, io, ident, img_d, oT_d, xs_d, h1, pos, gate, run, base, exp_i, src_i, tail_i, move, weights, sem("weights_in"))
            experts(nc, sem, ident, xs_d, ys_d, exp_i, src_i, pos, move, weights)
        combine(nc, sem, ys_d, h1, pos, gate, out)


def rotary_tables():
    f = np.float32
    inv_freq = (f(1.0) / f(10000.0) ** (np.arange(0, DH, 2, dtype=f) / f(DH))).astype(f)
    angle = inv_freq[:, None] * np.arange(SEQ, dtype=f)[None, :]
    both = np.tile(np.stack([np.cos(angle), np.sin(angle)], 1), (P // (DH // 2), 1, 1))
    return np.ascontiguousarray(np.stack([both * f(DH ** -0.5), both], 1).astype(f))


_INS = ["x", "txt", "L0_tok_log_dt", "L0_tok_inv_A_real", "L0_tok_A_imag", "L0_tok_B_ri",
        "L0_attn_Wq", "L0_attn_Wk", "L0_attn_Wv", "L0_attn_Wo",
        "L0_ffn_Wr", "L0_ffn_br", "L0_ffn_W1", "L0_ffn_b1", "L0_ffn_W2", "L0_ffn_b2"]


def kernel(**inputs):
    import numpy as _np
    import concourse.bacc as _bacc
    from concourse import mybir as _mybir
    from concourse.bass_utils import run_bass_kernel_spmd as _run

    nc = _bacc.Bacc("TRN2", target_bir_lowering=False, num_devices=1)
    arrays, args = {}, []
    for name, a in [(n, inputs[n]) for n in _INS] + [("rotary", rotary_tables())]:
        a = _np.ascontiguousarray(a)
        arrays[f"in_{name}_dram"] = a
        args.append(nc.dram_tensor(f"in_{name}_dram", a.shape, _mybir.dt.from_np(a.dtype), kind="ExternalInput").ap())
    args.append(nc.dram_tensor("out_0_dram", (NB, SEQ, D), F32, kind="ExternalOutput").ap())
    program(nc, *args)
    r = _run(nc, [arrays], core_ids=[0])
    return r.results[0]["out_0_dram"]
```

```python
import math
from contextlib import ExitStack

import numpy as np

import concourse.bass as bass
from concourse import mybir

P = 128
NB, SEQ, D = 8, 768, 256
IMG, TXT = 256, 512
NS = 64
HEADS, KV, DH = 16, 4, 64
GH = HEADS // KV
TT = SEQ // P
IT = IMG // P
KC = D // P
TOK = NB * SEQ
NE, FF, TOPK = 8, 512, 2
FC = FF // P
EPS = 1e-5
LOADED = (5 * KC + 3) * 16
NIT = NB * KV
STRIDE = TOK + P
SLOTS = NE * STRIDE
NT = TOK * TOPK // P + NE

F32 = mybir.dt.float32
F32R = mybir.dt.float32r
I32 = mybir.dt.int32
U32 = mybir.dt.uint32
ALU = mybir.AluOpType
ACT = mybir.ActivationFunctionType
AX = mybir.AxisListType


def hold(eng, sem, value):
    eng.wait_ge(sem, value)
    eng.nop(nofuse=True)


class Tally:

    def __init__(self, eng, sem, base=0):
        self.eng, self.sem, self.base, self.n = eng, sem, base, 0

    def mark(self, ins):
        self.n += 1
        ins.then_inc(self.sem, 1)
        return self.n

    def link(self, ins):
        self.eng.wait_ge(self.sem, self.base + self.mark(ins))


def vandermonde(nc, sem, io, ident, img_d, wq, wk, wv, wo, wr, br, loaded):
    AN, BN = 4, 64
    GM = NB * AN
    HH = IMG // P
    SL = 16
    SQUARE = [8, 16, 32]
    LOG2E, MAGIC = 1.4426950408889634, 12582912.0
    LN2HI, LN2LO = 0.693359375, -2.12194440e-4
    with ExitStack() as ctx:
        def sb(name, shape, dt=F32):
            return ctx.enter_context(nc.sbuf_tensor(name, shape, dt))

        logdt, dt = sb("logdt", [P, HH]), sb("dt", [P, HH])
        inva, aim = sb("inva", [P, HH, NS]), sb("aim", [P, HH, NS])
        bri = sb("bri", [P, HH, NS, 2])
        cnat = sb("cnat", [P, NB, HH, NS, 2])
        ex = [sb(f"ex{n}", [P, HH]) for n in range(6)]
        exi = sb("exi", [P, HH], I32)
        nat = [sb(f"nat{n}", [P, HH * NS]) for n in range(8)]
        zre, zim = sb("zre", [P, P]), sb("zim", [P, P])
        b2 = sb("b2", [P, HH, NS, 2])
        wre, wim = sb("wre", [P, BN + 1, P]), sb("wim", [P, BN + 1, P])
        ct = sb("ct", [P, NB, 2, P])
        b2t = sb("b2t", [P, 2, P])
        bare, baim = sb("bare", [P, AN, P]), sb("baim", [P, AN, P])
        ure, uim = sb("ure", [P, AN, P]), sb("uim", [P, AN, P])
        gre, gim = sb("gre", [P, AN, NB, P]), sb("gim", [P, AN, NB, P])
        tm = [sb(f"tm{n}", [P, SL, P]) for n in range(4)]
        kt = sb("kt", [P, HH * 32, BN])
        sq = kt[:].rearrange("p q b -> p (q b)").rearrange("p (r k h) -> p r k h", r=2, h=P)
        ps = ctx.enter_context(nc.psum_tensor("ps_v", [P, 8, 512], F32))

        loaded_a, loaded_c = sem("v_loaded_a"), sem("v_loaded_c")
        exp_done, dve = sem("v_exp_done"), sem("v_dve")
        nat_ready, tr_z, tr_c = sem("v_nat_ready"), sem("v_tr_z"), sem("v_tr_c")
        ct_ready, g_ready, bank_full, bank_out = sem("v_ct_ready"), sem("v_g_ready"), sem("v_bank_full"), sem("v_bank_out")
        stored = sem("v_stored")
        id_ready, known, sq_ready = sem("v_id_ready"), sem("v_known"), sem("v_sq_ready")

        with nc.Block() as block:
            @block.sync
            def _(sp):
                sp.dma_start(logdt[:], io["log_dt"].rearrange("(a p) -> p a", p=P), allow_slow_non_contiguous=True).then_inc(loaded_a, 16)
                sp.dma_start(inva[:], io["inv_A_real"].rearrange("(a p) n -> p a n", p=P)).then_inc(loaded_a, 16)
                sp.dma_start(aim[:], io["A_imag"].rearrange("(a p) n -> p a n", p=P)).then_inc(loaded_a, 16)
                sp.dma_start(bri[:], io["B_ri"].rearrange("(a p) n r -> p a n r", p=P)).then_inc(loaded_a, 16)
                for c in range(NB):
                    sp.dma_start(cnat[:, c], io["x"][c].rearrange("(a p) n r -> p a n r", p=P)).then_inc(loaded_c, 16)
                for c in range(KC):
                    rows = slice(P * c, P * c + P)
                    sp.dma_start(wv[:, c], io["Wv"][rows]).then_inc(loaded, 16)
                    for h in range(2):
                        half = slice(DH // 2 * h, DH // 2 * (h + 1))
                        for w, name in ((wk, "Wk"), (wq, "Wq")):
                            sp.dma_start(w[:, c, h].rearrange("p (x d) -> p x d", d=DH // 2),
                                         io[name][rows].rearrange("p (x d) -> p x d", d=DH)[:, :, half]).then_inc(loaded, 16)
                sp.dma_start(wo[:], io["Wo"].rearrange("(k p) n -> p k n", p=P)).then_inc(loaded, 16)
                sp.dma_start(wr[:], io["Wr"].rearrange("(k p) n -> p k n", p=P)).then_inc(loaded, 16)
                sp.dma_start(br[:], io["br"].unsqueeze(0).to_broadcast([P, NE])).then_inc(loaded, 16)
                out = img_d.rearrange("c (q j) (a b) -> j a c q b", j=4, a=AN)
                for hh in range(HH):
                    sp.wait_ge(bank_out, 4 * (hh + 1))
                    for j in range(4):
                        for a in range(AN):
                            row = AN * NB * j + NB * a
                            sp.dma_start(out[j, a][:, hh * 32:hh * 32 + 32, :], kt[row:row + NB, hh * 32:hh * 32 + 32, :]).then_inc(stored, 16)
                sp.wait_ge(stored, 16 * HH * 4 * AN)
                sp.wait_ge(loaded, LOADED)

            @block.gpsimd
            def _(pool):
                pool.memset(ident[:], 0.0).then_inc(id_ready, 1)
                pool.wait_ge(id_ready, 1)
                pool.affine_select(out=ident[:], in_=ident[:], compare_op=ALU.not_equal, fill=1.0, base=0,
                                   pattern=[[-1, P]], channel_multiplier=1).then_inc(id_ready, 1)

            @block.scalar
            def _(act):
                act.wait_ge(loaded_a, 64)
                act.activation(nat[0][:], inva[:].rearrange("p a n -> p (a n)"), ACT.Exp).then_inc(exp_done, 1)
                for stage, k in enumerate(SQUARE):
                    act.wait_ge(known, stage + 1)
                    b = slice(k // 2 + 1, k + 1)
                    act.activation(sq[:, 0, 0:k // 2], wre[:, b], ACT.Square)
                    act.activation(sq[:, 1, 0:k // 2], wim[:, b], ACT.Square).then_inc(sq_ready, 1)
                for q in range(4):
                    act.wait_ge(tr_c, q + 1)
                    act.activation(ct[:].rearrange("p c r h -> p (c r h)")[:, 512 * q:512 * q + 512], ps[:, 1 + q], ACT.Copy).then_inc(ct_ready, 1)
                for q in range(8):
                    act.wait_ge(bank_full, q + 1)
                    act.activation(kt[:, 8 * q:8 * q + 8, :], ps[:, q].rearrange("p (q b) -> p q b", b=BN), ACT.Copy).then_inc(bank_out, 1)

            @block.tensor
            def _(pe):
                pe.wait_ge(id_ready, 2)
                pe.wait_ge(loaded_c, 16 * NB)
                for q in range(4):
                    for k in range(4):
                        c, r = (4 * q + k) // 2, k % 2
                        last = pe.transpose(ps[:, 1 + q, P * k:P * k + P], cnat[:, c].rearrange("p a n r -> p (a n) r")[:, :, r], ident[:])
                    last.then_inc(tr_c, 1)
                pe.wait_ge(nat_ready, 1)
                b2v = b2[:].rearrange("p a n r -> p (a n) r")
                for k, src in enumerate((zre[:], zim[:], b2v[:, :, 0], b2v[:, :, 1])):
                    last = pe.transpose(ps[:, 0, P * k:P * k + P], src, ident[:])
                last.then_inc(tr_z, 1)
                for q in range(8):
                    if q < 4:
                        pe.wait_ge(g_ready, q + 1)
                    if q in (1, 2, 3, 4):
                        pe.wait_ge(ct_ready, q)
                    lo = NS * (q // 4)
                    for k in range(8):
                        for j in range(4):
                            h = 4 * (8 * (q % 4) + k) + j
                            for n, (g, w) in enumerate(((gre, wre), (gim, wim))):
                                last = pe.matmul(ps[GM * j:GM * j + GM, q, BN * k:BN * k + BN],
                                                 g[:].rearrange("p a c h -> p (a c) h")[lo:lo + NS, :, h],
                                                 w[lo:lo + NS, 0:BN, h], start=(n == 0), stop=(n == 1))
                    last.then_inc(bank_full, 1)

            @block.vector
            def _(v):
                t = Tally(v, dve)
                link, mark = t.link, t.mark
                v.wait_ge(loaded_a, 64)
                x, tk, kf, r, p, s = (e[:] for e in ex)
                link(v.tensor_scalar(x, logdt[:], 88.0, -87.0, ALU.min, ALU.max))
                link(v.tensor_scalar(tk, x, LOG2E, MAGIC, ALU.mult, ALU.add))
                link(v.tensor_scalar(kf, tk, MAGIC, None, ALU.subtract))
                link(v.scalar_tensor_tensor(out=r, in0=kf, scalar=-LN2HI, in1=x, op0=ALU.mult, op1=ALU.add))
                link(v.scalar_tensor_tensor(out=s, in0=kf, scalar=-LN2LO, in1=r, op0=ALU.mult, op1=ALU.add))
                link(v.tensor_scalar(p, s, 1 / math.factorial(7), None, ALU.mult))
                for n in range(6, 0, -1):
                    link(v.scalar_tensor_tensor(out=p, in0=p, scalar=1 / math.factorial(n), in1=s, op0=ALU.add, op1=ALU.mult))
                link(v.tensor_scalar(exi[:], kf, 127.0, None, ALU.add))
                link(v.tensor_scalar(exi[:], exi[:], 23, None, ALU.logical_shift_left))
                link(v.scalar_tensor_tensor(out=dt[:], in0=p, scalar=1.0, in1=exi[:].bitcast(F32), op0=ALU.add, op1=ALU.mult))
                e, a, w, d1, w2, num, rden, a2 = (n_[:] for n_ in nat)
                v.wait_ge(exp_done, 1)
                for hh in range(HH):
                    cols = slice(hh * NS, hh * NS + NS)
                    v.tensor_scalar(a[:, cols], e[:, cols], dt[:, hh:hh + 1], -0.5, ALU.mult, ALU.mult)
                    link(v.tensor_scalar(w[:, cols], aim[:, hh, :], dt[:, hh:hh + 1], 0.5, ALU.mult, ALU.mult))
                link(v.tensor_scalar(d1, a, -1.0, 1.0, ALU.mult, ALU.add))
                link(v.tensor_tensor(d1, d1, d1, ALU.mult))
                link(v.tensor_tensor(w2, w, w, ALU.mult))
                link(v.tensor_tensor(d1, d1, w2, ALU.add))
                link(v.reciprocal(rden, d1))
                link(v.tensor_tensor(a2, a, a, ALU.mult))
                link(v.tensor_tensor(a2, a2, w2, ALU.add))
                link(v.tensor_scalar(num, a2, -1.0, 1.0, ALU.mult, ALU.add))
                mark(v.tensor_tensor(zre[:], num, rden, ALU.mult))
                mark(v.scalar_tensor_tensor(out=zim[:], in0=w, scalar=2.0, in1=rden, op0=ALU.mult, op1=ALU.mult))
                v.tensor_scalar(b2[:], bri[:], 2.0, None, ALU.mult).then_inc(nat_ready, 1)
                mark(v.memset(wre[:, 0, :], 1.0))
                mark(v.memset(wim[:, 0, :], 0.0))
                mark(v.memset(ure[:, 0, :], 1.0))
                mark(v.memset(uim[:, 0, :], 0.0))
                v.wait_ge(tr_z, 1)
                mark(v.tensor_copy(wre[:, 1, :], ps[:, 0, 0:P]))
                mark(v.tensor_copy(wim[:, 1, :], ps[:, 0, P:2 * P]))
                link(v.tensor_copy(b2t[:], ps[:, 0, 2 * P:4 * P].rearrange("p (r h) -> p r h", r=2)))

                def cmul(ore, oim, ar, ai, br, bi):
                    n = ore.shape[1]
                    t1, t2, t3, t4 = (tm[k][:, 0:n] for k in range(4))
                    mark(v.tensor_tensor(t1, ar, br, ALU.mult))
                    mark(v.tensor_tensor(t2, ai, bi, ALU.mult))
                    mark(v.tensor_tensor(t3, ar, bi, ALU.mult))
                    link(v.tensor_tensor(t4, ai, br, ALU.mult))
                    mark(v.tensor_tensor(ore, t1, t2, ALU.subtract))
                    link(v.tensor_tensor(oim, t3, t4, ALU.add))

                def over(ap, n):
                    return ap.unsqueeze(1).to_broadcast([P, n, P])

                k = 1
                while k < SQUARE[0]:
                    cmul(wre[:, k + 1:2 * k + 1], wim[:, k + 1:2 * k + 1], wre[:, 1:k + 1], wim[:, 1:k + 1], over(wre[:, k], k), over(wim[:, k], k))
                    k *= 2
                for stage, k in enumerate(SQUARE):
                    v.nop().then_inc(known, 1)
                    odd, even = slice(k + 1, 2 * k, 2), slice(k + 2, 2 * k + 1, 2)
                    a, b = slice(k // 2, k), slice(k // 2 + 1, k + 1)
                    mark(v.scalar_tensor_tensor(out=wim[:, even], in0=wre[:, b], scalar=2.0, in1=wim[:, b], op0=ALU.mult, op1=ALU.mult))
                    cmul(wre[:, odd], wim[:, odd], wre[:, a], wim[:, a], wre[:, b], wim[:, b])
                    v.wait_ge(sq_ready, stage + 1)
                    link(v.tensor_tensor(wre[:, even], sq[:, 0, 0:k // 2], sq[:, 1, 0:k // 2], ALU.subtract))
                mark(v.tensor_copy(ure[:, 1, :], wre[:, BN, :]))
                link(v.tensor_copy(uim[:, 1, :], wim[:, BN, :]))
                for j in range(2, AN):
                    cmul(ure[:, j:j + 1], uim[:, j:j + 1], ure[:, j - 1:j], uim[:, j - 1:j], ure[:, 1:2], uim[:, 1:2])
                cmul(bare[:], baim[:], ure[:], uim[:], over(b2t[:, 0], AN), over(b2t[:, 1], AN))
                link(v.tensor_scalar(baim[:], baim[:], -1.0, None, ALU.mult))
                v.wait_ge(ct_ready, 4)
                for q in range(4):
                    heads = slice(P // 4 * q, P // 4 * (q + 1))
                    shape = [P, AN, NB, P // 4]
                    t1, t2, t3, t4 = (tm[k][:].rearrange("p s h -> p (s h)")[:, 0:AN * NB * P // 4].rearrange("p (a c h) -> p a c h", a=AN, c=NB) for k in range(4))
                    cr, ci = (ct[:, :, k, heads].unsqueeze(1).to_broadcast(shape) for k in range(2))
                    br, bi = (b[:, :, heads].unsqueeze(2).to_broadcast(shape) for b in (bare, baim))
                    mark(v.tensor_tensor(t1, br, cr, ALU.mult))
                    mark(v.tensor_tensor(t2, bi, ci, ALU.mult))
                    mark(v.tensor_tensor(t3, br, ci, ALU.mult))
                    link(v.tensor_tensor(t4, bi, cr, ALU.mult))
                    mark(v.tensor_tensor(gre[:, :, :, heads], t1, t2, ALU.add))
                    v.tensor_tensor(gim[:, :, :, heads], t4, t3, ALU.subtract).then_inc(g_ready, 1)
                    v.wait_ge(g_ready, q + 1)


def attention(nc, sem, io, ident, img_d, oT_d, wq, wk, wv, loaded):
    LAG = 3
    STEPS = GH * TT
    HALF = SEQ // 2
    CT = HALF // P
    GRP = 2 * CT
    NG = STEPS // GRP
    RING = 4
    HH = DH // 2
    HALVES = [(0, 0), (0, 1), (1, 0), (1, 1)]
    Q_USES = [(1 + 2 * n, "q", c, h) for n, (c, h) in enumerate(HALVES)]
    K_USES = [(9 + 2 * n, "k", c, h) for n, (c, h) in enumerate(HALVES)]
    N_USES = [(9 + 2 * n, "n", n, 0) for n in range(3)]
    V_USES = [(9 + 2 * n, "v", n, 0) for n in range(TT // 2)]
    USES = [Q_USES, Q_USES + N_USES, Q_USES + K_USES, Q_USES + V_USES]
    FIRST = N_USES + K_USES + Q_USES + V_USES
    PER_BATCH = sum(len(u) for u in USES)
    ROT_AT = {("q", 0): 4, ("q", 1): 9, ("k", 0): 14, ("k", 1): 19}
    PAIRS = [("q", 0), ("q", 1)]
    ROTS = [PAIRS, PAIRS, PAIRS + [("k", 0), ("k", 1)], PAIRS]
    FIRST_ROTS = [("k", 0), ("k", 1)] + PAIRS
    ROTS_BATCH = sum(len(u) for u in ROTS)
    LINKS = 10
    NORM_AT = 14
    NORMS = 2 * TT + 16
    VCOPY_AT = 22
    Q_MOVES, K_MOVES = 4 * GH, 8
    with ExitStack() as ctx:
        def sb(name, shape, dt=F32):
            return ctx.enter_context(nc.sbuf_tensor(name, shape, dt))

        table = sb("a_table", [P, 2, 2, SEQ])
        x, st, mv = sb("a_x", [P, TT, D]), sb("a_st", [P, TT, 6]), sb("a_mv", [P, TT, 2])
        ve, y, y2 = sb("a_ve", [P, TT]), sb("a_y", [P, TT]), sb("a_y2", [P, TT])
        xnow, xnext = sb("a_xnow", [P, KC, SEQ]), sb("a_xnext", [P, KC, SEQ])
        raw = sb("a_raw", [P, 2, 2, HALF])
        prod = sb("a_prod", [P, 4, HALF])
        qp, kp = sb("a_qp", [P, 2, 2, SEQ], F32R), sb("a_kp", [P, 2, 2, SEQ], F32R)
        qT = sb("a_qT", [P, 2, GH, SEQ], F32R)
        kT = sb("a_kT", [P, 2, 2, SEQ], F32R)
        vraw, val = sb("a_vraw", [P, TT, KV * DH]), sb("a_val", [P, 2, TT, DH])
        nmax, rsum, inv = sb("a_nmax", [P, RING]), sb("a_rsum", [P, RING]), sb("a_inv", [P, RING])
        prob = sb("a_prob", [P, RING, SEQ])
        probT = sb("a_probT", [P, 2, TT, 2, HALF])
        oT = sb("a_oT", [P, 2, HALF])
        S = ctx.enter_context(nc.psum_tensor("ps_s", [P, 2, 2, 512], F32))
        T = ctx.enter_context(nc.psum_tensor("ps_t", [P, 2, 512], F32))
        O = ctx.enter_context(nc.psum_tensor("ps_o", [P, 512], F32))
        X = ctx.enter_context(nc.psum_tensor("ps_x", [P, 512], F32))[:]

        table_in, xnow_in, x_in, norm_dve = sem("a_table_in"), sem("a_xnow_in"), sem("a_x_in"), sem("a_norm_dve")
        x_done, x_out, dve, v_ready = (sem(f"a_{n}") for n in ("x_done", "x_out", "dve", "v_ready"))
        q_in, k_in = ([sem(f"a_{n}_in{q}") for q in range(2)] for n in "qk")
        scores_ready, max_ready, exp_ready, inv_ready, norm_ready = (sem(f"a_{n}_ready") for n in ("scores", "max", "exp", "inv", "norm"))
        t_done, probT_ready, pv_done, o_out = sem("a_t_done"), sem("a_probT_ready"), sem("a_pv_done"), sem("a_o_out")
        o_stored = [sem(f"a_o_stored{q}") for q in range(2)]

        def wait(eng, s, value):
            if not isinstance(value, int) or value > 0:
                eng.wait_ge(s, value)

        def loop(eng, iteration, drain):
            for g in range(KV):
                iteration(0, g)
            with eng.Fori(1, NB - 1) as b:
                for g in range(KV):
                    iteration(b, g)
            for g in range(KV):
                iteration(NB - 1, g)
            if drain:
                drain()

        def first_bank(n):
            return [X, S[:, 0, 0], S[:, 0, 1], S[:, 1, 0]][n % 4]

        def use_no(b, g, n):
            before = g * len(Q_USES) if last_batch(b) else sum(len(u) for u in USES[:g])
            return b * PER_BATCH + (len(FIRST) + before + n)

        def rot_no(b, g, n):
            return b * ROTS_BATCH + (len(FIRST_ROTS) + sum(len(u) for u in ROTS[:g]) + n)

        def uses(b, g):
            if last_batch(b) and g == KV - 1:
                return []
            rows = USES[g][:len(Q_USES)] if last_batch(b) else USES[g]
            return [(use_no(b, g, n), s, job, c, h, rot_no(b, g, n // 2), n // 2 + sum(len(u) for u in ROTS[:g])) for n, (s, job, c, h) in enumerate(rows)]

        def rots(b, g):
            if last_batch(b) and g == KV - 1:
                return []
            rows = PAIRS if last_batch(b) else ROTS[g]
            return [(rot_no(b, g, n), n + sum(len(u) for u in ROTS[:g]), ROT_AT[job, c], job, c, use_no(b, g, 2 * n + 2)) for n, (job, c) in enumerate(rows)]

        def real(i, n):
            return n >= 0 or not (isinstance(i, int) and i == 0)

        last_batch = lambda b: isinstance(b, int) and b == NB - 1
        last_it = lambda i: isinstance(i, int) and i == NIT - 1

        def where(s):
            s %= STEPS
            return (s // GRP) % 2, (s % GRP) // 2, s % 2, s // GRP // 2

        with nc.Block() as block:
            @block.sync
            def _(sp):
                def load(b):
                    sp.dma_start(x[:, 0:IT, :], img_d[b].rearrange("(t p) d -> p t d", p=P)).then_inc(x_in, 16)
                    sp.dma_start(x[:, IT:TT, :], io["txt"][b].rearrange("(t p) d -> p t d", p=P)).then_inc(x_in, 16)

                load(0)
                sp.dma_start(table[:], io["rotary"]).then_inc(table_in, 16)
                sp.wait_ge(x_out, len(N_USES))
                sp.dma_start(xnow[:], xnext[:]).then_inc(xnow_in, 16)

                def move_k(par, g):
                    for w in range(2):
                        for x in range(2):
                            for h in range(2):
                                at = DH * (x ^ w) + HH * h
                                sp.dma_start(kT[at:at + HH, par, w, :].bitcast(F32), kp[HH * g:HH * g + HH, x, h, :].bitcast(F32)).then_inc(k_in[par], 16)

                def move_q(par, rot):
                    sp.wait_ge(dve, rot * LINKS + LINKS)
                    for x in range(2):
                        for h in range(2):
                            at = DH * x + HH * h
                            for j in range(GH):
                                sp.dma_start(qT[at:at + HH, par, j, :].bitcast(F32), qp[HH * j:HH * j + HH, x, h, :].bitcast(F32)).then_inc(q_in[par], 16)

                def iteration(b, g):
                    i, par = b * KV + g, g % 2
                    if last_batch(b) and g == KV - 1:
                        return
                    if g == 0 and not last_batch(b):
                        load(b + 1)
                    wait(sp, scores_ready, i * STEPS)
                    if g == KV - 1:
                        sp.wait_ge(dve, rot_no(b, g, 0) * LINKS)
                    move_k(1 - par, (g + 1) % KV)
                    if g == KV - 1:
                        sp.wait_ge(x_done, use_no(b, KV - 2, len(Q_USES)))
                        sp.dma_start(xnow[:], xnext[:]).then_inc(xnow_in, 16)
                    move_q(1 - par, rot_no(b, g, 1))

                sp.wait_ge(dve, 2 * LINKS)
                move_k(0, 0)
                move_q(0, len(FIRST_ROTS) - 1)
                loop(sp, iteration, None)

            @block.tensor
            def _(pe):
                def project(n, job, c, h, xn, g, X=X, ring=1):
                    wait(pe, x_out, n + 1 - ring)
                    if job == "n":
                        for m in range(4):
                            k, t = (4 * c + m) // TT, (4 * c + m) % TT
                            last = pe.transpose(X[:, P * m:P * m + P], x[:, t, P * k:P * k + P], ident[:])
                    elif job == "v":
                        for t in range(2):
                            tok = slice(P * (2 * c + t), P * (2 * c + t) + P)
                            for k in range(KC):
                                last = pe.matmul(X[:, KV * DH * t:KV * DH * (t + 1)], xn[:, k, tok], wv[:, k, :], start=(k == 0), stop=(k == KC - 1))
                    else:
                        for k in range(KC):
                            w = wq[:, k, h, P * g:P * g + P] if job == "q" else wk[:, k, h, :]
                            last = pe.matmul(X[:, 0:HALF], w, xn[:, k, HALF * c:HALF * c + HALF], start=(k == 0), stop=(k == KC - 1))
                    last.then_inc(x_done, 1)

                def scores(b, g, s):
                    i, par = b * KV + g, g % 2
                    hp, t, j, c = where(s)
                    if s == 0:
                        pe.wait_ge(k_in[par], (b * 2 + (g // 2 + 1)) * (K_MOVES * 16))
                        pe.wait_ge(q_in[par], (b * 2 + (g // 2 + 1)) * (Q_MOVES * 16))
                    wait(pe, exp_ready, i * STEPS + s - 1)
                    for r in range(2):
                        for w in range(2):
                            last = pe.matmul(S[:, s % 2, r, 0:HALF], qT[:, par, 2 * hp + j, HALF * c + P * t:HALF * c + P * t + P],
                                             kT[:, par, w, HALF * r:HALF * r + HALF], start=(w == 0), stop=(w == 1))
                    last.then_inc(scores_ready, 1)

                def turn_probs(i, s):
                    pe.wait_ge(norm_ready, i * STEPS + s + 1)
                    for half in range(2):
                        wait(pe, probT_ready, (i * STEPS + s) * 2 - 1 + half)
                        for n in range(CT):
                            kt = CT * half + n
                            last = pe.transpose(T[:, half, P * n:P * n + P], prob[:, s % RING, P * kt:P * kt + P], ident[:])
                        last.then_inc(t_done, 1)

                def values(i, par, g, kt):
                    if g == 0 and kt == 0:
                        pe.wait_ge(v_ready, i + 1)
                    if kt == 0:
                        pe.wait_ge(probT_ready, (i * NG + g) * 2 * GRP + 2 * GRP)
                        wait(pe, o_out, i * NG + g)
                    for j in range(2):
                        last = pe.matmul(O[DH * j:DH * j + DH, 0:HALF], val[:, (par + (g < 0)) % 2, kt, :], probT[:, g % 2, kt, j, :],
                                         start=(kt == 0), stop=(kt == TT - 1))
                    if kt == TT - 1:
                        last.then_inc(pv_done, 1)

                def back(i, par, s):
                    if real(i, s - LAG) and s - LAG < STEPS:
                        turn_probs(i, s - LAG)
                    g, kt = (s - LAG - GRP) // GRP, (s - LAG - GRP) % GRP
                    if real(i, g) and kt % 2 == 1:
                        values(i, par, g, kt - 1)
                        values(i, par, g, kt)

                def iteration(b, g):
                    i, par = b * KV + g, g % 2
                    now = {s: rest for rest in uses(b, g) for s in (rest[1],)}
                    for s in range(STEPS):
                        scores(b, g, s)
                        if s in now:
                            n, _, job, c, h, _, _ = now[s]
                            if (g, s) == (0, Q_USES[0][0]):
                                pe.wait_ge(xnow_in, b * 16 + 16)
                            if (job, c) == ("n", 0):
                                pe.wait_ge(norm_dve, b * NORMS + 2 * NORMS)
                            project(n, job, c, h, xnow if job == "q" and g < KV - 1 else xnext, (g + 1) % KV)
                        back(i, par, s)

                def drain():
                    for s in range(STEPS, STEPS + LAG + GRP):
                        back(NIT - 1, 1, s)

                pe.wait_ge(norm_dve, NORMS)
                pe.wait_ge(loaded, LOADED)
                for n, (_, job, c, h) in enumerate(FIRST):
                    if n == len(N_USES):
                        pe.wait_ge(x_out, n)
                    project(n, job, c, h, xnext, 0, first_bank(n), 4)
                pe.wait_ge(x_out, len(FIRST))
                loop(pe, iteration, drain)

            @block.scalar
            def _(act):
                def evacuate(n, job, c, h, rot, at, b, X=X):
                    act.wait_ge(x_done, n + 1)
                    if job == "n":
                        if c == 0:
                            wait(act, xnow_in, b * 16)
                        out = act.activation(xnext[:].rearrange("p c s -> p (c s)")[:, 4 * P * c:4 * P * (c + 1)], X, ACT.Copy)
                    elif job == "v":
                        if c == 0:
                            wait(act, v_ready, b * KV)
                        out = act.activation(vraw[:, 2 * c:2 * c + 2, :], X.rearrange("p (t d) -> p t d", t=2), ACT.Copy)
                    else:
                        if h == 0 and not (isinstance(rot, int) and rot < 2):
                            act.wait_ge(dve, (rot - 2) * LINKS + 4)
                        out = act.activation(raw[:, at % 2, h, :], X[:, 0:HALF], ACT.Copy)
                    out.then_inc(x_out, 1)

                def exps(i, s):
                    act.wait_ge(max_ready, i * STEPS + s + 1)
                    wait(act, t_done, (i * STEPS + s - RING + 1) * 2)
                    act.activation(prob[:, s % RING, :].rearrange("p (r k) -> p r k", r=2), S[:, s % 2, :, 0:HALF], ACT.Exp,
                                   bias=nmax[:, s % RING:s % RING + 1], scale=1.0,
                                   accum_out=rsum[:, s % RING:s % RING + 1]).then_inc(exp_ready, 1)

                def copy_probT(i, s):
                    hp, t, j, c = where(s)
                    g = s // GRP
                    if s % GRP == 0:
                        wait(act, pv_done, i * NG + g - 1)
                    for half in range(2):
                        act.wait_ge(t_done, (i * STEPS + s) * 2 + half + 1)
                        act.activation(probT[:, g % 2, CT * half:CT * half + CT, j, P * t:P * t + P],
                                       T[:, half, 0:HALF].rearrange("p (k q) -> p k q", k=CT), ACT.Copy).then_inc(probT_ready, 1)

                def copy_o(i, g):
                    act.wait_ge(pv_done, i * NG + g + 1)
                    wait(act, o_stored[g % 2], (i * (NG // 2) + g // 2) * 16)
                    act.activation(oT[:, g % 2, :], O[:, 0:HALF], ACT.Copy).then_inc(o_out, 1)

                def store_o(i, g):
                    act.wait_ge(o_out, i * NG + g + 1)
                    it, gg = (i, g) if g >= 0 else (i - 1, g + NG)
                    act.dma_start(oT_d[it][:, gg % 2, HALF * (gg // 2):HALF * (gg // 2) + HALF], oT[:, g % 2, :]).then_inc(o_stored[g % 2], 16)

                def result(i, s):
                    g, k = (s - LAG - 2 * GRP) // GRP, (s - LAG - 2 * GRP) % GRP
                    if k == 0 and real(i, g):
                        copy_o(i, g)

                def back(i, s):
                    g, k = (s - LAG - 2 * GRP) // GRP, (s - LAG - 2 * GRP) % GRP
                    n = s - LAG
                    if real(i, n) and n < STEPS:
                        copy_probT(i, n)
                    if k == 1 and real(i, g):
                        store_o(i, g)

                def iteration(b, g):
                    i = b * KV + g
                    now = {s: rest for rest in uses(b, g) for s in (rest[1],)}
                    for s in range(STEPS):
                        if real(i, s - 1):
                            exps(i, s - 1)
                        result(i, s)
                        if s in now:
                            n, _, job, c, h, rot, at = now[s]
                            evacuate(n, job, c, h, rot, at, b + 1)
                        back(i, s)

                def drain():
                    exps(NIT - 1, STEPS - 1)
                    for s in range(STEPS, STEPS + LAG + GRP + 2):
                        result(NIT - 1, s)
                        back(NIT - 1, s)
                    for q in range(2):
                        act.wait_ge(o_stored[q], NIT * NG // 2 * 16)

                for n, (_, job, c, h) in enumerate(FIRST):
                    rot = (n - len(N_USES)) // 2
                    evacuate(n, job, c, h, rot, rot, 0, first_bank(n))
                loop(act, iteration, drain)

            @block.gpsimd
            def _(pool):
                with pool.Fori(0, NIT * STEPS // RING) as k:
                    for s in range(RING):
                        hold(pool, inv_ready, k * RING + s + 1)
                        pool.tensor_scalar(prob[:, s, :], prob[:, s, :], inv[:, s:s + 1], 1.0, ALU.mult, ALU.mult).then_inc(norm_ready, 1)

            @block.vector
            def _(v):
                def rotate(rot, at, job, c, part, made, free):
                    k = Tally(v, dve, rot * LINKS)
                    k.n = 2 * part
                    tok = slice(HALF * c, HALF * c + HALF)
                    lower, upper = raw[:, at % 2, 0, :], raw[:, at % 2, 1, :]
                    cos, sin = table[:, "qk".index(job), 0, tok], table[:, "qk".index(job), 1, tok]
                    parts = qp if job == "q" else kp
                    out = [prod[:, 0, :], prod[:, 2, :]]
                    if part == 0:
                        wait(v, dve, k.base)
                        v.wait_ge(x_out, made)
                        k.mark(v.tensor_tensor(prod[:, 0, :], lower, cos, ALU.mult))
                        k.mark(v.tensor_tensor(prod[:, 1, :], upper, sin, ALU.mult))
                        return
                    if part == 1:
                        k.mark(v.tensor_tensor(prod[:, 2, :], upper, cos, ALU.mult))
                        k.mark(v.tensor_tensor(prod[:, 3, :], lower, sin, ALU.mult))
                        return
                    v.wait_ge(dve, k.base + k.n)
                    if part == 2:
                        k.mark(v.tensor_tensor(out[0], prod[:, 0, :], prod[:, 1, :], ALU.subtract))
                        k.mark(v.tensor_tensor(out[1], prod[:, 2, :], prod[:, 3, :], ALU.add))
                    if part == 3:
                        if free:
                            v.wait_ge(*free)
                        for h in range(2):
                            k.mark(v.tensor_copy(parts[:, 0, h, tok], out[h]))
                    if part == 4:
                        for h in range(2):
                            k.mark(v.tensor_tensor(parts[:, 1, h, tok], out[h], parts[:, 0, h, tok].bitcast(F32), ALU.subtract))

                def norm(n, part):
                    k = Tally(v, norm_dve, n * NORMS)
                    k.n = (0, TT // 2, TT, 2 * TT + 1, NORMS - 1, NORMS - 1)[part]
                    link = k.link
                    half = range(TT // 2 * (part % 2), TT // 2 * (part % 2 + 1))
                    if part == 0:
                        hold(v, x_in, n * 32 + 32)
                    if part < 2:
                        for t in half:
                            k.mark(v.bn_stats(st[:, t, :], x[:, t, :]))
                    elif part == 2:
                        hold(v, norm_dve, k.base + k.n)
                        for t in range(TT):
                            k.mark(v.bn_aggr(mv[:, t, :], st[:, t, :]))
                        v.wait_ge(norm_dve, k.base + k.n)
                        link(v.tensor_scalar(ve[:], mv[:, :, 1], EPS, None, ALU.add))
                    elif part == 3:
                        link(v.tensor_scalar(y[:].bitcast(I32), ve[:].bitcast(I32), 1, None, ALU.arith_shift_right))
                        link(v.tensor_scalar(y[:].bitcast(I32), y[:].bitcast(I32), -1.0, float(0x5f3759df), ALU.mult, ALU.add))
                        for _ in range(3):
                            link(v.tensor_tensor(y2[:], y[:], y[:], ALU.mult))
                            link(v.tensor_tensor(y2[:], y2[:], ve[:], ALU.mult))
                            link(v.tensor_scalar(y2[:], y2[:], -0.5, 1.5, ALU.mult, ALU.add))
                            link(v.tensor_tensor(y[:], y[:], y2[:], ALU.mult))
                        assert k.n == NORMS - 1, k.n
                    else:
                        for t in half:
                            last = v.tensor_scalar(x[:, t, :], x[:, t, :], mv[:, t, 0:1], y[:, t:t + 1], ALU.subtract, ALU.mult)
                        if part == 5:
                            k.mark(last)

                def copy_v(n, par, g):
                    wait(v, pv_done, (n - 1) * NG)
                    v.tensor_copy(val[:, par], vraw[:, :, DH * g:DH * g + DH]).then_inc(v_ready, 1)

                def maxima(i, s):
                    v.wait_ge(scores_ready, i * STEPS + s + 1)
                    v.tensor_reduce(nmax[:, s % RING:s % RING + 1], S[:, s % 2, :, 0:HALF], AX.XY, ALU.max, negate=True).then_inc(max_ready, 1)

                def invert(i, s):
                    v.wait_ge(exp_ready, i * STEPS + s + 1)
                    v.reciprocal(inv[:, s % RING:s % RING + 1], rsum[:, s % RING:s % RING + 1]).then_inc(inv_ready, 1)

                def iteration(b, g):
                    i, par = b * KV + g, g % 2
                    moved = {"q": (q_in[par], (b * 2 + (g // 2 + 1)) * (Q_MOVES * 16)), "k": (k_in[1], (b * 2 + 2) * (K_MOVES * 16))}
                    for s in range(STEPS):
                        maxima(i, s)
                        if real(i, s - 1):
                            invert(i, s - 1)
                        for rot, at, first, job, c, made in rots(b, g):
                            if first <= s < first + 5:
                                rotate(rot, at, job, c, s - first, made, moved[job] if c == 0 else None)
                        if g == 0 and not last_batch(b) and NORM_AT <= s < NORM_AT + 6:
                            norm(b + 1, s - NORM_AT)
                        if s == VCOPY_AT and not last_it(i):
                            if g == KV - 1:
                                v.wait_ge(x_out, use_no(b + 1, 0, 0))
                            copy_v(i + 1, 1 - par, (g + 1) % KV)

                for part in range(6):
                    norm(0, part)
                v.wait_ge(table_in, 16)
                for rot, (job, c) in enumerate(FIRST_ROTS):
                    for part in range(5):
                        rotate(rot, rot, job, c, part, len(N_USES) + 2 * rot + 2, None)
                v.wait_ge(x_out, len(FIRST))
                copy_v(0, 0, 0)
                loop(v, iteration, lambda: invert(NIT - 1, STEPS - 1))


def route(nc, sem, io, ident, img_d, oT_d, xs_d, h1, pos, gate, run, base, exp_i, src_i, tail_i, move, wo, wr, br, weights, weights_in):
    w1, w2, b1, b2 = weights
    with ExitStack() as ctx:
        def sb(name, shape, dt=F32):
            return ctx.enter_context(nc.sbuf_tensor(name, shape, dt))

        below, ones = sb("r_below", [P, P]), sb("r_ones", [P, P])
        eight = sb("r_eight", [P, NE])
        oT = sb("r_oT", [P, 3, KV, 2, P])
        st, mv = sb("r_st", [P, TT, 6]), sb("r_mv", [P, TT, 2])
        ve, sd, y, y2, rstd = (sb(f"r_s{n}", [P, TT]) for n in range(5))
        xn = sb("r_xn", [P, 2, TT, D])
        xT = sb("r_xT", [P, KC, SEQ])
        lg, m8, i8 = sb("r_lg", [P, TT, NE]), sb("r_m8", [P, TT, 8]), sb("r_i8", [P, TT, 8], U32)
        top = sb("r_top", [P, TT, TOPK])
        hot = sb("r_hot", [P, TOPK, TT, NE])
        mask, off, slot = sb("r_mask", [P, TT, NE]), sb("r_off", [P, TT, NE]), sb("r_slot", [P, TT, NE])
        pick = sb("r_pick", [P, TOPK, TT, NE])
        posf = sb("r_posf", [P, TOPK, TT])
        idx = sb("r_idx", [P, 2, TOPK, TT], U32)
        gr = sb("r_gr", [P, TT])
        tile_no, zeros = sb("r_tile_no", [P, NT]), sb("r_zeros", [P, D])
        dl, ex, den = (sb(f"r_g{n}", [P, TT]) for n in range(3))
        A = ctx.enter_context(nc.psum_tensor("ps_ra", [P, 3, 512], F32))
        XT = ctx.enter_context(nc.psum_tensor("ps_rx", [P, 3, 512], F32))
        L = ctx.enter_context(nc.psum_tensor("ps_rl", [P, 512], F32))
        C = ctx.enter_context(nc.psum_tensor("ps_rc", [P, 2, TT, NE], F32))

        const = sem("r_const")
        h_in = [sem(f"r_h_in{q}") for q in range(2)]
        oT_in = [sem(f"r_oT_in{q}") for q in range(3)]
        oT_free, h1_ready, var_ready, sd_ready, xn_ready = (sem(f"r_{n}") for n in ("oT_free", "h1_ready", "var_ready", "sd_ready", "xn_ready"))
        rstd_ready, run_ready, xn_free = sem("r_rstd_ready"), sem("r_run_ready"), sem("r_xn_free")
        tr_done, xT_ready, lg_done = sem("r_tr_done"), sem("r_xT_ready"), sem("r_lg_done")
        mask_ready, count_done, gap_ready, ex_ready, idx_ready = (sem(f"r_{n}") for n in ("mask_ready", "count_done", "gap_ready", "ex_ready", "idx_ready"))
        table_dve, table_ready, zeroed = (sem(f"r_{n}") for n in ("table_dve", "table_ready", "zeroed"))
        norm_dve, pick_dve, place_dve = sem("r_norm_dve"), sem("r_pick_dve"), sem("r_place_dve")
        scattered = [sem(f"r_scattered{q}") for q in range(2)]
        TURN_AT, LOGITS_AT = 2, 3
        NORM, PICK, PLACE = 2 * TT + 4, 2 * TT + 4, TT + 8

        def loop(iteration, drain, eng):
            iteration(0, 0)
            with eng.Fori(0, (NB - 2) // 2) as k:
                iteration(k * 2 + 1, 1)
                iteration(k * 2 + 2, 0)
            iteration(NB - 1, 1)
            drain()

        first = lambda b: isinstance(b, int) and b == 0

        with nc.Block() as block:
            @block.sync
            def _(sp):
                oT_b = oT_d.rearrange("(b g) p h s -> b p g h s", g=KV)
                sp.nop().then_inc(oT_free, 3)

                def load(b):
                    for t in range(TT):
                        sp.wait_ge(oT_free, b * TT + t + 1)
                        for g in range(KV):
                            sp.dma_start(oT[:, t % 3, g], oT_b[b][:, g, :, P * t:P * t + P]).then_inc(oT_in[t % 3], 16)

                assert NE == NB
                with sp.Fori(0, NB) as b:
                    load(b)
                    sp.dma_start(w1[:, b], io["W1"][b].rearrange("(c p) f -> p c f", p=P)).then_inc(weights_in, 16)
                    sp.dma_start(b1[:, b], io["b1"][b].unsqueeze(0).to_broadcast([P, FF])).then_inc(weights_in, 16)
                    sp.dma_start(w2[:, b], io["W2"][b].rearrange("(c p) f -> p c f", p=P)).then_inc(weights_in, 16)
                    sp.dma_start(b2[:, b], io["b2"][b].unsqueeze(0).to_broadcast([P, D])).then_inc(weights_in, 16)
                sp.wait_ge(weights_in, 4 * NE * 16)
                sp.wait_ge(table_ready, 1)
                for x in range(NE):
                    row = sp.value_load(tail_i[0:1, x:x + 1], min_val=x * STRIDE, max_val=x * STRIDE + TOK)
                    sp.dma_start(xs_d[bass.ds(row, P), :], zeros[:]).then_inc(zeroed, 16)
                sp.wait_ge(zeroed, 16 * NE)
                for q in range(2):
                    sp.wait_ge(scattered[q], NB // 2 * TT * TOPK * 16)

            @block.gpsimd
            def _(pool):
                pool.memset(ones[:], 1.0).then_inc(const, 1)
                pool.wait_ge(const, 1)
                pool.affine_select(out=below[:], in_=ones[:], compare_op=ALU.is_gt, fill=0.0, base=0,
                                   pattern=[[1, P]], channel_multiplier=-1).then_inc(const, 1)
                pool.iota(eight[:], [[1, NE]], base=0, channel_multiplier=0, allow_small_or_imprecise_dtypes=True).then_inc(const, 1)
                pool.iota(base[:], [[STRIDE, NE]], base=0, channel_multiplier=0, allow_small_or_imprecise_dtypes=True).then_inc(const, 1)
                pool.iota(tile_no[:], [[1, NT]], base=0, channel_multiplier=0, allow_small_or_imprecise_dtypes=True).then_inc(const, 1)
                pool.memset(zeros[:], 0.0).then_inc(const, 1)
                pool.nop().then_inc(xn_free, 2)
                with pool.Fori(0, NB // 2) as k:
                    for q in range(2):
                        hold(pool, idx_ready, k * 2 + q + 2)
                        for t in range(TT):
                            for e in range(TOPK):
                                pool.indirect_dma_start(out=xs_d, out_offset=bass.IndirectOffsetOnAxis(ap=idx[:, q, e, t:t + 1], axis=0),
                                                        in_=xn[:, q, t, :], in_offset=None).then_inc(scattered[q], 16)
                        pool.wait_ge(scattered[q], k * (TT * TOPK * 16) + TT * TOPK * 16)
                        pool.nop().then_inc(xn_free, 1)

            @block.tensor
            def _(pe):
                def project(b, t):
                    pe.wait_ge(oT_in[t % 3], b * (TT // 3 * KV * 16) + (t // 3 + 1) * KV * 16)
                    pe.wait_ge(h1_ready, b * TT + t + 1)
                    for c in range(KV * 2):
                        last = pe.matmul(A[:, t % 3, 0:D], oT[:, t % 3, c // 2, c % 2, :], wo[:, c, :], start=(c == 0), stop=(c == KV * 2 - 1))
                    last.then_inc(oT_free, 1)

                def turn(b, q):
                    pe.wait_ge(xn_ready, b + 1)
                    for n in range(3):
                        for m in range(4):
                            c, t = (4 * n + m) // TT, (4 * n + m) % TT
                            last = pe.transpose(XT[:, n, P * m:P * m + P], xn[:, q, t, P * c:P * c + P], ident[:])
                        last.then_inc(tr_done, 1)

                def logits(b):
                    pe.wait_ge(xT_ready, b * 3 + 3)
                    pe.wait_ge(mask_ready, b + 1)
                    for t in range(TT):
                        for c in range(KC):
                            last = pe.matmul(L[:, NE * t:NE * t + NE], xT[:, c, P * t:P * t + P], wr[:, c, :], start=(c == 0), stop=(c == KC - 1))
                    last.then_inc(lg_done, 1)

                def counts(b):
                    pe.wait_ge(mask_ready, b + 2)
                    pe.wait_ge(idx_ready, b + 1)
                    m = mask[:].rearrange("p t e -> p (t e)")
                    pe.matmul(C[:, 0].rearrange("p t e -> p (t e)"), below[:], m, start=True, stop=True)
                    pe.matmul(C[:, 1].rearrange("p t e -> p (t e)"), ones[:], m, start=True, stop=True).then_inc(count_done, 1)

                def iteration(b, q):
                    for t in range(TT):
                        project(b, t)
                        if not first(b) and t == TURN_AT:
                            turn(b - 1, 1 - q)
                        if not first(b) and t == LOGITS_AT:
                            logits(b - 1)
                    if not first(b):
                        counts(b - 1)

                def drain():
                    turn(NB - 1, 1)
                    logits(NB - 1)
                    counts(NB - 1)

                pe.wait_ge(const, 4)
                loop(iteration, drain, pe)

            @block.scalar
            def _(act):
                def root(b):
                    act.wait_ge(var_ready, b + 1)
                    act.activation(sd[:], ve[:], ACT.Sqrt).then_inc(sd_ready, 1)

                def turned(b):
                    for n in range(3):
                        act.wait_ge(tr_done, b * 3 + n + 1)
                        act.activation(xT[:].rearrange("p c s -> p (c s)")[:, 512 * n:512 * n + 512], XT[:, n], ACT.Copy).then_inc(xT_ready, 1)

                def exp_gap(b):
                    act.wait_ge(gap_ready, b + 1)
                    act.activation(ex[:], dl[:], ACT.Exp).then_inc(ex_ready, 1)

                def load(b, q):
                    act.dma_start(h1[:, b, 0:IT, :], img_d[b].rearrange("(t p) d -> p t d", p=P)).then_inc(h_in[q], 16)
                    act.dma_start(h1[:, b, IT:TT, :], io["txt"][b].rearrange("(t p) d -> p t d", p=P)).then_inc(h_in[q], 16)

                def iteration(b, q):
                    if not first(b):
                        turned(b - 1)
                        if not isinstance(b, int):
                            load(b + 1, 1 - q)
                        exp_gap(b - 1)
                    root(b)

                load(0, 0)
                load(1, 1)

                def drain():
                    turned(NB - 1)
                    exp_gap(NB - 1)

                loop(iteration, drain, act)

            @block.vector
            def _(v):
                def add(b, q, t):
                    if t == 0:
                        v.wait_ge(h_in[q], (b >> 1) * 32 + 32)
                    if t < TT:
                        v.wait_ge(oT_free, b * TT + t + 4)
                        v.tensor_tensor(h1[:, b, t, :], A[:, t % 3, 0:D], h1[:, b, t, :], ALU.add).then_inc(h1_ready, 1)
                    if t > 0:
                        hold(v, h1_ready, b * TT + t + 3)
                        v.bn_stats(st[:, t - 1, :], h1[:, b, t - 1, :]).then_inc(norm_dve, 1)

                def norm(b, q):
                    k = Tally(v, norm_dve, b * NORM)
                    k.n = TT
                    hold(v, norm_dve, k.base + k.n)
                    for t in range(TT):
                        k.mark(v.bn_aggr(mv[:, t, :], st[:, t, :]))
                    v.wait_ge(norm_dve, k.base + k.n)
                    v.tensor_scalar(ve[:], mv[:, :, 1], EPS, None, ALU.add).then_inc(var_ready, 1)
                    v.wait_ge(sd_ready, b + 1)
                    k.link(v.reciprocal(y[:], sd[:]))
                    k.link(v.tensor_tensor(y2[:], y[:], y[:], ALU.mult))
                    k.link(v.tensor_tensor(y2[:], y2[:], ve[:], ALU.mult))
                    k.link(v.tensor_scalar(y2[:], y2[:], -0.5, 1.5, ALU.mult, ALU.add))
                    assert k.n == NORM
                    v.tensor_tensor(rstd[:], y[:], y2[:], ALU.mult).then_inc(rstd_ready, 1)
                    v.wait_ge(rstd_ready, b + 1)
                    v.wait_ge(xn_free, b + 1)
                    for t in range(TT):
                        last = v.tensor_scalar(xn[:, q, t, :], h1[:, b, t, :], mv[:, t, 0:1], rstd[:, t:t + 1], ALU.subtract, ALU.mult)
                    last.then_inc(xn_ready, 1)

                def choose(b):
                    k = Tally(v, pick_dve, b * PICK)
                    v.wait_ge(lg_done, b + 1)
                    k.mark(v.tensor_tensor(lg[:], L[:, 0:TT * NE].rearrange("p (t e) -> p t e", e=NE), br[:].unsqueeze(1).to_broadcast([P, TT, NE]), ALU.add))
                    hold(v, pick_dve, k.base + k.n)
                    for t in range(TT):
                        k.mark(v.max(m8[:, t, :], lg[:, t, :]))
                    hold(v, pick_dve, k.base + k.n)
                    for t in range(TT):
                        k.mark(v.max_index(i8[:, t, :], m8[:, t, :], lg[:, t, :]))
                    v.wait_ge(pick_dve, k.base + k.n)
                    k.link(v.tensor_copy(top[:], i8[:, :, 0:TOPK]))
                    for e in range(TOPK):
                        k.mark(v.tensor_tensor(hot[:, e], eight[:].unsqueeze(1).to_broadcast([P, TT, NE]),
                                               top[:, :, e:e + 1].to_broadcast([P, TT, NE]), ALU.is_equal))
                    v.wait_ge(pick_dve, k.base + k.n)
                    assert k.n == PICK
                    v.tensor_tensor(mask[:], hot[:, 0], hot[:, 1], ALU.add).then_inc(mask_ready, 1)
                    v.tensor_tensor(dl[:], m8[:, :, 1], m8[:, :, 0], ALU.subtract).then_inc(gap_ready, 1)

                def place(b, q):
                    k = Tally(v, place_dve, b * PLACE)
                    v.wait_ge(ex_ready, b + 1)
                    k.link(v.tensor_scalar(den[:], ex[:], 1.0, None, ALU.add))
                    k.link(v.reciprocal(gr[:], den[:]))
                    v.tensor_copy(gate[:, b, 0, :], gr[:])
                    v.tensor_tensor(gate[:, b, 1, :], ex[:], gr[:], ALU.mult)
                    v.wait_ge(count_done, b + 1)
                    k.link(v.tensor_copy(off[:, 0, :], run[:]))
                    for t in range(TT):
                        out = off[:, t + 1, :] if t < TT - 1 else run[:]
                        k.link(v.tensor_tensor(out, off[:, t, :], C[:, 1, t, :], ALU.add))
                    k.link(v.tensor_tensor(slot[:], off[:], C[:, 0], ALU.add))
                    for e in range(TOPK):
                        k.mark(v.tensor_tensor(pick[:, e], hot[:, e], slot[:], ALU.mult))
                    v.wait_ge(place_dve, k.base + k.n)
                    k.mark(v.tensor_reduce(posf[:], pick[:], AX.X, ALU.add))
                    v.wait_ge(place_dve, k.base + k.n)
                    k.mark(v.tensor_copy(pos[:, b, :, :], posf[:]))
                    assert k.n == PLACE, k.n
                    v.tensor_copy(idx[:, q], posf[:]).then_inc(idx_ready, 1)

                def iteration(b, q):
                    for t in range(TT + 1):
                        add(b, q, t)
                        if not first(b) and t == LOGITS_AT:
                            choose(b - 1)
                    norm(b, q)
                    if not first(b):
                        place(b - 1, 1 - q)

                def drain():
                    choose(NB - 1)
                    place(NB - 1, 1)
                    tile_table(v, sb, table_dve, run, base, tile_no, exp_i, src_i, tail_i, move).then_inc(table_ready, 1)

                v.nop().then_inc(h1_ready, 3)
                v.nop().then_inc(mask_ready, 1)
                v.nop().then_inc(idx_ready, 1)
                v.wait_ge(const, 6)
                v.tensor_copy(run[:], base[:]).then_inc(run_ready, 1)
                v.wait_ge(run_ready, 1)
                loop(iteration, drain, v)


def tile_table(v, sb, dve, run, base, j, exp_i, src_i, tail_i, move):
    n, cnt, end = sb("t_n", [P, NE]), sb("t_cnt", [P, NE]), sb("t_end", [P, NE])
    ni = sb("t_ni", [P, NE], I32)
    last = sb("t_last", [P, 1])
    jr, e, start, ind = (sb(f"t_{x}", [P, NT]) for x in ("jr", "e", "start", "ind"))
    k = Tally(v, dve)
    link, mark = k.link, k.mark
    mark(v.tensor_copy(tail_i[:], run[:]))
    mark(v.memset(e[:], 0.0))
    mark(v.memset(start[:], 0.0))
    link(v.tensor_tensor(n[:], run[:], base[:], ALU.subtract))
    link(v.tensor_scalar(ni[:], n[:], float(P - 1), None, ALU.add))
    link(v.tensor_scalar(ni[:], ni[:], 7, None, ALU.arith_shift_right))
    link(v.tensor_copy(cnt[:], ni[:]))
    mark(v.tensor_scalar(move[:], cnt[:], float(P), -float(STRIDE), ALU.mult, ALU.add))
    link(v.tensor_copy(end[:, 0:1], cnt[:, 0:1]))
    for x in range(1, NE):
        link(v.tensor_tensor(end[:, x:x + 1], end[:, x - 1:x], cnt[:, x:x + 1], ALU.add))
    link(v.tensor_scalar(last[:], end[:, NE - 1:NE], -1.0, None, ALU.add))
    link(v.tensor_scalar(jr[:], j[:], last[:], None, ALU.min))
    for x in range(NE - 1):
        link(v.tensor_scalar(ind[:], jr[:], end[:, x:x + 1], None, ALU.is_ge))
        mark(v.tensor_tensor(e[:], e[:], ind[:], ALU.add))
        link(v.scalar_tensor_tensor(out=start[:], in0=ind[:], scalar=cnt[:, x:x + 1], in1=start[:], op0=ALU.mult, op1=ALU.add))
    link(v.tensor_tensor(start[:], jr[:], start[:], ALU.subtract))
    link(v.tensor_scalar(start[:], start[:], float(P), None, ALU.mult))
    mark(v.tensor_copy(exp_i[:], e[:]))
    return v.scalar_tensor_tensor(out=src_i[:], in0=e[:], scalar=float(STRIDE), in1=start[:], op0=ALU.mult, op1=ALU.add)


def experts(nc, sem, ident, xs_d, ys_d, exp_i, src_i, pos, move, weights):
    RING = 4
    w1, w2, b1, b2 = weights
    with ExitStack() as ctx:
        def sb(name, shape, dt=F32):
            return ctx.enter_context(nc.sbuf_tensor(name, shape, dt))

        x, xT = sb("e_x", [P, RING, D]), sb("e_xT", [P, 2, D])
        h, hT, y = sb("e_h", [P, 2, FF]), sb("e_hT", [P, 2, FF]), sb("e_y", [P, RING, D])
        X = ctx.enter_context(nc.psum_tensor("ps_ex", [P, 2, 512], F32))
        H = ctx.enter_context(nc.psum_tensor("ps_eh", [P, 2, 512], F32))
        HT = ctx.enter_context(nc.psum_tensor("ps_et", [P, 2, 512], F32))
        Y = ctx.enter_context(nc.psum_tensor("ps_ey", [P, 2, 512], F32))
        x_in = [sem(f"e_x_in{q}") for q in range(RING)]
        xt_done, xT_ready, h_done, h_ready, ht_done, hT_ready, y_done, y_ready = (
            sem(f"e_{n}") for n in ("xt_done", "xT_ready", "h_done", "h_ready", "ht_done", "hT_ready", "y_done", "y_ready"))
        stored = [sem(f"e_stored{q}") for q in range(RING)]

        def wait(eng, s, value):
            if not isinstance(value, int) or value > 0:
                eng.wait_ge(s, value)

        where, moved, past = (sb(f"e_{x}", [P, NB * TOPK * TT]) for x in ("where", "moved", "past"))
        pos_dve = sem("e_pos_dve")

        def loop(eng, tile, between=None):
            for n in range(RING):
                tile(n, n)
            if between:
                between()
            with eng.Fori(1, NT // RING - 1) as k:
                for n in range(RING):
                    tile(k * RING + n, n)
            for n in range(RING):
                tile(NT - RING + n, n)

        def more(j, ahead):
            return not (isinstance(j, int) and j + ahead >= NT)

        def at(table, j):
            return table[0:1, bass.ds(j, 1)]

        with nc.Block() as block:
            @block.sync
            def _(sp):
                def load(j, n):
                    row = sp.value_load(at(src_i, j), min_val=0, max_val=SLOTS - P)
                    sp.dma_start(x[:, n, :], xs_d[bass.ds(row, P), :]).then_inc(x_in[n], 16)
                for n in range(RING):
                    load(n, n)

                def tile(j, n):
                    if more(j, RING):
                        sp.wait_ge(xt_done, j + 1)
                        load(j + RING, n)

                loop(sp, tile)

            @block.tensor
            def _(pe):
                def turn_x(j, n):
                    q = n % 2
                    pe.wait_ge(x_in[n], (j >> 2) * 16 + 16)
                    wait(pe, xT_ready, j - 1)
                    for c in range(KC):
                        last = pe.transpose(X[:, q, P * c:P * c + P], x[:, n, P * c:P * c + P], ident[:])
                    last.then_inc(xt_done, 1)

                def up(j, q, ex):
                    pe.wait_ge(xT_ready, j + 1)
                    wait(pe, h_ready, j - 1)
                    for c in range(KC):
                        last = pe.matmul(H[:, q, :], xT[:, q, P * c:P * c + P], w1[:, bass.ds(ex, 1), c, :], start=(c == 0), stop=(c == KC - 1))
                    last.then_inc(h_done, 1)

                def turn_h(j, q):
                    pe.wait_ge(h_ready, j + 1)
                    wait(pe, hT_ready, j - 1)
                    for c in range(FC):
                        last = pe.transpose(HT[:, q, P * c:P * c + P], h[:, q, P * c:P * c + P], ident[:])
                    last.then_inc(ht_done, 1)

                def down(j, q, ex):
                    pe.wait_ge(hT_ready, j + 1)
                    wait(pe, y_ready, j - 1)
                    for c in range(FC):
                        last = pe.matmul(Y[:, q, 0:D], hT[:, q, P * c:P * c + P], w2[:, bass.ds(ex, 1), c, :], start=(c == 0), stop=(c == FC - 1))
                    last.then_inc(y_done, 1)

                def expert(j):
                    return pe.value_load(at(exp_i, j), min_val=0, max_val=NE - 1)

                def tile(j, n):
                    q = n % 2
                    if more(j, 1):
                        turn_x(j + 1, (n + 1) % RING)
                    up(j, q, expert(j))
                    if not (isinstance(j, int) and j == 0):
                        down(j - 1, 1 - q, expert(j - 1))
                    turn_h(j, q)

                turn_x(0, 0)
                loop(pe, tile)
                down(NT - 1, 1, expert(NT - 1))

            @block.scalar
            def _(act):
                def copy_x(j, q):
                    act.wait_ge(xt_done, j + 1)
                    wait(act, h_done, j - 1)
                    act.activation(xT[:, q, :], X[:, q, 0:D], ACT.Copy).then_inc(xT_ready, 1)

                def relu_h(j, q):
                    act.wait_ge(ht_done, j + 1)
                    wait(act, y_done, j - 1)
                    act.activation(hT[:, q, :], HT[:, q, :], ACT.Relu).then_inc(hT_ready, 1)

                def store(j, n):
                    act.wait_ge(y_ready, j + 1)
                    act.dma_start(ys_d[j], y[:, n, :]).then_inc(stored[n], 16)

                def tile(j, n):
                    q = n % 2
                    if more(j, 1):
                        copy_x(j + 1, 1 - q)
                    relu_h(j, q)
                    if not (isinstance(j, int) and j < 2):
                        store(j - 2, (n - 2) % RING)

                copy_x(0, 0)
                loop(act, tile)
                for n in (2, 3):
                    store(NT - RING + n, n)
                for n in range(RING):
                    act.wait_ge(stored[n], NT // RING * 16)

            @block.vector
            def _(v):
                def bias_h(j, q):
                    ex = v.value_load(at(exp_i, j), min_val=0, max_val=NE - 1)
                    v.wait_ge(h_done, j + 1)
                    wait(v, ht_done, j - 1)
                    v.tensor_tensor(h[:, q, :], H[:, q, :], b1[:, bass.ds(ex, 1), :].rearrange("p o f -> p (o f)"), ALU.add).then_inc(h_ready, 1)

                def bias_y(j, n):
                    q = n % 2
                    ex = v.value_load(at(exp_i, j), min_val=0, max_val=NE - 1)
                    v.wait_ge(y_done, j + 1)
                    wait(v, stored[n], (j >> 2) * 16)
                    v.tensor_tensor(y[:, n, :], Y[:, q, 0:D], b2[:, bass.ds(ex, 1), :].rearrange("p o f -> p (o f)"), ALU.add).then_inc(y_ready, 1)

                def tile(j, n):
                    bias_h(j, n % 2)
                    if not (isinstance(j, int) and j == 0):
                        bias_y(j - 1, (n - 1) % RING)

                def renumber():
                    k = Tally(v, pos_dve)
                    k.link(v.tensor_copy(where[:], pos[:].rearrange("p b k t -> p (b k t)")))
                    k.link(v.tensor_copy(moved[:], where[:]))
                    for x in range(NE - 1):
                        k.link(v.tensor_scalar(past[:], where[:], float((x + 1) * STRIDE), None, ALU.is_ge))
                        k.link(v.scalar_tensor_tensor(out=moved[:], in0=past[:], scalar=move[:, x:x + 1], in1=moved[:], op0=ALU.mult, op1=ALU.add))
                    k.link(v.tensor_copy(pos[:].rearrange("p b k t -> p (b k t)"), moved[:]))

                loop(v, tile, renumber)
                bias_y(NT - 1, RING - 1)


def combine(nc, sem, ys_d, h1, pos, gate, out):
    with ExitStack() as ctx:
        def sb(name, shape, dt=F32):
            return ctx.enter_context(nc.sbuf_tensor(name, shape, dt))

        idx = sb("c_idx", [P, 2, TOPK, TT], U32)
        gt = sb("c_gt", [P, 2, TOPK, TT])
        yg = sb("c_yg", [P, 2, TOPK, TT, D])
        part, res = sb("c_part", [P, TT, D]), sb("c_res", [P, 2, TT, D])
        idx_ready, gt_ready, part_ready, res_ready = (sem(f"c_{n}") for n in ("idx_ready", "gt_ready", "part_ready", "res_ready"))
        gathered = [sem(f"c_gathered{q}") for q in range(2)]
        stored = [sem(f"c_stored{q}") for q in range(2)]

        with nc.Block() as block:
            @block.vector
            def _(v):
                def indices(b, q):
                    v.tensor_copy(gt[:, q], gate[:, b, :, :]).then_inc(gt_ready, 1)
                    v.tensor_copy(idx[:, q], pos[:, b, :, :]).then_inc(idx_ready, 1)

                def total(b, k, q):
                    v.wait_ge(gathered[q], k * (TT * TOPK * 16) + TT * TOPK * 16)
                    v.wait_ge(gt_ready, b + 1)
                    for t in range(TT):
                        last = v.scalar_tensor_tensor(out=part[:, t, :], in0=yg[:, q, 0, t, :], scalar=gt[:, q, 0, t:t + 1], in1=h1[:, b, t, :],
                                                      op0=ALU.mult, op1=ALU.add)
                    last.then_inc(part_ready, 1)
                    v.wait_ge(part_ready, b + 1)
                    v.wait_ge(stored[q], k * 16 + 16)
                    for t in range(TT):
                        last = v.scalar_tensor_tensor(out=res[:, q, t, :], in0=yg[:, q, 1, t, :], scalar=gt[:, q, 1, t:t + 1], in1=part[:, t, :],
                                                      op0=ALU.mult, op1=ALU.add)
                    last.then_inc(res_ready, 1)
                    v.wait_ge(res_ready, b + 1)

                indices(0, 0)
                indices(1, 1)
                with v.Fori(0, NB // 2 - 1) as k:
                    for q in range(2):
                        total(k * 2 + q, k, q)
                        indices(k * 2 + q + 2, q)
                for q in range(2):
                    total(NB - 2 + q, NB // 2 - 1, q)

            @block.gpsimd
            def _(pool):
                with pool.Fori(0, NB // 2) as k:
                    for q in range(2):
                        hold(pool, idx_ready, k * 2 + q + 1)
                        for t in range(TT):
                            for e in range(TOPK):
                                pool.indirect_dma_start(out=yg[:, q, e, t, :], out_offset=None, in_=ys_d.rearrange("t p d -> (t p) d"),
                                                        in_offset=bass.IndirectOffsetOnAxis(ap=idx[:, q, e, t:t + 1], axis=0)).then_inc(gathered[q], 16)

            @block.sync
            def _(sp):
                for q in range(2):
                    sp.nop().then_inc(stored[q], 16)
                with sp.Fori(0, NB // 2) as k:
                    for q in range(2):
                        sp.wait_ge(res_ready, k * 2 + q + 1)
                        sp.dma_start(out[k * 2 + q].rearrange("(t p) d -> p t d", p=P), res[:, q]).then_inc(stored[q], 16)
                for q in range(2):
                    sp.wait_ge(stored[q], NB // 2 * 16 + 16)


def program(nc, x, txt, log_dt, inv_A_real, A_imag, B_ri, Wq, Wk, Wv, Wo, Wr, br, W1, b1, W2, b2, rotary, out):
    io = dict(x=x, txt=txt, log_dt=log_dt, inv_A_real=inv_A_real, A_imag=A_imag, B_ri=B_ri, Wo=Wo, Wr=Wr, br=br,
              W1=W1, b1=b1, W2=W2, b2=b2, rotary=rotary, Wq=Wq, Wk=Wk, Wv=Wv)
    img_d = nc.dram_tensor("img_d", (NB, IMG, D), F32, kind="Internal").ap()
    oT_d = nc.dram_tensor("oT_d", (NIT, P, 2, SEQ), F32, kind="Internal").ap()
    xs_d = nc.dram_tensor("xs_d", (SLOTS, D), F32, kind="Internal").ap()
    ys_d = nc.dram_tensor("ys_d", (NT, P, D), F32, kind="Internal").ap()
    with ExitStack() as ctx:
        def sb(name, shape, dt=F32):
            return ctx.enter_context(nc.sbuf_tensor(name, shape, dt))

        def sem(name):
            return ctx.enter_context(nc.semaphore(name))

        ident = sb("ident", [P, P])
        wo, wr, br = sb("wo", [P, KV * 2, D]), sb("wr", [P, KC, NE]), sb("br", [P, NE])
        with ExitStack() as held:
            def early(name, shape):
                return held.enter_context(nc.sbuf_tensor(name, shape, F32))

            wq, wk, wv = early("wq", [P, KC, 2, HEADS * DH // 2]), early("wk", [P, KC, 2, KV * DH // 2]), early("wv", [P, KC, KV * DH])
            loaded = sem("loaded")
            vandermonde(nc, sem, io, ident, img_d, wq, wk, wv, wo, wr, br, loaded)
            attention(nc, sem, io, ident, img_d, oT_d, wq, wk, wv, loaded)
        h1 = sb("h1", [P, NB, TT, D])
        pos = sb("pos", [P, NB, TOPK, TT], U32)
        gate = sb("gate", [P, NB, TOPK, TT])
        run, base = sb("run", [P, NE]), sb("base", [P, NE])
        exp_i, src_i = sb("exp_i", [P, NT], I32), sb("src_i", [P, NT], I32)
        tail_i, move = sb("tail_i", [P, NE], I32), sb("move", [P, NE])
        with ExitStack() as held:
            def weight(name, shape):
                return held.enter_context(nc.sbuf_tensor(name, shape, F32))

            weights = (weight("ew1", [P, NE, KC, FF]), weight("ew2", [P, NE, FC, D]), weight("eb1", [P, NE, FF]), weight("eb2", [P, NE, D]))
            route(nc, sem, io, ident, img_d, oT_d, xs_d, h1, pos, gate, run, base, exp_i, src_i, tail_i, move, wo, wr, br, weights, sem("weights_in"))
            experts(nc, sem, ident, xs_d, ys_d, exp_i, src_i, pos, move, weights)
        combine(nc, sem, ys_d, h1, pos, gate, out)


def rotary_tables():
    f = np.float32
    inv_freq = (f(1.0) / f(10000.0) ** (np.arange(0, DH, 2, dtype=f) / f(DH))).astype(f)
    angle = inv_freq[:, None] * np.arange(SEQ, dtype=f)[None, :]
    both = np.tile(np.stack([np.cos(angle), np.sin(angle)], 1), (P // (DH // 2), 1, 1))
    return np.ascontiguousarray(np.stack([both * f(DH ** -0.5), both], 1).astype(f))


_INS = ["x", "txt", "L0_tok_log_dt", "L0_tok_inv_A_real", "L0_tok_A_imag", "L0_tok_B_ri",
        "L0_attn_Wq", "L0_attn_Wk", "L0_attn_Wv", "L0_attn_Wo",
        "L0_ffn_Wr", "L0_ffn_br", "L0_ffn_W1", "L0_ffn_b1", "L0_ffn_W2", "L0_ffn_b2"]


def kernel(**inputs):
    import numpy as _np
    import concourse.bacc as _bacc
    from concourse import mybir as _mybir
    from concourse.bass_utils import run_bass_kernel_spmd as _run

    nc = _bacc.Bacc("TRN2", target_bir_lowering=False, num_devices=1)
    arrays, args = {}, []
    for name, a in [(n, inputs[n]) for n in _INS] + [("rotary", rotary_tables())]:
        a = _np.ascontiguousarray(a)
        arrays[f"in_{name}_dram"] = a
        args.append(nc.dram_tensor(f"in_{name}_dram", a.shape, _mybir.dt.from_np(a.dtype), kind="ExternalInput").ap())
    args.append(nc.dram_tensor("out_0_dram", (NB, SEQ, D), F32, kind="ExternalOutput").ap())
    program(nc, *args)
    r = _run(nc, [arrays], core_ids=[0])
    return r.results[0]["out_0_dram"]
```
